# Optimizing a Trainium2 kernel written in Bass

```python
import numpy as np
import jax
import jax.numpy as jnp

def _softmax(x, axis=-1):
    return jax.nn.softmax(x, axis=axis)

def _gelu(x):
    return jax.nn.gelu(x, approximate=True)

def _silu(x):
    return jax.nn.silu(x)

def _sigmoid(x):
    return jax.nn.sigmoid(x)

def _layernorm(x, axis=-1, eps=1e-05):
    m = jnp.mean(x, axis=axis, keepdims=True)
    v = jnp.var(x, axis=axis, keepdims=True)
    return (x - m) / jnp.sqrt(v + eps)

def _scatter_add(tgt, idx, src, axis=0):
    return tgt.at[idx].add(src)

def _segment_sum(src, seg, n):
    return jax.ops.segment_sum(src, seg, n)
kernel_name = 'mk_prb_d2_jaxref_r4_970872'

def setup_inputs(seed: int=0):
    np.random.seed(seed)
    _w = jnp.asarray

    def _L0_attn_setup():
        import jax, jax.numpy as jnp
        import numpy as np
        D_MODEL, D_STATE, D_CONV, EXPAND = (256, 16, 4, 2)
        D_INNER = EXPAND * D_MODEL
        B, L = (2, 1024)
        LN_EPS = 1e-05

        def _layernorm(x, gamma, beta):
            mu = jnp.mean(x, axis=-1, keepdims=True)
            var = jnp.mean(jnp.square(x - mu), axis=-1, keepdims=True)
            return (x - mu) * jax.lax.rsqrt(var + LN_EPS) * gamma + beta

        def _causal_depthwise_conv(xp, conv_w, conv_b):
            lhs = jnp.pad(xp.transpose(0, 2, 1), ((0, 0), (0, 0), (D_CONV - 1, 0)))
            out = jax.lax.conv_general_dilated(lhs, conv_w, window_strides=(1,), padding='VALID', dimension_numbers=('NCH', 'OIH', 'NCH'), feature_group_count=D_INNER)
            return out.transpose(0, 2, 1) + conv_b
        key = jax.random.key(seed)
        ks = jax.random.split(key, 6)
        x = jax.random.normal(ks[0], (B, L, D_MODEL), dtype=jnp.float32)
        ln_gamma = jnp.ones((D_MODEL,), jnp.float32)
        ln_beta = jnp.zeros((D_MODEL,), jnp.float32)
        W_in = jax.random.normal(ks[1], (2 * D_INNER, D_MODEL), jnp.float32) / np.sqrt(D_MODEL).astype(np.float32)
        conv_w = jax.random.normal(ks[2], (D_INNER, 1, D_CONV), jnp.float32) * 0.1
        conv_b = jnp.zeros((D_INNER,), jnp.float32)
        W_out = jax.random.normal(ks[3], (D_MODEL, D_INNER), jnp.float32) / np.sqrt(D_INNER).astype(np.float32)
        A = jnp.eye(D_STATE, dtype=jnp.float32)
        Bm = jax.random.normal(ks[4], (D_STATE, D_INNER), jnp.float32) * 0.01
        Cm = jax.random.normal(ks[5], (D_STATE, D_INNER), jnp.float32) * 0.01
        return dict(x=x, ln_gamma=ln_gamma, ln_beta=ln_beta, W_in=W_in, conv_w=conv_w, conv_b=conv_b, W_out=W_out, A=A, Bm=Bm, Cm=Cm)
    _L0_attn_in = _L0_attn_setup()

    def _L0_ffn_setup():
        import jax, jax.numpy as jnp
        import numpy as np
        H = 8
        QD = 64
        HALF = QD // 2
        DIMS = (32, 32)
        TOPK = 16
        DTK = 4
        EPS_BN = 1e-05
        EPS_NORM = 1e-12

        def _l2norm(x):
            n = jnp.linalg.norm(x, axis=-1, keepdims=True)
            return x / jnp.maximum(n, EPS_NORM)
        key = jax.random.key(seed)
        ks = jax.random.split(key, 6)
        B, S, D, O, E = (2, 128, 256, 256, 256)
        hidden_states = jax.random.normal(ks[0], (B, S, D), jnp.float32)
        Wq = jax.random.normal(ks[1], (D, H * QD), jnp.float32) * 0.02
        bq = jnp.zeros((H * QD,), jnp.float32)
        bn_gamma = jnp.ones((QD,), jnp.float32)
        bn_beta = jnp.zeros((QD,), jnp.float32)
        sub_key0 = jax.random.normal(ks[2], (DIMS[0], HALF), jnp.float32) * 0.02
        sub_key1 = jax.random.normal(ks[3], (DIMS[1], HALF), jnp.float32) * 0.02
        expert_down = jax.random.normal(ks[4], (E, D), jnp.float32) * 0.02
        expert_up = jax.random.normal(ks[5], (E, O), jnp.float32) * 0.02
        return {'hidden_states': hidden_states, 'Wq': Wq, 'bq': bq, 'bn_gamma': bn_gamma, 'bn_beta': bn_beta, 'sub_key0': sub_key0, 'sub_key1': sub_key1, 'expert_down': expert_down, 'expert_up': expert_up}
    _L0_ffn_in = _L0_ffn_setup()

    def _L1_attn_setup():
        import jax, jax.numpy as jnp
        import numpy as np
        EMB_DIM = 256
        N_HEADS = 16
        HEAD_DIM = EMB_DIM // N_HEADS
        SEQ = 512
        BSZ = 2

        def _rope_pair(q, k):
            bsz, seq_len, d_model = q.shape
            freq_range = jnp.arange(d_model // 2, dtype=jnp.float32)
            freq_cis = jnp.power(10000.0, -2.0 * freq_range / d_model)
            pos = jnp.arange(seq_len, dtype=jnp.float32)
            freq = jnp.einsum('i,j->ij', pos, freq_cis)
            sin_e = jnp.sin(freq)[None]
            cos_e = jnp.cos(freq)[None]
            q_even, q_odd = (q[..., ::2], q[..., 1::2])
            k_even, k_odd = (k[..., ::2], k[..., 1::2])
            q_rot = jnp.concatenate([q_even * cos_e - q_odd * sin_e, q_even * sin_e - q_odd * cos_e], axis=-1)
            k_rot = jnp.concatenate([k_even * cos_e - k_odd * sin_e, k_even * sin_e - k_odd * cos_e], axis=-1)
            return (q_rot, k_rot)
        key = jax.random.key(seed)
        ks = jax.random.split(key, 9)
        s = 1.0 / np.sqrt(EMB_DIM)
        return {'x': jax.random.normal(ks[0], (BSZ, SEQ, EMB_DIM), dtype=jnp.float32), 'Wq': jax.random.normal(ks[1], (EMB_DIM, EMB_DIM), dtype=jnp.float32) * s, 'bq': jax.random.normal(ks[2], (EMB_DIM,), dtype=jnp.float32) * 0.02, 'Wk': jax.random.normal(ks[3], (EMB_DIM, EMB_DIM), dtype=jnp.float32) * s, 'bk': jax.random.normal(ks[4], (EMB_DIM,), dtype=jnp.float32) * 0.02, 'Wv': jax.random.normal(ks[5], (EMB_DIM, EMB_DIM), dtype=jnp.float32) * s, 'bv': jax.random.normal(ks[6], (EMB_DIM,), dtype=jnp.float32) * 0.02, 'Wo': jax.random.normal(ks[7], (EMB_DIM, EMB_DIM), dtype=jnp.float32) * s, 'bo': jax.random.normal(ks[8], (EMB_DIM,), dtype=jnp.float32) * 0.02}
    _L1_attn_in = _L1_attn_setup()

    def _L1_ffn_setup():
        import math
        import jax, jax.numpy as jnp
        import numpy as np
        B, L, D, F_FF, E = (4, 512, 256, 1024, 8)
        TOP_K = 1
        CAPACITY_FACTOR = 1.25
        key = jax.random.key(seed)
        ks = jax.random.split(key, 4)
        h = jax.random.normal(ks[0], (B, L, D), dtype=jnp.float32)
        gate_w = jax.random.normal(ks[1], (E, D), dtype=jnp.float32) * 0.02
        gate_b = jnp.zeros((E,), dtype=jnp.float32)
        w1 = jax.random.normal(ks[2], (E, D, F_FF), dtype=jnp.float32) * 0.02
        b1 = jnp.zeros((E, F_FF), dtype=jnp.float32)
        w2 = jax.random.normal(ks[3], (E, F_FF, D), dtype=jnp.float32) * 0.02
        b2 = jnp.zeros((E, D), dtype=jnp.float32)
        return {'h': h, 'gate_w': gate_w, 'gate_b': gate_b, 'w1': w1, 'b1': b1, 'w2': w2, 'b2': b2}
    _L1_ffn_in = _L1_ffn_setup()
    _d = {'L0_attn_x': _L0_attn_in['x'], 'L0_attn_ln_gamma': _L0_attn_in['ln_gamma'], 'L0_attn_ln_beta': _L0_attn_in['ln_beta'], 'L0_attn_W_in': _L0_attn_in['W_in'], 'L0_attn_conv_w': _L0_attn_in['conv_w'], 'L0_attn_conv_b': _L0_attn_in['conv_b'], 'L0_attn_W_out': _L0_attn_in['W_out'], 'L0_attn_A': _L0_attn_in['A'], 'L0_attn_Bm': _L0_attn_in['Bm'], 'L0_attn_Cm': _L0_attn_in['Cm'], 'L0_ffn_Wq': _L0_ffn_in['Wq'], 'L0_ffn_bq': _L0_ffn_in['bq'], 'L0_ffn_bn_gamma': _L0_ffn_in['bn_gamma'], 'L0_ffn_bn_beta': _L0_ffn_in['bn_beta'], 'L0_ffn_sub_key0': _L0_ffn_in['sub_key0'], 'L0_ffn_sub_key1': _L0_ffn_in['sub_key1'], 'L0_ffn_expert_down': _L0_ffn_in['expert_down'], 'L0_ffn_expert_up': _L0_ffn_in['expert_up'], 'L1_attn_Wq': _L1_attn_in['Wq'], 'L1_attn_bq': _L1_attn_in['bq'], 'L1_attn_Wk': _L1_attn_in['Wk'], 'L1_attn_bk': _L1_attn_in['bk'], 'L1_attn_Wv': _L1_attn_in['Wv'], 'L1_attn_bv': _L1_attn_in['bv'], 'L1_attn_Wo': _L1_attn_in['Wo'], 'L1_attn_bo': _L1_attn_in['bo'], 'L1_ffn_gate_w': _L1_ffn_in['gate_w'], 'L1_ffn_gate_b': _L1_ffn_in['gate_b'], 'L1_ffn_w1': _L1_ffn_in['w1'], 'L1_ffn_b1': _L1_ffn_in['b1'], 'L1_ffn_w2': _L1_ffn_in['w2'], 'L1_ffn_b2': _L1_ffn_in['b2']}
    _x0 = _d['L0_attn_x']
    _d['L0_attn_x'] = jax.random.normal(jax.random.fold_in(jax.random.key(seed), 1), (2, 2048, 256), dtype=_x0.dtype)
    del _x0
    return _d

def reference(L0_attn_x, L0_attn_ln_gamma, L0_attn_ln_beta, L0_attn_W_in, L0_attn_conv_w, L0_attn_conv_b, L0_attn_W_out, L0_attn_A, L0_attn_Bm, L0_attn_Cm, L0_ffn_Wq, L0_ffn_bq, L0_ffn_bn_gamma, L0_ffn_bn_beta, L0_ffn_sub_key0, L0_ffn_sub_key1, L0_ffn_expert_down, L0_ffn_expert_up, L1_attn_Wq, L1_attn_bq, L1_attn_Wk, L1_attn_bk, L1_attn_Wv, L1_attn_bv, L1_attn_Wo, L1_attn_bo, L1_ffn_gate_w, L1_ffn_gate_b, L1_ffn_w1, L1_ffn_b1, L1_ffn_w2, L1_ffn_b2):

    def _L0_attn_ref(x, ln_gamma, ln_beta, W_in, conv_w, conv_b, W_out, A, Bm, Cm):
        import jax, jax.numpy as jnp
        import numpy as np
        D_MODEL, D_STATE, D_CONV, EXPAND = (256, 16, 4, 2)
        D_INNER = EXPAND * D_MODEL
        B, L = (2, 1024)
        LN_EPS = 1e-05

        def _layernorm(x, gamma, beta):
            mu = jnp.mean(x, axis=-1, keepdims=True)
            var = jnp.mean(jnp.square(x - mu), axis=-1, keepdims=True)
            return (x - mu) * jax.lax.rsqrt(var + LN_EPS) * gamma + beta

        def _causal_depthwise_conv(xp, conv_w, conv_b):
            lhs = jnp.pad(xp.transpose(0, 2, 1), ((0, 0), (0, 0), (D_CONV - 1, 0)))
            out = jax.lax.conv_general_dilated(lhs, conv_w, window_strides=(1,), padding='VALID', dimension_numbers=('NCH', 'OIH', 'NCH'), feature_group_count=D_INNER)
            return out.transpose(0, 2, 1) + conv_b
        xn = _layernorm(x, ln_gamma, ln_beta)
        xz = jnp.einsum('bld,ed->ble', xn, W_in)
        x_part, z = jnp.split(xz, 2, axis=-1)
        x_conv = jax.nn.silu(_causal_depthwise_conv(x_part, conv_w, conv_b))
        u_seq = x_part.transpose(1, 0, 2)
        xc_seq = x_conv.transpose(1, 0, 2)
        z_seq = z.transpose(1, 0, 2)

        def step(state, inp):
            u_t, xc_t, z_t = inp
            state = state @ A.T + u_t @ Bm.T
            out = (xc_t + state @ Cm) * jax.nn.sigmoid(z_t)
            return (state, out)
        state0 = jnp.zeros((x.shape[0], D_STATE), x.dtype)
        _, ys = jax.lax.scan(step, state0, (u_seq, xc_seq, z_seq))
        y = ys.transpose(1, 0, 2)
        residual = jnp.einsum('bli,di->bld', y, W_out)
        return x + residual

    def _L0_ffn_ref(hidden_states, Wq, bq, bn_gamma, bn_beta, sub_key0, sub_key1, expert_down, expert_up):
        import jax, jax.numpy as jnp
        import numpy as np
        H = 8
        QD = 64
        HALF = QD // 2
        DIMS = (32, 32)
        TOPK = 16
        DTK = 4
        EPS_BN = 1e-05
        EPS_NORM = 1e-12

        def _l2norm(x):
            n = jnp.linalg.norm(x, axis=-1, keepdims=True)
            return x / jnp.maximum(n, EPS_NORM)
        B, S, D = hidden_states.shape
        q = (hidden_states @ Wq + bq).reshape(B, S, H, QD)
        mean = q.mean(axis=(0, 1, 2))
        var = q.var(axis=(0, 1, 2))
        q = (q - mean) / jnp.sqrt(var + EPS_BN) * bn_gamma + bn_beta
        q0 = _l2norm(q[..., :HALF])
        q1 = _l2norm(q[..., HALF:])
        k0 = _l2norm(sub_key0)
        k1 = _l2norm(sub_key1)
        s0 = jnp.einsum('bshq,kq->bshk', q0, k0)
        s1 = jnp.einsum('bshq,kq->bshk', q1, k1)
        ts0, ti0 = jax.lax.top_k(s0, DTK)
        ts1, ti1 = jax.lax.top_k(s1, DTK)
        comb_s = (ts0[..., :, None] + ts1[..., None, :]).reshape(B, S, H, DTK * DTK)
        comb_i = (ti0[..., :, None] * DIMS[1] + ti1[..., None, :]).reshape(B, S, H, DTK * DTK)
        top_s, pos = jax.lax.top_k(comb_s, TOPK)
        idx = jnp.take_along_axis(comb_i, pos, axis=-1)
        w = jax.nn.softmax(top_s, axis=-1)
        down = expert_down[idx]
        up = expert_up[idx]
        eh = jnp.einsum('bshkd,bsd->bshk', down, hidden_states)
        eh = jax.nn.gelu(eh, approximate=False)
        out = jnp.einsum('bshko,bshk->bso', up, eh * w)
        return out

    def _L1_attn_ref(x, Wq, bq, Wk, bk, Wv, bv, Wo, bo):
        import jax, jax.numpy as jnp
        import numpy as np
        EMB_DIM = 256
        N_HEADS = 16
        HEAD_DIM = EMB_DIM // N_HEADS
        SEQ = 512
        BSZ = 2

        def _rope_pair(q, k):
            bsz, seq_len, d_model = q.shape
            freq_range = jnp.arange(d_model // 2, dtype=jnp.float32)
            freq_cis = jnp.power(10000.0, -2.0 * freq_range / d_model)
            pos = jnp.arange(seq_len, dtype=jnp.float32)
            freq = jnp.einsum('i,j->ij', pos, freq_cis)
            sin_e = jnp.sin(freq)[None]
            cos_e = jnp.cos(freq)[None]
            q_even, q_odd = (q[..., ::2], q[..., 1::2])
            k_even, k_odd = (k[..., ::2], k[..., 1::2])
            q_rot = jnp.concatenate([q_even * cos_e - q_odd * sin_e, q_even * sin_e - q_odd * cos_e], axis=-1)
            k_rot = jnp.concatenate([k_even * cos_e - k_odd * sin_e, k_even * sin_e - k_odd * cos_e], axis=-1)
            return (q_rot, k_rot)
        bsz, n, d = x.shape
        Q = x @ Wq + bq
        K = x @ Wk + bk
        V = x @ Wv + bv
        Q, K = _rope_pair(Q, K)
        Q = Q.reshape(bsz, n, N_HEADS, HEAD_DIM).transpose(0, 2, 1, 3)
        K = K.reshape(bsz, n, N_HEADS, HEAD_DIM).transpose(0, 2, 1, 3)
        V = V.reshape(bsz, n, N_HEADS, HEAD_DIM).transpose(0, 2, 1, 3)
        scores = jnp.einsum('bhqd,bhkd->bhqk', Q, K)
        causal = jnp.triu(jnp.ones((n, n), dtype=bool), k=1)
        scores = jnp.where(causal, -jnp.inf, scores)
        attn = jax.nn.softmax(scores / jnp.sqrt(jnp.float32(HEAD_DIM)), axis=-1)
        ctx = jnp.einsum('bhqk,bhkd->bhqd', attn, V)
        ctx = ctx.transpose(0, 2, 1, 3).reshape(bsz, n, d)
        return ctx @ Wo + bo

    def _L1_ffn_ref(h, gate_w, gate_b, w1, b1, w2, b2):
        import math
        import jax, jax.numpy as jnp
        import numpy as np
        B, L, D, F_FF, E = (4, 512, 256, 1024, 8)
        TOP_K = 1
        CAPACITY_FACTOR = 1.25
        Bh, Lh, Dh = h.shape
        T = Bh * Lh
        capacity = max(1, math.ceil(CAPACITY_FACTOR * (T * TOP_K / E)))
        x = h.reshape(T, Dh)
        logits = x @ gate_w.T + gate_b
        probs = jax.nn.softmax(logits, axis=-1)
        idx = jnp.argmax(probs, axis=-1)
        top_prob = jnp.max(probs, axis=-1)
        one_hot = jax.nn.one_hot(idx, E, dtype=jnp.int32)
        pos = jnp.take_along_axis(jnp.cumsum(one_hot, axis=0), idx[:, None], axis=1)[:, 0] - 1
        keep = pos < capacity
        safe_pos = jnp.where(keep, pos, 0)
        buf = jnp.zeros((E, capacity, Dh), dtype=x.dtype)
        buf = buf.at[idx, safe_pos].add(x * keep[:, None].astype(x.dtype))
        hdn = jax.nn.relu(jnp.einsum('ecd,edf->ecf', buf, w1) + b1[:, None, :])
        eout = jnp.einsum('ecf,efd->ecd', hdn, w2) + b2[:, None, :]
        gathered = eout[idx, safe_pos]
        out = gathered * (top_prob * keep.astype(x.dtype))[:, None]
        return out.reshape(Bh, Lh, Dh)
    x = L0_attn_x
    xn = _layernorm(x, axis=-1)
    x = x + _L0_attn_ref(xn, L0_attn_ln_gamma, L0_attn_ln_beta, L0_attn_W_in, L0_attn_conv_w, L0_attn_conv_b, L0_attn_W_out, L0_attn_A, L0_attn_Bm, L0_attn_Cm) + _L0_ffn_ref(xn, L0_ffn_Wq, L0_ffn_bq, L0_ffn_bn_gamma, L0_ffn_bn_beta, L0_ffn_sub_key0, L0_ffn_sub_key1, L0_ffn_expert_down, L0_ffn_expert_up)
    xn = _layernorm(x, axis=-1)
    x = x + _L1_attn_ref(xn, L1_attn_Wq, L1_attn_bq, L1_attn_Wk, L1_attn_bk, L1_attn_Wv, L1_attn_bv, L1_attn_Wo, L1_attn_bo) + _L1_ffn_ref(xn, L1_ffn_gate_w, L1_ffn_gate_b, L1_ffn_w1, L1_ffn_b1, L1_ffn_w2, L1_ffn_b2)
    return x

_drawn_inputs = setup_inputs


def setup_inputs(seed=0):
    import zlib

    import numpy as np

    out = dict(_drawn_inputs(seed))
    spreads = {'L0_attn_ln_gamma': (1.0, 0.6),
     'L0_attn_ln_beta': (0.0, 0.1),
     'L0_attn_conv_b': (0.0, 0.522),
     'L0_ffn_bq': (0.0, 0.8),
     'L0_ffn_bn_gamma': (1.0, 0.6),
     'L0_ffn_bn_beta': (0.0, 0.8),
     'L1_ffn_gate_b': (0.0, 0.8),
     'L1_ffn_b1': (0.0, 0.8),
     'L1_ffn_b2': (0.0, 0.8)}
    factors = {'L0_ffn_Wq': 8.0,
     'L0_ffn_sub_key0': 8.0,
     'L0_ffn_sub_key1': 8.0,
     'L0_ffn_expert_down': 5.517,
     'L0_ffn_expert_up': 5.307,
     'L1_attn_bq': 64.0,
     'L1_attn_bk': 64.0,
     'L1_attn_bv': 5.588,
     'L1_attn_bo': 6.116,
     'L1_ffn_gate_w': 3.631,
     'L1_ffn_w1': 5.049,
     'L1_ffn_w2': 4.036}
    for name, (base, spread) in spreads.items():
        noise = np.random.default_rng([zlib.crc32(name.encode()), seed]).standard_normal(out[name].shape)
        drawn = base * np.exp(spread * noise) if base else spread * noise
        out[name] = jnp.asarray(drawn.astype(out[name].dtype))
    for name, factor in factors.items():
        out[name] = (out[name] * factor).astype(out[name].dtype)
    return out
```

```python
from contextlib import ExitStack

import numpy as np

import concourse.bass as bass
from concourse import mybir

F32 = mybir.dt.float32
BF16 = mybir.dt.bfloat16
I32 = mybir.dt.int32
U32 = mybir.dt.uint32
ALU = mybir.AluOpType
ACT = mybir.ActivationFunctionType
AX_X = mybir.AxisListType.X

P = 128
BATCH, SEQ, D = 2, 2048, 256
TOK = BATCH * SEQ
TILES = TOK // P
BLK = 512
BLOCKS = TOK // BLK
SUB = BLK // P
DC = D // P
EPS = 1e-5

INNER, STATE, TAPS = 512, 16, 4
IC = INNER // P
GROUPS = P // STATE

PK_HEADS, QD, NKEY, TOPK_DIM = 8, 64, 32, 4
HALF = QD // 2
SETS = 2 * PK_HEADS
PK_EXP = 256
ROWS_IN = PK_EXP // NKEY
QCH = PK_HEADS * QD // P

HEADS, HD = 16, 16
HPG = 4
HG = HEADS // HPG
QT = SEQ // BLK
KT = SEQ // P
PADV = 32
TERMS = 6
MROW = TERMS * HD

EXPERTS, FF, CAP = 8, 1024, 640
CT = CAP // P
FC = FF // P
SLOTS = EXPERTS * CAP

PARTS_Q = (0, 0, 1, 1, 0, 2)
PARTS_K = (0, 1, 0, 1, 2, 0)


def program(nc, inp, out):
    ctx = ExitStack()
    with ctx:
        def sem(name):
            return ctx.enter_context(nc.semaphore(name))

        def keep(name, shape, dt=F32):
            return ctx.enter_context(nc.sbuf_tensor(name, shape, dt))

        res = keep("res", [P, TILES, D])
        ident = keep("ident", [P, P])
        identb = keep("identb", [P, P], BF16)
        rowsT = nc.dram_tensor("split_rows", (2, 3, BATCH * D, SEQ), BF16, kind="Internal").ap()
        v_pad = nc.dram_tensor("v_padded", (BATCH * HG, P, KT, HPG * PADV), F32, kind="Internal").ap()
        moe_in = nc.dram_tensor("moe_in", (SLOTS + TOK, D), F32, kind="Internal").ap()
        moe_out = nc.dram_tensor("moe_out", (SLOTS, D), F32, kind="Internal").ap()

        weight = keep("weight", [P, TILES])
        gather_at = keep("gather_at", [P, TILES], I32)
        with ExitStack() as c0:
            normT = c0.enter_context(nc.sbuf_tensor("normT", [P, DC, TOK], F32))
            with ExitStack() as c1:
                ssmT = c1.enter_context(nc.sbuf_tensor("ssmT", [P, DC, TOK], F32))
                norm_first(nc, sem, inp, res, normT, ssmT, ident, identb, moe_in)
                ssm(nc, sem, inp, res, ssmT, ident)
            product_keys(nc, sem, inp, res, normT, ident)
            with ExitStack() as c2:
                rows = c2.enter_context(nc.sbuf_tensor("rows", [P, TILES, D], F32))
                logits = c2.enter_context(nc.sbuf_tensor("logits", [P, TILES, EXPERTS], F32))
                norm_second(nc, sem, res, rows, normT, ident)
                project(nc, sem, inp, normT, rowsT, v_pad, logits)
                route(nc, sem, inp, rows, logits, weight, gather_at, moe_in)
        attention(nc, sem, inp, res, rowsT, v_pad, ident, identb)
        moe(nc, sem, inp, res, weight, gather_at, moe_in, moe_out, ident, out)


def norm_first(nc, sem, inp, res, normT, ssmT, ident, identb, moe_in):
    x = inp["x"].rearrange("b (t p) d -> p (b t) d", p=P)
    with ExitStack() as c:
        def sb(name, shape, dt=F32):
            return c.enter_context(nc.sbuf_tensor("n1_" + name, shape, dt))
        xin = sb("xin", [P, TILES, D])
        xn = sb("xn", [P, SUB, D])
        x2 = sb("x2", [P, SUB, D])
        stats = sb("stats", [P, 2, SUB, 6])
        mv = sb("mv", [P, 2, SUB, 2])
        std = sb("std", [P, 2, SUB])
        rstd = sb("rstd", [P, 2, SUB])
        gb = sb("gb", [P, 2, DC])
        zeros = sb("zeros", [P, 2 * D])
        ps = c.enter_context(nc.psum_tensor("n1_ps", [P, 2 * DC, BLK], F32))
        x_in, const_in = sem("n1_x_in"), sem("n1_const_in")
        made, var_ok, std_ok = sem("n1_made"), sem("n1_var_ok"), sem("n1_std_ok")
        xn_ok, x2_ok, res_ok = sem("n1_xn_ok"), sem("n1_x2_ok"), sem("n1_res_ok")
        turned1, turned2 = sem("n1_turned1"), sem("n1_turned2")
        out1, out2 = sem("n1_out1"), sem("n1_out2")
        relay, sp_relay = sem("n1_relay"), sem("n1_sp_relay")
        zero_ok, zeroed = sem("n1_zero_ok"), sem("n1_zeroed")
        with nc.Block() as block:
            @block.sync
            def _(sp):
                for t, src in ((ident, inp["c_ident"]), (gb, inp["gb"])):
                    sp.dma_start(t[:], src).then_inc(const_in, 16)
                sp.wait_ge(const_in, 32)
                with sp.Fori(0, BLOCKS) as j:
                    sp.dma_start(xin[:, bass.ds(j * SUB, SUB), :],
                                 x[:, bass.ds(j * SUB, SUB), :]).then_inc(x_in, 16)
                    sp.wait_ge(x_in, j * 16 + 16)
                    sp.nop().then_inc(sp_relay, 1)
                sp.wait_ge(zero_ok, 1)
                n = SLOTS // (2 * P)
                for k in range(n):
                    sp.dma_start(moe_in[k * 2 * P:(k + 1) * 2 * P, :].rearrange("(p a) d -> p (a d)", p=P),
                                 zeros[:]).then_inc(zeroed, 16)
                sp.wait_ge(zeroed, 16 * n)

            @block.gpsimd
            def _(pool):
                nc.gpsimd.memset(zeros[:], 0.0).then_inc(zero_ok, 1)
                with pool.Fori(0, BLOCKS) as j:
                    pool.wait_ge(xn_ok, j * SUB + SUB)
                    nc.gpsimd.tensor_tensor(res[:, bass.ds(j * SUB, SUB), :],
                                            xin[:, bass.ds(j * SUB, SUB), :], xn[:], ALU.add).then_inc(res_ok, 1)

            @block.vector
            def _(dve):
                with dve.Fori(0, BLOCKS) as j:
                    dve.wait_ge(x_in, j * 16 + 16)
                    blk = xin[:, bass.ds(j * SUB, SUB), :]
                    for r in range(2):
                        for s in range(SUB):
                            src = blk[:, s, :] if r == 0 else xn[:, s, :]
                            nc.vector.bn_stats(stats[:, r, s, :], src).then_inc(made, 1)
                        dve.wait_ge(made, j * 16 + 8 * r + 4)
                        dve.nop().then_inc(relay, 1)
                        for s in range(SUB):
                            nc.vector.bn_aggr(mv[:, r, s, :], stats[:, r, s, :]).then_inc(made, 1)
                        dve.wait_ge(made, j * 16 + 8 * r + 8)
                        nc.vector.tensor_scalar(std[:, r, :], mv[:, r, :, 1], EPS, None, ALU.add).then_inc(var_ok, 1)
                        dve.wait_ge(std_ok, j * 2 + r + 1)
                        nc.vector.reciprocal(rstd[:, r, :], std[:, r, :]).then_inc(var_ok, 1)
                        dve.wait_ge(var_ok, j * 4 + 2 * r + 2)
                        if r == 0:
                            dve.wait_ge(turned1, j * DC + 1)
                            dve.wait_ge(res_ok, j + 1)
                        else:
                            dve.wait_ge(turned2, j * DC + 1)
                        for s in range(SUB):
                            src = blk[:, s, :] if r == 0 else xn[:, s, :]
                            dst = xn if r == 0 else x2
                            nc.vector.tensor_scalar(dst[:, s, :], src, mv[:, r, s, 0:1], rstd[:, r, s:s + 1],
                                                    ALU.subtract, ALU.mult).then_inc(xn_ok if r == 0 else x2_ok, 1)
                        if r == 0:
                            dve.wait_ge(xn_ok, j * SUB + SUB)
                    for d in range(DC):
                        dve.wait_ge(turned1, j * DC + d + 2)
                        nc.vector.tensor_copy(normT[:, d, bass.ds(j * BLK, BLK)], ps[:, d, :]).then_inc(out1, 1)

            @block.tensor
            def _(pe):
                pe.wait_ge(const_in, 32)
                pe.nop().then_inc(turned1, 1)
                pe.nop().then_inc(turned2, 1)
                with pe.Fori(0, BLOCKS) as j:
                    pe.wait_ge(xn_ok, j * SUB + SUB)
                    pe.wait_ge(out1, j * DC + 2)
                    for d in range(DC):
                        for s in range(SUB):
                            last = nc.tensor.transpose(ps[:, d, s * P:(s + 1) * P], xn[:, s, d * P:(d + 1) * P], ident[:])
                        last.then_inc(turned1, 1)
                    pe.wait_ge(x2_ok, j * SUB + SUB)
                    pe.wait_ge(out2, j * DC + 2)
                    for d in range(DC):
                        for s in range(SUB):
                            last = nc.tensor.transpose(ps[:, DC + d, s * P:(s + 1) * P], x2[:, s, d * P:(d + 1) * P], ident[:])
                        last.then_inc(turned2, 1)

            @block.scalar
            def _(act):
                act.wait_ge(const_in, 32)
                nc.scalar.activation(identb[:], ident[:], ACT.Copy)
                act.nop().then_inc(out1, 2)
                act.nop().then_inc(out2, 2)
                act.nop().then_inc(res_ok, 1)
                with act.Fori(0, BLOCKS) as j:
                    for r in range(2):
                        act.wait_ge(var_ok, j * 4 + 2 * r + 1)
                        nc.scalar.activation(std[:, r, :], std[:, r, :], ACT.Sqrt).then_inc(std_ok, 1)
                    for d in range(DC):
                        act.wait_ge(turned2, j * DC + d + 2)
                        nc.scalar.activation(ssmT[:, d, bass.ds(j * BLK, BLK)], ps[:, DC + d, :], ACT.Identity,
                                             scale=gb[:, 0, d:d + 1], bias=gb[:, 1, d:d + 1]).then_inc(out2, 1)


def ssm(nc, sem, inp, res, ssmT, ident):
    with ExitStack() as c:
        def sb(name, shape, dt=F32):
            return c.enter_context(nc.sbuf_tensor("ss_" + name, shape, dt))
        w_in = sb("w_in", [P, DC, 2 * INNER])
        w_ine = sb("w_ine", [P, IC, D])
        w_out = sb("w_out", [P, IC, D])
        bmT = sb("bmT", [P, IC, STATE])
        cm = sb("cm", [P, INNER])
        own = sb("own", [P, GROUPS])
        stj = sb("stj", [P, BLK])
        cw = sb("cw", [P, IC, TAPS + 1])
        vw = sb("vw", [P, DC, 2 * P])
        pw = sb("pw", [P, 2, 2, P + STATE])
        sh = sb("sh", [P, 2, P])
        st = sb("st", [P, BLK])
        halo = TAPS - 1
        u = sb("u", [P, IC, halo + BLK])
        sz = sb("sz", [P, IC, BLK])
        cv = sb("cv", [P, IC, BLK])
        sg = sb("sg", [P, IC, BLK])
        y = sb("y", [P, IC, BLK])
        pU = c.enter_context(nc.psum_tensor("ss_pU", [P, 2, BLK], F32))
        pZ = c.enter_context(nc.psum_tensor("ss_pZ", [P, 2, BLK], F32))
        pB = c.enter_context(nc.psum_tensor("ss_pB", [P, 2, BLK], F32))
        pC = c.enter_context(nc.psum_tensor("ss_pC", [P, 2, BLK], F32))
        w_ok, wz = sem("ss_w_ok"), sem("ss_wz")
        fold, folded, scanp, scanv = sem("ss_fold"), sem("ss_folded"), sem("ss_scanp"), sem("ss_scanv")
        powp, powv, shv, sh_zero = sem("ss_powp"), sem("ss_powv"), sem("ss_shv"), sem("ss_sh_zero")
        STEPS = (BLK - 1).bit_length()
        LEVELS = STEPS + (SEQ // BLK - 1).bit_length()
        with nc.Block() as block:
            @block.sync
            def _(sp):
                sp.wait_ge(wz, 2)
                for g in range(GROUPS):
                    at = slice(g * STATE, (g + 1) * STATE)
                    sp.dma_start(cm[at, :], inp["Cm"]).then_inc(w_ok, 16)
                    for q in range(2):
                        sp.dma_start(pw[at, 0, q, STATE + g * STATE:STATE + (g + 1) * STATE],
                                     inp["A_T"] if q == 0 else inp["A"]).then_inc(w_ok, 16)
                for t, name in ((w_in, "W_inT"), (w_ine, "W_inE"), (w_out, "W_outT"), (bmT, "BmT"), (cw, "conv"), (own, "c_own")):
                    sp.dma_start(t[:], inp[name]).then_inc(w_ok, 16)
            W_ALL = 16 * (3 * GROUPS + 6)

            @block.gpsimd
            def _(pool):
                nc.gpsimd.memset(pw[:], 0.0).then_inc(wz, 1)
                nc.gpsimd.memset(vw[:], 0.0).then_inc(wz, 1)

            @block.tensor
            def _(pe):
                pe.wait_ge(w_ok, W_ALL)
                for d in range(DC):
                    for k in range(IC):
                        last = nc.tensor.matmul(pC[:, d, 0:STATE], w_ine[:, k, d * P:(d + 1) * P], bmT[:, k, :],
                                                start=k == 0, stop=k == IC - 1)
                last.then_inc(fold, 1)
                pe.wait_ge(folded, DC)
                for j in range(BLOCKS):
                    for d in range(DC):
                        last = nc.tensor.matmul(pB[:, 0, :], vw[:, d, P - STATE * j:2 * P - STATE * j],
                                                ssmT[:, d, j * BLK:(j + 1) * BLK],
                                                start=j == 0 and d == 0, stop=j == BLOCKS - 1 and d == DC - 1)
                last.then_inc(scanp, 1)
                for k in range(LEVELS):
                    cur = k % 2
                    pe.wait_ge(shv, k + 1)
                    pe.wait_ge(scanv, k + 1)
                    if k < STEPS:
                        n = 1 << k
                        nc.tensor.matmul(pB[:, 1, n:BLK], pw[:, cur, 0, STATE:], st[:, 0:BLK - n], start=True, stop=True)
                        last = nc.tensor.matmul(pB[:, 1, 0:n], sh[:, cur, :], st[:, BLK - n:BLK], start=True, stop=True)
                    else:
                        last = nc.tensor.matmul(pB[:, 1, :], sh[:, cur, :], st[:], start=True, stop=True)
                    last.then_inc(scanp, 1)
                    if k < LEVELS - 1:
                        nc.tensor.matmul(pC[:, 0, 0:P], pw[:, cur, 1, STATE:], pw[:, cur, 0, STATE:], start=True, stop=True)
                        nc.tensor.matmul(pC[:, 0, P:2 * P], pw[:, cur, 0, STATE:], pw[:, cur, 1, STATE:],
                                         start=True, stop=True).then_inc(powp, 1)

            @block.vector
            def _(dve):
                dve.wait_ge(fold, 1)
                dve.wait_ge(wz, 2)
                for d in range(DC):
                    nc.vector.tensor_copy(vw[:, d, P:P + STATE], pC[:, d, 0:STATE]).then_inc(folded, 1)
                dve.wait_ge(scanp, 1)
                nc.vector.tensor_copy(st[:], pB[:, 0, :]).then_inc(scanv, 1)
                per = SEQ // BLK * STATE
                dve.wait_ge(w_ok, W_ALL)
                for k in range(LEVELS):
                    cur = k % 2
                    if k:
                        dve.wait_ge(powp, k)
                        dve.wait_ge(scanp, k + 1)
                        for q in range(2):
                            nc.vector.tensor_copy(pw[:, cur, q, STATE:], pC[:, 0, q * P:(q + 1) * P]).then_inc(powv, 1)
                        dve.wait_ge(powv, 2 * k)
                    far = max(0, k - STEPS)
                    w = STATE << far
                    nc.vector.memset(sh[:, cur, :], 0.0).then_inc(sh_zero, 1)
                    dve.wait_ge(sh_zero, 1 + k)
                    for b in range(BATCH):
                        last = nc.vector.tensor_copy(sh[:, cur, b * per + w:(b + 1) * per],
                                                     pw[:, cur, 0, STATE + b * per:STATE + (b + 1) * per - w])
                    last.then_inc(shv, 1)
                    dve.wait_ge(scanp, k + 2)
                    dve.wait_ge(scanv, k + 1)
                    nc.vector.tensor_tensor(st[:], st[:], pB[:, 1, :], ALU.add).then_inc(scanv, 1)

        u_made, u_left, z_made, z_left = sem("mx_u_made"), sem("mx_u_left"), sem("mx_z_made"), sem("mx_z_left")
        c_made, c_left, o_made, o_left = sem("mx_c_made"), sem("mx_c_left"), sem("mx_o_made"), sem("mx_o_left")
        own_ok = sem("mx_own_ok")
        halo_ok, conv_ok, gate_ok, silu_ok, y_ok = (sem("mx_" + n) for n in ("halo_ok", "conv_ok", "gate_ok", "silu_ok", "y_ok"))
        PB = SEQ // BLK
        with nc.Block() as block:
            @block.tensor
            def _(pe):
                with pe.Fori(0, BLOCKS) as j:
                    cols = bass.ds(j * BLK, BLK)
                    for m in range(IC):
                        pe.wait_ge(u_left, j * IC + m + 1)
                        for d in range(DC):
                            last = nc.tensor.matmul(pU[:, m % 2, :], w_in[:, d, m * P:(m + 1) * P], ssmT[:, d, cols],
                                                    start=d == 0, stop=d == DC - 1)
                        last.then_inc(u_made, 1)
                        pe.wait_ge(z_left, j * IC + m + 1)
                        for d in range(DC):
                            last = nc.tensor.matmul(pZ[:, m % 2, :], w_in[:, d, INNER + m * P:INNER + (m + 1) * P],
                                                    ssmT[:, d, cols], start=d == 0, stop=d == DC - 1)
                        last.then_inc(z_made, 1)
                    pe.wait_ge(own_ok, j + 1)
                    for m in range(IC):
                        pe.wait_ge(c_left, j * IC + m + 1)
                        nc.tensor.matmul(pB[:, m % 2, :], cm[:, m * P:(m + 1) * P], stj[:], start=True, stop=True).then_inc(c_made, 1)
                    pe.wait_ge(y_ok, j * IC + IC + 1)
                    for s in range(SUB):
                        pe.wait_ge(o_left, j * SUB + s + 1)
                        for k in range(IC):
                            last = nc.tensor.matmul(pC[:, s % 2, 0:D], y[:, k, s * P:(s + 1) * P], w_out[:, k, :],
                                                    start=k == 0, stop=k == IC - 1)
                        last.then_inc(o_made, 1)

            @block.scalar
            def _(act):
                act.nop().then_inc(c_made, 1)
                act.nop().then_inc(y_ok, 1)
                act.nop().then_inc(u_left, 2)
                act.nop().then_inc(z_left, 2)
                with act.Fori(0, BATCH) as b:
                    with act.Fori(0, PB) as i:
                        j = b * PB + i
                        act.wait_ge(halo_ok, b * (PB + 1) + i + 2)
                        act.wait_ge(c_made, j * IC + 1)
                        nc.scalar.activation(stj[:], st[:], ACT.Copy, scale=own[:, bass.ds(j, 1)]).then_inc(own_ok, 1)
                        act.wait_ge(y_ok, j * IC + 1)
                        for m in range(IC):
                            act.wait_ge(u_made, j * IC + m + 1)
                            nc.scalar.activation(u[:, m, halo:], pU[:, m % 2, :], ACT.Copy).then_inc(u_left, 1)
                            act.wait_ge(z_made, j * IC + m + 1)
                            nc.scalar.activation(sz[:, m, :], pZ[:, m % 2, :], ACT.Sigmoid).then_inc(z_left, 1)
                        for m in range(IC):
                            act.wait_ge(conv_ok, (j * IC + m) * TAPS + TAPS)
                            nc.scalar.activation(sg[:, m, :], cv[:, m, :], ACT.Sigmoid).then_inc(gate_ok, 1)

            @block.vector
            def _(dve):
                dve.nop().then_inc(halo_ok, 1)
                dve.nop().then_inc(o_made, 1)
                dve.nop().then_inc(c_left, 2)
                dve.nop().then_inc(o_left, 2)
                with dve.Fori(0, BATCH) as b:
                    dve.wait_ge(halo_ok, b * (PB + 1) + 1)
                    nc.vector.memset(u[:, :, 0:halo], 0.0).then_inc(halo_ok, 1)
                    with dve.Fori(0, PB) as i:
                        j = b * PB + i
                        dve.wait_ge(halo_ok, b * (PB + 1) + i + 2)
                        for m in range(IC):
                            dve.wait_ge(u_left, j * IC + m + 3)
                            n = (j * IC + m) * TAPS
                            nc.vector.tensor_scalar(cv[:, m, :], u[:, m, halo:], cw[:, m, TAPS - 1:TAPS], cw[:, m, TAPS:],
                                                    ALU.mult, ALU.add).then_inc(conv_ok, 1)
                            for k in range(TAPS - 1):
                                dve.wait_ge(conv_ok, n + k + 1)
                                nc.vector.scalar_tensor_tensor(cv[:, m, :], u[:, m, k:k + BLK], cw[:, m, k:k + 1], cv[:, m, :],
                                                               ALU.mult, ALU.add).then_inc(conv_ok, 1)
                        dve.wait_ge(conv_ok, (j + 1) * IC * TAPS)
                        nc.vector.tensor_copy(u[:, :, 0:halo], u[:, :, BLK:]).then_inc(halo_ok, 1)
                        for m in range(IC):
                            dve.wait_ge(gate_ok, j * IC + m + 1)
                            nc.vector.tensor_tensor(cv[:, m, :], cv[:, m, :], sg[:, m, :], ALU.mult).then_inc(silu_ok, 1)
                        for m in range(IC):
                            dve.wait_ge(silu_ok, j * IC + m + 1)
                            dve.wait_ge(c_made, j * IC + m + 2)
                            nc.vector.tensor_tensor(sg[:, m, :], cv[:, m, :], pB[:, m % 2, :], ALU.add).then_inc(c_left, 1)
                        dve.wait_ge(z_left, j * IC + IC + 2)
                        dve.wait_ge(o_made, j * SUB + 1)
                        for m in range(IC):
                            dve.wait_ge(c_left, j * IC + m + 3)
                            nc.vector.tensor_tensor(y[:, m, :], sg[:, m, :], sz[:, m, :], ALU.mult).then_inc(y_ok, 1)
                        for s in range(SUB):
                            dve.wait_ge(o_made, j * SUB + s + 2)
                            row = res[:, bass.ds(j * SUB + s, 1), :].rearrange("p a n -> p (a n)")
                            nc.vector.tensor_tensor(row, row, pC[:, s % 2, 0:D], ALU.add).then_inc(o_left, 1)


class Steps:

    def __init__(self, sem, per_round, i=0):
        self.sem, self.per, self.i, self.n = sem, per_round, i, 0

    def inc(self, instruction):
        instruction.then_inc(self.sem, 1)
        self.n += 1
        assert self.n <= self.per
        return self.n

    def at(self, n):
        return self.i * self.per + n


def product_keys(nc, sem, inp, res, normT, ident):
    SCORES = SETS * NKEY
    with ExitStack() as c:
        def sb(name, shape, dt=F32):
            return c.enter_context(nc.sbuf_tensor("pk_" + name, shape, dt))
        wq = sb("wq", [P, DC, PK_HEADS * QD])
        vec = sb("vec", [P, QCH + 2])
        keys = sb("keys", [P, P])
        keysq = sb("keysq", [P, P])
        knorm = sb("knorm", [P, P])
        ones = sb("ones", [P, P])
        heads = sb("heads", [P, P])
        halves = sb("halves", [P, P // HALF])
        down = sb("down", [P, DC, PK_EXP])
        upw = sb("upw", [P, DC, PK_EXP])
        q = sb("q", [P, QCH, TOK])
        stats = sb("stats", [P, QCH, BLOCKS, 6])
        mv = sb("mv", [P, QCH, 2])
        mom = sb("mom", [P, 4])
        ab = sb("ab", [P, 2])
        qn = sb("qn", [P, QCH, BLK])
        qs = sb("qs", [P, QCH, BLK])
        nrm = sb("nrm", [P, 2, SUB * SETS])
        s_ = sb("s", [P, 2, SCORES])
        ex = sb("ex", [P, 2, SCORES])
        rep = sb("rep", [P, SCORES])
        top = sb("top", [P, SETS, 8])
        pm = sb("pm", [P, 2, SCORES])
        z = sb("z", [P, SETS])
        small = sb("small", [P, 4, PK_HEADS])
        a0 = sb("a0", [P, 2, PK_HEADS * ROWS_IN])
        last_w = sb("last_w", [P, 2])
        prod = sb("prod", [P, 2, PK_HEADS, PK_EXP])
        wt = sb("wt", [P, 2, PK_EXP])
        g = sb("g", [P, DC, BLK])
        gw = sb("gw", [P, DC, BLK])
        pS = c.enter_context(nc.psum_tensor("pk_pS", [P, 2, BLK], F32))
        pN = c.enter_context(nc.psum_tensor("pk_pN", [P, BLK], F32))
        pG = c.enter_context(nc.psum_tensor("pk_pG", [P, 2, BLK], F32))
        pT = c.enter_context(nc.psum_tensor("pk_pT", [P, 2, BLK], F32))
        w_ok, kz, knp, kn1, kn2 = (sem("pk_" + n) for n in ("w_ok", "kz", "knp", "kn1", "kn2"))
        qp, qo, stat, moment, vstep, vstd = (sem("pk_" + n) for n in ("qp", "qo", "stat", "moment", "vstep", "vstd"))
        relay = sem("pk_relay")
        names = ("qn_ok", "sq_ok", "n2_ok", "root_ok", "sc_ok", "s_ok", "ex_ok", "step", "a0_ok", "prod_ok",
                 "wt_ok", "dot_ok", "g_ok", "turn_ok", "gw_ok", "o_ok", "o_left")
        (qn_ok, sq_ok, n2_ok, root_ok, sc_ok, s_ok, ex_ok, step, a0_ok, prod_ok,
         wt_ok, dot_ok, g_ok, turn_ok, gw_ok, o_ok, o_left) = (sem("pk_" + n) for n in names)
        with nc.Block() as block:
            @block.sync
            def _(sp):
                sp.wait_ge(kz, 1)
                n = 0
                for k in range(P // HALF):
                    at = slice(k * HALF, (k + 1) * HALF)
                    sp.dma_start(keys[at, at], inp[f"key{k % 2}T"]).then_inc(w_ok, 16)
                    n += 16
                for t, name in ((wq, "Wq0"), (vec, "pk_vec"), (ones, "c_ones"), (heads, "c_heads"),
                                (halves, "c_halves"), (down, "downT"), (upw, "up")):
                    sp.dma_start(t[:], inp[name]).then_inc(w_ok, 16)
                    n += 16
            W_ALL = 16 * (P // HALF + 7)

            @block.gpsimd
            def _(pool):
                nc.gpsimd.memset(keys[:], 0.0).then_inc(kz, 1)

            @block.tensor
            def _(pe):
                pe.nop().then_inc(qo, 1)
                pe.wait_ge(w_ok, W_ALL)
                pe.wait_ge(kn1, 1)
                nc.tensor.matmul(pN[:, 0:P], ones[:], keysq[:], start=True, stop=True).then_inc(knp, 1)
                with pe.Fori(0, BLOCKS) as j:
                    for m in range(QCH):
                        pe.wait_ge(qo, j * QCH + m + 1)
                        for d in range(DC):
                            bank = (pS[:, m, :] if m < 2 else pG[:, m - 2, :])
                            last = nc.tensor.matmul(bank, wq[:, d, m * P:(m + 1) * P], normT[:, d, bass.ds(j * BLK, BLK)],
                                                    start=d == 0, stop=d == DC - 1)
                        last.then_inc(qp, 1)
                pe.wait_ge(moment, 3)
                for m in range(QCH):
                    last = nc.tensor.matmul(pN[:, P:P + 2], heads[:], mv[:, m, :], start=m == 0, stop=m == QCH - 1)
                last.then_inc(knp, 1)

            @block.scalar
            def _(act):
                act.wait_ge(w_ok, W_ALL)
                nc.scalar.activation(keysq[:], keys[:], ACT.Square).then_inc(kn1, 1)
                act.wait_ge(knp, 1)
                nc.scalar.activation(knorm[:], pN[:, 0:P], ACT.Sqrt).then_inc(kn2, 1)
                with act.Fori(0, BLOCKS) as j:
                    for m in range(QCH):
                        bank = (pS[:, m, :] if m < 2 else pG[:, m - 2, :])
                        act.wait_ge(qp, j * QCH + m + 1)
                        nc.scalar.activation(q[:, m, bass.ds(j * BLK, BLK)], bank, ACT.Identity,
                                             bias=vec[:, m:m + 1]).then_inc(qo, 1)
                act.wait_ge(vstep, 6)
                nc.scalar.activation(mom[:, 3:4], mom[:, 2:3], ACT.Sqrt).then_inc(vstd, 1)

            @block.vector
            def _(dve):
                dve.wait_ge(kn2, 1)
                nc.vector.tensor_scalar(knorm[:], knorm[:], 1e-12, None, ALU.max).then_inc(vstep, 1)
                dve.wait_ge(vstep, 1)
                nc.vector.reciprocal(knorm[:], knorm[:]).then_inc(vstep, 1)
                dve.wait_ge(vstep, 2)
                nc.vector.tensor_tensor(keys[:], keys[:], knorm[:], ALU.mult).then_inc(vstep, 1)
                with dve.Fori(0, BLOCKS) as j:
                    for m in range(QCH):
                        dve.wait_ge(qo, j * QCH + m + 2)
                        nc.vector.bn_stats(stats[:, m, bass.ds(j, 1), :].rearrange("p a n -> p (a n)"),
                                           q[:, m, bass.ds(j * BLK, BLK)]).then_inc(stat, 1)
                dve.wait_ge(stat, BLOCKS * QCH)
                for m in range(QCH):
                    last = nc.vector.bn_aggr(mv[:, m, :], stats[:, m, :, :].rearrange("p a n -> p (a n)"))
                last.then_inc(moment, 1)
                dve.wait_ge(moment, 1)
                nc.vector.tensor_tensor(stats[:, :, 0, 0:1], mv[:, :, 0:1], mv[:, :, 0:1], ALU.mult).then_inc(moment, 1)
                dve.wait_ge(moment, 2)
                nc.vector.tensor_tensor(mv[:, :, 1:2], mv[:, :, 1:2], stats[:, :, 0, 0:1], ALU.add).then_inc(moment, 1)
                dve.wait_ge(knp, 2)
                nc.vector.tensor_copy(mom[:, 0:2], pN[:, P:P + 2]).then_inc(vstep, 1)
                dve.wait_ge(vstep, 4)
                nc.vector.scalar_tensor_tensor(mom[:, 2:3], mom[:, 0:1], mom[:, 0:1], mom[:, 1:2], ALU.mult,
                                               ALU.subtract).then_inc(vstep, 1)
                dve.wait_ge(vstep, 5)
                nc.vector.tensor_scalar(mom[:, 2:3], mom[:, 2:3], -1.0, EPS, ALU.mult, ALU.add).then_inc(vstep, 1)
                dve.wait_ge(vstd, 1)
                nc.vector.reciprocal(mom[:, 3:4], mom[:, 3:4]).then_inc(vstep, 1)
                dve.wait_ge(vstep, 7)
                nc.vector.tensor_tensor(ab[:, 0:1], mom[:, 3:4], vec[:, QCH:QCH + 1], ALU.mult).then_inc(vstep, 1)
                dve.wait_ge(vstep, 8)
                nc.vector.tensor_tensor(mom[:, 1:2], mom[:, 0:1], ab[:, 0:1], ALU.mult).then_inc(vstep, 1)
                dve.wait_ge(vstep, 9)
                nc.vector.tensor_tensor(ab[:, 1:2], vec[:, QCH + 1:QCH + 2], mom[:, 1:2], ALU.subtract).then_inc(vstep, 1)

        with nc.Block() as block:
            @block.tensor
            def _(pe):
                with pe.Fori(0, BLOCKS) as j:
                    pe.wait_ge(sq_ok, j + 1)
                    for t in range(SUB):
                        for m in range(QCH):
                            at = t * SETS + m * SETS // QCH
                            last = nc.tensor.matmul(pN[:, at:at + SETS // QCH], qs[:, m, t * P:(t + 1) * P], halves[:],
                                                    start=True, stop=True)
                    last.then_inc(n2_ok, 1)
                    for t in range(SUB):
                        if t < 2:
                            pe.wait_ge(o_left, j * SUB + 2)
                        else:
                            pe.wait_ge(s_ok, j * SUB + t - 1 + 1)
                        for m in range(QCH):
                            last = nc.tensor.matmul(pS[:, t % 2, m * P:(m + 1) * P], qn[:, m, t * P:(t + 1) * P], keys[:],
                                                    start=True, stop=True)
                        last.then_inc(sc_ok, 1)
                        if t == 0:
                            for e in range(DC):
                                for d in range(DC):
                                    last = nc.tensor.matmul(pG[:, e, :], down[:, d, e * P:(e + 1) * P],
                                                            normT[:, d, bass.ds(j * BLK, BLK)], start=d == 0, stop=d == DC - 1)
                            last.then_inc(dot_ok, 1)
                    for t in range(SUB):
                        pe.wait_ge(wt_ok, j * SUB + t + 1)
                        for e in range(DC):
                            last = nc.tensor.transpose(pT[:, e, t * P:(t + 1) * P], wt[:, t % 2, e * P:(e + 1) * P], ident[:])
                        last.then_inc(turn_ok, 1)
                    pe.wait_ge(gw_ok, j * DC + DC + 1)
                    for t in range(SUB):
                        pe.wait_ge(o_left, j * SUB + t + 1)
                        for e in range(DC):
                            last = nc.tensor.matmul(pS[:, t % 2, 0:D], gw[:, e, t * P:(t + 1) * P], upw[:, e, :],
                                                    start=e == 0, stop=e == DC - 1)
                        last.then_inc(o_ok, 1)

            @block.scalar
            def _(act):
                act.nop().then_inc(sc_ok, 1)
                act.nop().then_inc(s_ok, 1)
                act.nop().then_inc(gw_ok, 1)
                with act.Fori(0, BLOCKS) as j:
                    act.wait_ge(sc_ok, j * SUB + 1)
                    nc.scalar.activation(qn[:], q[:, :, bass.ds(j * BLK, BLK)], ACT.Identity, scale=ab[:, 0:1],
                                         bias=ab[:, 1:2]).then_inc(qn_ok, 1)
                    act.wait_ge(qn_ok, j + 1)
                    nc.scalar.activation(qs[:], qn[:], ACT.Square).then_inc(sq_ok, 1)
                    act.wait_ge(n2_ok, j + 1)
                    act.wait_ge(s_ok, j * SUB + 1)
                    nc.scalar.activation(nrm[:, 0, :], pN[:, 0:SUB * SETS], ACT.Sqrt).then_inc(root_ok, 1)
                    act.wait_ge(dot_ok, j + 1)
                    act.wait_ge(gw_ok, j * DC + 1)
                    nc.scalar.activation(g[:], pG[:], ACT.Gelu).then_inc(g_ok, 1)
                    for t in range(SUB):
                        act.wait_ge(s_ok, j * SUB + t + 2)
                        nc.scalar.activation(ex[:, t % 2, :], s_[:, t % 2, :], ACT.Exp).then_inc(ex_ok, 1)

            @block.gpsimd
            def _(pool):
                with pool.Fori(0, BLOCKS) as j:
                    for t in range(SUB):
                        pool.wait_ge(a0_ok, j * SUB + t + 1)
                        first = a0[:, t % 2, :].rearrange("p (h a) -> p h a", h=PK_HEADS).unsqueeze(3)
                        second = pm[:, t % 2, :].rearrange("p (h f b) -> p h f b", h=PK_HEADS, f=2)[:, :, 1:2, :]
                        shape = (P, PK_HEADS, ROWS_IN, NKEY)
                        nc.gpsimd.tensor_tensor(prod[:, t % 2].rearrange("p h (a b) -> p h a b", a=ROWS_IN),
                                                first.broadcast_to(shape), second.broadcast_to(shape), ALU.mult).then_inc(prod_ok, 1)

            PER_T = 14
            @block.vector
            def _(dve):
                dve.nop().then_inc(ex_ok, 1)
                dve.nop().then_inc(prod_ok, 1)
                dve.nop().then_inc(turn_ok, 1)
                dve.nop().then_inc(o_ok, 1)
                dve.nop().then_inc(o_left, 2)
                with dve.Fori(0, BLOCKS) as j:
                    st = Steps(step, 2 + PER_T * SUB, j)

                    def then(ins):
                        dve.wait_ge(step, st.at(st.inc(ins)))

                    dve.wait_ge(root_ok, j + 1)
                    then(nc.vector.tensor_scalar(nrm[:, 0, :], nrm[:, 0, :], 1e-12, None, ALU.max))
                    then(nc.vector.reciprocal(nrm[:, 1, :], nrm[:, 0, :]))

                    def front(t):
                        u = t % 2
                        dve.wait_ge(sc_ok, j * SUB + t + 2)
                        s3 = s_[:, u, :].rearrange("p (a k) -> p a k", k=NKEY)
                        dve.wait_ge(ex_ok, j * SUB + max(t - 1, 0) + 1)
                        nc.vector.tensor_tensor(s3, pS[:, u, :].rearrange("p (a k) -> p a k", k=NKEY),
                                                nrm[:, 1, t * SETS:(t + 1) * SETS].unsqueeze(2).broadcast_to((P, SETS, NKEY)),
                                                ALU.mult).then_inc(s_ok, 1)
                        dve.wait_ge(s_ok, j * SUB + t + 2)
                        dve.nop().then_inc(relay, 1)
                        for k in range(SETS):
                            last = nc.vector.max(top[:, k, :], s3[:, k, :])
                        then(last)
                        then(nc.vector.memset(top[:, :, TOPK_DIM:], 9.0))
                        dve.nop().then_inc(relay, 1)
                        for k in range(SETS):
                            last = nc.vector.match_replace(rep[:, k * NKEY:(k + 1) * NKEY], top[:, k, :], s3[:, k, :], -1000.0)
                        then(last)
                        dve.wait_ge(ex_ok, j * SUB + t + 2)
                        dve.wait_ge(prod_ok, j * SUB + max(t - 1, 0) + 1)
                        then(nc.vector.scalar_tensor_tensor(pm[:, u, :], rep[:], -500.0, ex[:, u, :], ALU.is_lt, ALU.mult))
                        p4 = pm[:, u, :].rearrange("p (h f k) -> p h f k", h=PK_HEADS, f=2)
                        then(nc.vector.tensor_reduce(z[:], p4, AX_X, ALU.add))
                        z3 = z[:].rearrange("p (h f) -> p h f", f=2)
                        st.inc(nc.vector.tensor_reduce(small[:, 2, :], p4[:, :, 0, ROWS_IN:], AX_X, ALU.add))
                        then(nc.vector.tensor_tensor(small[:, 0, :], z3[:, :, 0], z3[:, :, 1], ALU.mult))
                        then(nc.vector.reciprocal(small[:, 1, :], small[:, 0, :]))
                        nc.vector.tensor_tensor(a0[:, u, :].rearrange("p (h a) -> p h a", h=PK_HEADS), p4[:, :, 0, 0:ROWS_IN],
                                                small[:, 1, :].unsqueeze(2).broadcast_to((P, PK_HEADS, ROWS_IN)),
                                                ALU.mult).then_inc(a0_ok, 1)
                        then(nc.vector.tensor_tensor(small[:, 3, :], small[:, 2, :], small[:, 1, :], ALU.mult))
                        then(nc.vector.tensor_tensor(small[:, 0, :], small[:, 3, :], z3[:, :, 1], ALU.mult))
                        then(nc.vector.tensor_reduce(last_w[:, u:u + 1], small[:, 0, :], AX_X, ALU.add))

                    def back(t):
                        u = t % 2
                        dve.wait_ge(prod_ok, j * SUB + t + 2)
                        dve.wait_ge(turn_ok, j * SUB + max(t - 1, 0) + 1)
                        then(nc.vector.tensor_reduce(wt[:, u, :], prod[:, u].rearrange("p h e -> p e h"), AX_X, ALU.add))
                        e = slice(PK_EXP - 1, PK_EXP)
                        nc.vector.tensor_tensor(wt[:, u, e], wt[:, u, e], last_w[:, u:u + 1], ALU.add).then_inc(wt_ok, 1)

                    for t in range(SUB + 1):
                        if t < SUB:
                            front(t)
                        if t:
                            back(t - 1)
                    dve.wait_ge(turn_ok, j * SUB + SUB + 1)
                    dve.wait_ge(g_ok, j + 1)
                    dve.wait_ge(o_ok, j * SUB + 1)
                    for e in range(DC):
                        nc.vector.tensor_tensor(gw[:, e, :], g[:, e, :], pT[:, e, :], ALU.mult).then_inc(gw_ok, 1)
                    for t in range(SUB):
                        dve.wait_ge(o_ok, j * SUB + t + 2)
                        row = res[:, bass.ds(j * SUB + t, 1), :].rearrange("p a n -> p (a n)")
                        nc.vector.tensor_tensor(row, row, pS[:, t % 2, 0:D], ALU.add).then_inc(o_left, 1)
                    assert st.n <= st.per
                    while st.n < st.per:
                        st.inc(dve.nop())


def norm_second(nc, sem, res, rows, normT, ident):
    with ExitStack() as c:
        def sb(name, shape, dt=F32):
            return c.enter_context(nc.sbuf_tensor("n2_" + name, shape, dt))
        xn = sb("xn", [P, 2, SUB, D])
        stats = sb("stats", [P, SUB, 6])
        mv = sb("mv", [P, SUB, 2])
        std = sb("std", [P, SUB])
        rstd = sb("rstd", [P, SUB])
        ps = c.enter_context(nc.psum_tensor("n2_ps", [P, 2, DC, BLK], F32))
        stat, var_ok, std_ok, xn_ok, turned, left, kept, relay = (
            sem("n2_" + n) for n in ("stat", "var_ok", "std_ok", "xn_ok", "turned", "left", "kept", "relay"))
        with nc.Block() as block:
            @block.vector
            def _(dve):
                dve.nop().then_inc(kept, 1)
                with dve.Fori(0, BLOCKS // 2) as jj:
                    for h in range(2):
                        j = jj * 2 + h
                        dve.wait_ge(kept, j + 1)
                        for s in range(SUB):
                            row = res[:, bass.ds(j * SUB + s, 1), :].rearrange("p a n -> p (a n)")
                            nc.vector.bn_stats(stats[:, s, :], row).then_inc(stat, 1)
                        dve.wait_ge(stat, j * 2 * SUB + SUB)
                        dve.nop().then_inc(relay, 1)
                        for s in range(SUB):
                            nc.vector.bn_aggr(mv[:, s, :], stats[:, s, :]).then_inc(stat, 1)
                        dve.wait_ge(stat, j * 2 * SUB + 2 * SUB)
                        nc.vector.tensor_scalar(std[:], mv[:, :, 1], EPS, None, ALU.add).then_inc(var_ok, 1)
                        dve.wait_ge(std_ok, j + 1)
                        nc.vector.reciprocal(rstd[:], std[:]).then_inc(var_ok, 1)
                        dve.wait_ge(var_ok, j * 2 + 2)
                        for s in range(SUB):
                            row = res[:, bass.ds(j * SUB + s, 1), :].rearrange("p a n -> p (a n)")
                            nc.vector.tensor_scalar(xn[:, h, s, :], row, mv[:, s, 0:1], rstd[:, s:s + 1],
                                                    ALU.subtract, ALU.mult).then_inc(xn_ok, 1)

            @block.gpsimd
            def _(pool):
                with pool.Fori(0, BLOCKS // 2) as jj:
                    for h in range(2):
                        j = jj * 2 + h
                        pool.wait_ge(xn_ok, j * SUB + SUB)
                        nc.gpsimd.tensor_copy(rows[:, bass.ds(j * SUB, SUB), :], xn[:, h]).then_inc(kept, 1)

            @block.tensor
            def _(pe):
                with pe.Fori(0, BLOCKS // 2) as jj:
                    for h in range(2):
                        j = jj * 2 + h
                        pe.wait_ge(xn_ok, j * SUB + SUB)
                        pe.wait_ge(left, j + 1)
                        for d in range(DC):
                            for s in range(SUB):
                                last = nc.tensor.transpose(ps[:, h, d, s * P:(s + 1) * P], xn[:, h, s, d * P:(d + 1) * P], ident[:])
                        last.then_inc(turned, 1)

            @block.scalar
            def _(act):
                act.nop().then_inc(left, 2)
                with act.Fori(0, BLOCKS // 2) as jj:
                    for h in range(2):
                        j = jj * 2 + h
                        act.wait_ge(var_ok, j * 2 + 1)
                        nc.scalar.activation(std[:], std[:], ACT.Sqrt).then_inc(std_ok, 1)
                        act.wait_ge(turned, j + 1)
                        nc.scalar.activation(normT[:, :, bass.ds(j * BLK, BLK)], ps[:, h], ACT.Copy).then_inc(left, 1)


def project(nc, sem, inp, normT, rowsT, v_pad, logits):
    with ExitStack() as c:
        def sb(name, shape, dt=F32):
            return c.enter_context(nc.sbuf_tensor("pj_" + name, shape, dt))
        w = [sb("w" + n, [P, DC, D]) for n in "qkv"]
        b = [sb("b" + n, [P, 2]) for n in "qk"]
        bv = sb("bv", [P, D])
        gate = sb("gate", [P, DC, EXPERTS])
        gate_b = sb("gate_b", [P, EXPERTS])
        cos = sb("cos", [P, SEQ])
        sin = sb("sin", [P, SEQ])
        xT = sb("xT", [P, DC, BLK])
        turn = sb("turn", [P, 4, BLK])
        r = sb("r", [P, 2, BLK])
        rest = sb("rest", [P, 2, BLK])
        parts = sb("parts", [P, 2, 3, 2, BLK], BF16)
        vp = sb("vp", [P, SUB, HEADS, PADV])
        pE = c.enter_context(nc.psum_tensor("pj_pE", [P, 4, BLK], F32))
        pV = c.enter_context(nc.psum_tensor("pj_pV", [P, 2, BLK], F32))
        pL = c.enter_context(nc.psum_tensor("pj_pL", [P, BLK], F32))
        (w_ok, x_ok, p_ok, p_left, v_ok, v_left, l_ok, l_left, rot, r_ok, part0, part1, part2, rest1, vp_ok, stored,
         vstored, v_clean) = (sem("pj_" + n) for n in (
             "w_ok", "x_ok", "p_ok", "p_left", "v_ok", "v_left", "l_ok", "l_left", "rot", "r_ok", "part0", "part1",
             "part2", "rest1", "vp_ok", "stored", "vstored", "v_clean"))
        PB = SEQ // BLK
        v_by_batch = v_pad.rearrange("(b g) p t c -> b t p g c", b=BATCH)
        with nc.Block() as block:
            @block.sync
            def _(sp):
                loads = [(w[0], inp["Wq"]), (w[1], inp["Wk"]), (w[2], inp["Wv"]), (b[0], inp["bq"]), (b[1], inp["bk"]),
                         (gate, inp["gate"]), (cos, inp["c_cos"]), (sin, inp["c_sin"]),
                         (bv, inp["bv"].broadcast_to((P, D))), (gate_b, inp["gate_b"].broadcast_to((P, EXPERTS)))]
                assert len(loads) == 10
                for t, src in loads:
                    sp.dma_start(t[:], src).then_inc(w_ok, 16)
                with sp.Fori(0, BATCH) as bt:
                    with sp.Fori(0, PB) as i:
                        j = bt * PB + i
                        for qk in range(2):
                            sp.wait_ge(part2, j * 2 + qk + 2)
                            for half in range(2):
                                sp.dma_start(rowsT[qk, :, bass.ds(bt * D + half * P, P), bass.ds(i * BLK, BLK)]
                                             .rearrange("a p t -> p a t"),
                                             parts[:, qk, :, half, :]).then_inc(stored, 16)
                        sp.wait_ge(vp_ok, j * SUB + SUB)
                        for s in range(SUB):
                            sp.dma_start(v_by_batch[bass.ds(bt, 1), bass.ds(i * SUB + s, 1), :, :, :]
                                         .rearrange("a t p g c -> (a t p) g c"),
                                         vp[:, s].rearrange("p (g h) c -> p g (h c)", g=HG)).then_inc(vstored, 16)
                        sp.wait_ge(stored, j * 64 + 64)
                        sp.wait_ge(vstored, j * 64 + 64)
                        sp.nop().then_inc(v_clean, 1)
            W_ALL = 160

            @block.gpsimd
            def _(pool):
                pool.nop().then_inc(l_ok, 1)
                pool.nop().then_inc(part2, 1)
                nc.gpsimd.memset(vp[:, :, :, HD:], 0.0).then_inc(x_ok, 1)
                pool.wait_ge(x_ok, 1)
                nc.gpsimd.memset(vp[:, :, :, HD:HD + 1], 1.0).then_inc(x_ok, 1)
                pool.wait_ge(x_ok, 2)
                with pool.Fori(0, BLOCKS) as j:
                    pool.wait_ge(l_ok, j + 1)
                    nc.gpsimd.tensor_copy(xT[:], normT[:, :, bass.ds(j * BLK, BLK)]).then_inc(x_ok, 1)
                    for qk in range(2):
                        pool.wait_ge(part0, j * 2 + qk + 1)
                        pool.wait_ge(part2, j * 2 + qk + 1)
                        nc.gpsimd.tensor_tensor(rest[:], r[:], parts[:, qk, 0], ALU.subtract).then_inc(rest1, 1)
                        pool.wait_ge(part1, j * 2 + qk + 1)
                        nc.gpsimd.tensor_tensor(parts[:, qk, 2], rest[:], parts[:, qk, 1], ALU.subtract).then_inc(part2, 1)

            @block.scalar
            def _(act):
                act.nop().then_inc(v_clean, 1)
                with act.Fori(0, BLOCKS) as j:
                    act.wait_ge(v_clean, j + 1)
                    for qk in range(2):
                        act.wait_ge(r_ok, j * 2 + qk + 2)
                        nc.scalar.activation(parts[:, qk, 0], r[:], ACT.Copy).then_inc(part0, 1)
                        act.wait_ge(rest1, j * 2 + qk + 2)
                        nc.scalar.activation(parts[:, qk, 1], rest[:], ACT.Copy).then_inc(part1, 1)

            @block.tensor
            def _(pe):
                pe.nop().then_inc(l_left, 1)
                pe.wait_ge(w_ok, W_ALL)
                with pe.Fori(0, BLOCKS) as j:
                    pe.wait_ge(x_ok, j + 3)
                    for qk in range(2):
                        pe.wait_ge(p_left, j * 2 + qk + 1)
                        for eo in range(2):
                            for d in range(DC):
                                last = nc.tensor.matmul(pE[:, qk * 2 + eo, :], w[qk][:, d, eo * P:(eo + 1) * P], xT[:, d, :],
                                                        start=d == 0, stop=d == DC - 1)
                        last.then_inc(p_ok, 1)
                    for s in range(SUB):
                        pe.wait_ge(v_left, j * SUB + s + 1)
                        for d in range(DC):
                            last = nc.tensor.matmul(pV[:, s % 2, 0:D], xT[:, d, s * P:(s + 1) * P], w[2][:, d, :],
                                                    start=d == 0, stop=d == DC - 1)
                        last.then_inc(v_ok, 1)
                    pe.wait_ge(l_left, j + 1)
                    for s in range(SUB):
                        for d in range(DC):
                            last = nc.tensor.matmul(pL[:, s * EXPERTS:(s + 1) * EXPERTS], xT[:, d, s * P:(s + 1) * P], gate[:, d, :],
                                                    start=d == 0, stop=d == DC - 1)
                    last.then_inc(l_ok, 1)

            @block.vector
            def _(dve):
                dve.nop().then_inc(r_ok, 1)
                dve.nop().then_inc(rest1, 1)
                dve.nop().then_inc(p_left, 2)
                dve.nop().then_inc(v_left, 2)
                dve.wait_ge(w_ok, W_ALL)
                with dve.Fori(0, BATCH) as bt:
                    with dve.Fori(0, PB) as i:
                        j = bt * PB + i
                        at = bass.ds(i * BLK, BLK)
                        for qk in range(2):
                            dve.wait_ge(p_ok, j * 2 + qk + 1)
                            dve.wait_ge(r_ok, j * 2 + qk + 1)
                            for k, (eo, table) in enumerate(((0, cos), (0, sin), (1, sin), (1, cos))):
                                last = nc.vector.scalar_tensor_tensor(turn[:, k, :], pE[:, qk * 2 + eo, :], b[qk][:, eo:eo + 1],
                                                                      table[:, at], ALU.add, ALU.mult)
                                last.then_inc(rot, 1)
                            dve.wait_ge(rot, (j * 2 + qk) * 4 + 4)
                            dve.nop().then_inc(p_left, 1)
                            dve.wait_ge(rest1, j * 2 + qk + 1)
                            nc.vector.tensor_tensor(r[:], turn[:, 0:2, :], turn[:, 2:4, :], ALU.subtract).then_inc(r_ok, 1)
                        dve.wait_ge(v_clean, j + 1)
                        dve.wait_ge(x_ok, 2)
                        for s in range(SUB):
                            dve.wait_ge(v_ok, j * SUB + s + 1)
                            nc.vector.tensor_tensor(vp[:, s, :, 0:HD], pV[:, s % 2, 0:D].rearrange("p (h c) -> p h c", c=HD),
                                                    bv[:].rearrange("p (h c) -> p h c", c=HD), ALU.add).then_inc(v_left, 1)
                            dve.wait_ge(v_left, j * SUB + s + 3)
                            dve.nop().then_inc(vp_ok, 1)
                        dve.wait_ge(l_ok, j + 2)
                        lg = logits[:, bass.ds(j * SUB, SUB), :]
                        nc.vector.tensor_tensor(lg, pL[:, 0:SUB * EXPERTS].rearrange("p (s e) -> p s e", e=EXPERTS),
                                                gate_b[:].unsqueeze(1).broadcast_to((P, SUB, EXPERTS)), ALU.add).then_inc(l_left, 1)


def route(nc, sem, inp, rows, logits, weight, gather_at, moe_in):
    TE = TILES * EXPERTS
    with ExitStack() as c:
        def sb(name, shape, dt=F32):
            return c.enter_context(nc.sbuf_tensor("rt_" + name, shape, dt))
        before = sb("before", [P, P])
        ones = sb("ones", [P, P])
        expert = sb("expert", [P, EXPERTS])
        trash = sb("trash", [P, TILES])
        e = sb("e", [P, TILES, EXPERTS])
        hot = sb("hot", [P, TILES, EXPERTS])
        cand = sb("cand", [P, TILES, EXPERTS])
        sums = sb("sums", [P, 2, TILES, EXPERTS])
        at = sb("at", [P, TILES, EXPERTS])
        v = sb("v", [P, 12, TILES])
        scatter_at = sb("scatter_at", [P, TILES], I32)
        pc = c.enter_context(nc.psum_tensor("rt_pc", [P, 2, BLK], F32))
        w_ok, step, exp_ok, cum, where_ok, sent = (sem("rt_" + n) for n in ("w_ok", "step", "exp_ok", "cum", "where_ok", "sent"))
        MX, SUM, IDX, POS, KEEP, SLOT, FAR, TMP = range(8)
        with nc.Block() as block:
            @block.sync
            def _(sp):
                for t, name in ((before, "c_before"), (ones, "c_ones"), (expert, "c_expert"), (trash, "c_trash")):
                    sp.dma_start(t[:], inp[name]).then_inc(w_ok, 16)

            @block.tensor
            def _(pe):
                pe.wait_ge(w_ok, 64)
                pe.wait_ge(step, 7)
                nc.tensor.matmul(pc[:, 0, 0:TE], before[:], hot[:].rearrange("p t e -> p (t e)"), start=True, stop=True)
                nc.tensor.matmul(pc[:, 1, 0:TE], ones[:], hot[:].rearrange("p t e -> p (t e)"), start=True,
                                 stop=True).then_inc(cum, 1)

            @block.scalar
            def _(act):
                act.wait_ge(step, 2)
                nc.scalar.activation(e[:], e[:], ACT.Exp).then_inc(exp_ok, 1)

            @block.vector
            def _(dve):
                st = Steps(step, 99)

                def then(ins):
                    dve.wait_ge(step, st.at(st.inc(ins)))

                def by_token(k):
                    return v[:, k, :].unsqueeze(2).broadcast_to((P, TILES, EXPERTS))

                per_expert = expert[:].unsqueeze(1).broadcast_to((P, TILES, EXPERTS))
                dve.wait_ge(w_ok, 64)
                then(nc.vector.tensor_reduce(v[:, MX, :], logits[:], AX_X, ALU.max))
                then(nc.vector.tensor_tensor(e[:], logits[:], by_token(MX), ALU.subtract))
                then(nc.vector.tensor_tensor(hot[:], logits[:], by_token(MX), ALU.is_equal))
                then(nc.vector.tensor_scalar(cand[:], hot[:], -float(EXPERTS), None, ALU.mult))
                then(nc.vector.tensor_tensor(cand[:], cand[:], per_expert, ALU.add))
                then(nc.vector.tensor_reduce(v[:, IDX, :], cand[:], AX_X, ALU.min))
                then(nc.vector.tensor_tensor(hot[:], cand[:], by_token(IDX), ALU.is_equal))
                then(nc.vector.tensor_scalar(v[:, IDX, :], v[:, IDX, :], float(EXPERTS), None, ALU.add))
                dve.wait_ge(exp_ok, 1)
                then(nc.vector.tensor_reduce(v[:, SUM, :], e[:], AX_X, ALU.add))
                then(nc.vector.reciprocal(v[:, MX, :], v[:, SUM, :]))
                dve.wait_ge(cum, 1)
                then(nc.vector.memset(sums[:], 0.0))
                then(nc.vector.tensor_copy(sums[:, 0, 1:, :], pc[:, 1, 0:TE].rearrange("p (t e) -> p t e", e=EXPERTS)[:, :TILES - 1]))
                cur, n = 0, 1
                while n < TILES:
                    st.inc(nc.vector.tensor_copy(sums[:, 1 - cur, 0:n, :], sums[:, cur, 0:n, :]))
                    then(nc.vector.tensor_tensor(sums[:, 1 - cur, n:, :], sums[:, cur, n:, :], sums[:, cur, :TILES - n, :], ALU.add))
                    cur, n = 1 - cur, 2 * n
                then(nc.vector.tensor_tensor(at[:], sums[:, cur], pc[:, 0, 0:TE].rearrange("p (t e) -> p t e", e=EXPERTS), ALU.add))
                then(nc.vector.tensor_tensor(at[:], at[:], hot[:], ALU.mult))
                then(nc.vector.tensor_reduce(v[:, POS, :], at[:], AX_X, ALU.add))
                then(nc.vector.tensor_scalar(v[:, KEEP, :], v[:, POS, :], float(CAP), None, ALU.is_le))
                then(nc.vector.tensor_tensor(weight[:], v[:, MX, :], v[:, KEEP, :], ALU.mult))
                then(nc.vector.tensor_scalar(v[:, POS, :], v[:, POS, :], -1.0, None, ALU.add))
                then(nc.vector.tensor_tensor(v[:, POS, :], v[:, POS, :], v[:, KEEP, :], ALU.mult))
                then(nc.vector.scalar_tensor_tensor(v[:, SLOT, :], v[:, IDX, :], float(CAP), v[:, POS, :], ALU.mult, ALU.add))
                then(nc.vector.tensor_tensor(v[:, FAR, :], trash[:], v[:, SLOT, :], ALU.subtract))
                then(nc.vector.tensor_scalar(v[:, TMP, :], v[:, KEEP, :], -1.0, 1.0, ALU.mult, ALU.add))
                then(nc.vector.tensor_tensor(v[:, FAR, :], v[:, FAR, :], v[:, TMP, :], ALU.mult))
                then(nc.vector.tensor_tensor(v[:, FAR, :], v[:, FAR, :], v[:, SLOT, :], ALU.add))
                nc.vector.tensor_copy(gather_at[:], v[:, SLOT, :]).then_inc(where_ok, 1)
                nc.vector.tensor_copy(scatter_at[:], v[:, FAR, :]).then_inc(where_ok, 1)

            @block.gpsimd
            def _(pool):
                pool.wait_ge(where_ok, 2)
                for t in range(TILES):
                    pool.indirect_dma_start(moe_in, bass.IndirectOffsetOnAxis(ap=scatter_at[:, t:t + 1], axis=0),
                                            rows[:, t, :], None).then_inc(sent, 16)
                pool.wait_ge(sent, 16 * TILES)


def attention(nc, sem, inp, res, rowsT, v_pad, ident, identb):
    G = BATCH * HG
    ROWS = MROW + 32
    STEPS = [4 * qt + SUB for qt in range(QT)]
    FIRST = [sum(STEPS[:qt]) for qt in range(QT)]
    PER = sum(STEPS)
    UNITS = [[(qs, ch) for qs in range(SUB) for ch in range(qt + 1)] for qt in range(QT)]
    UFIRST = [sum(len(u) for u in UNITS[:qt]) * HPG for qt in range(QT)]
    UPER = sum(len(u) for u in UNITS) * HPG
    with ExitStack() as c:
        def sb(name, shape, dt=F32):
            return c.enter_context(nc.sbuf_tensor("at_" + name, shape, dt))
        ctxt = sb("ctxt", [P, G, KT, HPG * HD])
        q = sb("q", [P, 2, HPG, SEQ], BF16)
        k = sb("k", [P, 2, HPG, SEQ], BF16)
        v = sb("v", [P, 2, KT, HPG * PADV])
        prob = sb("prob", [P, 3, HPG, BLK])
        masks = sb("masks", [P, 2, P])
        masksb = sb("masksb", [P, 2, P], BF16)
        mask_k, mask_q = masksb[:, 0, :], masksb[:, 1, :]
        peak = sb("peak", [P, HPG, SUB, QT])
        neg = sb("neg", [P, 2, HPG, SUB], BF16)
        mrow = sb("mrow", [P, BLK], BF16)
        o = sb("o", [P, BLK])
        inv = sb("inv", [P, SUB, HPG])
        bo = sb("bo", [P, D])
        wo = sb("wo", [P, DC, D])
        pS = c.enter_context(nc.psum_tensor("at_pS", [P, 2, 2, BLK], F32))
        pM = c.enter_context(nc.psum_tensor("at_pM", [P, 2, BLK], F32))
        pR = c.enter_context(nc.psum_tensor("at_pR", [P, BLK], F32))
        pO = c.enter_context(nc.psum_tensor("at_pO", [P, BLK], F32))
        names = ("w_ok", "set", "m_made", "m_left", "neg_ok", "row_made", "row_ok", "row_in",
                 "s_made", "p_ok", "pv", "o_made", "o_ok", "turned", "inv_ok", "ctx_ok", "kv_done", "relay")
        (w_ok, set_, m_made, m_left, neg_ok, row_made, row_ok, row_in,
         s_made, p_ok, pv, o_made, o_ok, turned, inv_ok, ctx_ok, kv_done, relay) = (sem("at_" + n) for n in names)
        g_in = [sem(f"at_g_in{s}") for s in range(2)]
        masks_ok = sem("at_masks_ok")
        G_IN = 16 * (2 * TERMS + 1)
        ITEMS = [(s, qt) for s in range(2) for qt in range(QT)]
        with nc.Block() as block:
            @block.sync
            def _(sp):
                for t, src in ((masks, inp["c_masks"]), (wo, inp["Wo"]),
                               (bo, inp["bo"].broadcast_to((P, D)))):
                    sp.dma_start(t[:], src).then_inc(w_ok, 16)
                with sp.Fori(0, G // 2) as gg:
                    for s in range(2):
                        g = gg * 2 + s
                        sp.wait_ge(kv_done, g + 1)
                        for t, parts, dst in ((0, PARTS_Q, q), (1, PARTS_K, k)):
                            for n, part in enumerate(parts):
                                src = rowsT[t, part, bass.ds(g * HPG * HD, HPG * HD), :].rearrange("(h d) s -> d h s", d=HD)
                                sp.dma_start(dst[n * HD:(n + 1) * HD, s], src).then_inc(g_in[s], 16)
                        sp.dma_start(v[:, s], v_pad[bass.ds(g, 1), :, :, :].rearrange("a p t c -> p (a t) c")).then_inc(g_in[s], 16)

            @block.gpsimd
            def _(pool):
                for s in range(2):
                    nc.gpsimd.memset(q[MROW:, s], 0.0).then_inc(set_, 1)
                    nc.gpsimd.memset(k[MROW:, s], 0.0).then_inc(set_, 1)
                pool.wait_ge(set_, 4)
                for s in range(2):
                    nc.gpsimd.memset(k[MROW:MROW + 1, s], 1.0).then_inc(set_, 1)
                pool.wait_ge(w_ok, 48)
                pool.wait_ge(set_, 6)
                for t in range(TILES):
                    nc.gpsimd.tensor_tensor(res[:, t, :], res[:, t, :], bo[:], ALU.add)
                with pool.Fori(0, G // 2) as gg:
                    for it, (s, qt) in enumerate(ITEMS):
                        pool.wait_ge(row_ok, gg * len(ITEMS) + it + 2)
                        pool.nop().then_inc(relay, 1)
                        for h in range(HPG):
                            pool.dma_start(q[MROW:MROW + 1, s, h, qt * BLK:(qt + 1) * BLK], mrow[32 * h:32 * h + 1, :]).then_inc(row_in, 16)

            @block.tensor
            def _(pe):
                pe.nop().then_inc(row_ok, 1)
                pe.nop().then_inc(ctx_ok, 1)
                pe.nop().then_inc(o_ok, 1)
                pe.wait_ge(w_ok, 48)
                pe.wait_ge(set_, 6)
                pe.wait_ge(masks_ok, 1)
                with pe.Fori(0, G // 2) as gg:
                    def first_pass(it, lo, hi):
                        s, qt = ITEMS[it]
                        g = gg * 2 + s
                        for n in range(lo, hi):
                            (qs, ch), h = UNITS[qt][n // HPG], n % HPG
                            i = 4 * qt + qs
                            width = min(BLK, P * (i + 1) - BLK * ch)
                            u = UFIRST[qt] + n
                            pe.wait_ge(m_left, g * UPER + u + 1)
                            last = nc.tensor.matmul(pM[:, u % 2, 0:width], q[0:MROW, s, h, i * P:(i + 1) * P],
                                                    k[0:MROW, s, h, ch * BLK:ch * BLK + width], start=True, stop=ch < qt)
                            if ch == qt:
                                last = nc.tensor.matmul(pM[:, u % 2, width - P:width], identb[:], mask_k, start=False, stop=True)
                            last.then_inc(m_made, 1)

                    def maxima_row(it):
                        n = gg * len(ITEMS) + it
                        pe.wait_ge(neg_ok, n + 2)
                        pe.wait_ge(row_ok, n + 1)
                        pe.wait_ge(ctx_ok, gg * len(ITEMS) + max(it - 1, 0) + 1)
                        for h in range(HPG):
                            for qs in range(SUB):
                                last = nc.tensor.matmul(pR[32 * h:32 * h + 1, qs * P:(qs + 1) * P], neg[:, it % 2, h, qs:qs + 1], identb[:],
                                                        start=True, stop=True, tile_position=(0, 32 * h))
                        last.then_inc(row_made, 1)

                    def scores(it, kt):
                        s, qt = ITEMS[it]
                        g = gg * 2 + s
                        n = FIRST[qt] + kt
                        r = max(0, kt - 4 * qt)
                        for pair in range(2):
                            pe.wait_ge(p_ok, (g * PER + n) * 2 + pair + 1)
                            for x in range(2):
                                h = pair * 2 + x
                                diag = kt >= 4 * qt
                                last = nc.tensor.matmul(pS[:, pair, x, r * P:], k[0:ROWS, s, h, kt * P:(kt + 1) * P],
                                                        q[0:ROWS, s, h, qt * BLK + r * P:(qt + 1) * BLK], start=True, stop=not diag)
                                if diag:
                                    last = nc.tensor.matmul(pS[:, pair, x, r * P:(r + 1) * P], identb[:], mask_q, start=False, stop=True)
                            last.then_inc(s_made, 1)

                    def values(it, kt):
                        s, qt = ITEMS[it]
                        g = gg * 2 + s
                        n = FIRST[qt] + kt
                        r = max(0, kt - 4 * qt)
                        if kt == 0:
                            pe.wait_ge(o_ok, g * QT + qt + 1)
                        pe.wait_ge(p_ok, (g * PER + n) * 2 + 4)
                        for h in range(HPG):
                            last = nc.tensor.matmul(pO[32 * h:32 * (h + 1), r * P:], v[:, s, kt, h * PADV:(h + 1) * PADV],
                                                    prob[:, n % 3, h, r * P:], start=kt == 0, stop=kt == STEPS[qt] - 1,
                                                    tile_position=(0, 32 * h))
                        last.then_inc(pv, 1)

                    def turn_out(it):
                        n = gg * len(ITEMS) + it
                        pe.wait_ge(o_ok, n + 2)
                        pe.wait_ge(row_ok, gg * len(ITEMS) + min(it + 2, len(ITEMS)) + 1)
                        pe.wait_ge(ctx_ok, n + 1)
                        for qs in range(SUB):
                            last = nc.tensor.transpose(pR[:, qs * P:(qs + 1) * P], o[:, qs * P:(qs + 1) * P], ident[:])
                        last.then_inc(turned, 1)

                    pe.wait_ge(g_in[0], (gg + 1) * G_IN)
                    first_pass(0, 0, len(UNITS[0]) * HPG)
                    maxima_row(0)
                    for it, (s, qt) in enumerate(ITEMS):
                        pe.wait_ge(row_in, (gg * len(ITEMS) + it + 1) * 16 * HPG)
                        more = len(UNITS[ITEMS[it + 1][1]]) * HPG if it + 1 < len(ITEMS) else 0
                        if more and ITEMS[it + 1][1] == 0:
                            pe.wait_ge(g_in[1], (gg + 1) * G_IN)
                        done = 0
                        scores(it, 0)
                        for kt in range(STEPS[qt]):
                            if kt + 1 < STEPS[qt]:
                                scores(it, kt + 1)
                            upto = more * (kt + 1) // STEPS[qt]
                            if upto > done:
                                first_pass(it + 1, done, upto)
                            done = upto
                            values(it, kt)
                        if qt == QT - 1:
                            pe.wait_ge(pv, (gg * 2 + s + 1) * PER + 1)
                            pe.nop().then_inc(kv_done, 1)
                        if more:
                            maxima_row(it + 1)
                        turn_out(it)

            @block.scalar
            def _(act):
                act.nop().then_inc(pv, 1)
                act.wait_ge(w_ok, 48)
                nc.scalar.activation(masksb[:], masks[:], ACT.Copy).then_inc(masks_ok, 1)
                act.nop().then_inc(p_ok, 2)
                with act.Fori(0, G // 2) as gg:
                    for s, qt in ITEMS:
                        g = gg * 2 + s
                        for kt in range(STEPS[qt]):
                            n = FIRST[qt] + kt
                            r = max(0, kt - 4 * qt)
                            for pair in range(2):
                                act.wait_ge(s_made, (g * PER + n) * 2 + pair + 1)
                                if n >= 3:
                                    act.wait_ge(pv, g * PER + n - 2 + 1)
                                else:
                                    act.wait_ge(pv, g * PER + 1)
                                nc.scalar.activation(prob[:, n % 3, pair * 2:pair * 2 + 2, r * P:], pS[:, pair, :, r * P:],
                                                     ACT.Exp, scale=HD ** -0.5).then_inc(p_ok, 1)

            @block.vector
            def _(dve):
                dve.nop().then_inc(neg_ok, 1)
                dve.nop().then_inc(turned, 1)
                dve.nop().then_inc(m_left, 2)
                dve.nop().then_inc(kv_done, 2)
                with dve.Fori(0, G // 2) as gg:
                    def maxima(it):
                        s, qt = ITEMS[it]
                        g, n = gg * 2 + s, gg * len(ITEMS) + it
                        dve.wait_ge(neg_ok, n + 1)
                        for u in range(len(UNITS[qt]) * HPG):
                            (qs, ch), h = UNITS[qt][u // HPG], u % HPG
                            i = 4 * qt + qs
                            width = min(BLK, P * (i + 1) - BLK * ch)
                            x = UFIRST[qt] + u
                            dve.wait_ge(m_made, g * UPER + x + 1)
                            nc.vector.tensor_reduce(peak[:, h, qs, ch:ch + 1], pM[:, x % 2, 0:width], AX_X, ALU.max).then_inc(m_left, 1)
                        dve.wait_ge(m_left, g * UPER + UFIRST[qt] + len(UNITS[qt]) * HPG + 2)
                        nc.vector.tensor_reduce(neg[:, it % 2], peak[:, :, :, 0:qt + 1], AX_X, ALU.max, negate=True).then_inc(neg_ok, 1)
                        dve.wait_ge(row_made, n + 1)
                        for h in range(HPG):
                            last = nc.vector.tensor_copy(mrow[32 * h:32 * h + 1, :], pR[32 * h:32 * h + 1, :])
                        last.then_inc(row_ok, 1)

                    def outputs(it):
                        s, qt = ITEMS[it]
                        g, n = gg * 2 + s, gg * len(ITEMS) + it
                        dve.wait_ge(pv, g * PER + FIRST[qt] + STEPS[qt] + 1)
                        dve.wait_ge(turned, n + 1)
                        nc.vector.tensor_copy(o[:], pO[:]).then_inc(o_ok, 1)
                        dve.wait_ge(turned, n + 2)
                        t4 = pR[:].rearrange("p (s h c) -> p s h c", s=SUB, h=HPG)
                        dve.wait_ge(ctx_ok, n + 1)
                        nc.vector.reciprocal(inv[:], t4[:, :, :, HD]).then_inc(inv_ok, 1)
                        dve.wait_ge(inv_ok, n + 1)
                        to = ctxt[:, bass.ds(g, 1), qt * SUB:(qt + 1) * SUB, :].rearrange("p a s (h c) -> p (a s) h c", h=HPG)
                        nc.vector.tensor_tensor(to, t4[:, :, :, 0:HD], inv[:].unsqueeze(3).broadcast_to((P, SUB, HPG, HD)),
                                                ALU.mult).then_inc(ctx_ok, 1)

                    maxima(0)
                    for it in range(len(ITEMS)):
                        if it + 1 < len(ITEMS):
                            maxima(it + 1)
                        outputs(it)

        with ExitStack() as c3:
            cx = c3.enter_context(nc.sbuf_tensor("ao_cx", [P, SUB, D], F32))
            cT = c3.enter_context(nc.sbuf_tensor("ao_cT", [P, DC, BLK], F32))
            got, turned2, cT_ok, made, left = (sem("ao_" + n) for n in ("got", "turned", "cT_ok", "made", "left"))
            with nc.Block() as block:
                @block.gpsimd
                def _(pool):
                    pool.nop().then_inc(turned2, 1)
                    with pool.Fori(0, BATCH) as b:
                        with pool.Fori(0, QT) as i:
                            j = b * QT + i
                            pool.wait_ge(turned2, j + 1)
                            nc.gpsimd.tensor_copy(cx[:].rearrange("p s (g c) -> p g s c", g=HG),
                                                  ctxt[:, bass.ds(b * HG, HG), bass.ds(i * SUB, SUB), :]).then_inc(got, 1)

                @block.tensor
                def _(pe):
                    pe.nop().then_inc(cT_ok, 1)
                    with pe.Fori(0, BLOCKS) as j:
                        pe.wait_ge(got, j + 1)
                        pe.wait_ge(cT_ok, j + 1)
                        for d in range(DC):
                            for s in range(SUB):
                                last = nc.tensor.transpose(pS[:, 0, d, s * P:(s + 1) * P], cx[:, s, d * P:(d + 1) * P], ident[:])
                        last.then_inc(turned2, 1)
                        pe.wait_ge(cT_ok, j + 2)
                        for s in range(SUB):
                            pe.wait_ge(left, j * SUB + s + 1)
                            for d in range(DC):
                                last = nc.tensor.matmul(pM[:, s % 2, 0:D], cT[:, d, s * P:(s + 1) * P], wo[:, d, :],
                                                        start=d == 0, stop=d == DC - 1)
                            last.then_inc(made, 1)

                @block.scalar
                def _(act):
                    act.nop().then_inc(made, 1)
                    with act.Fori(0, BLOCKS) as j:
                        act.wait_ge(turned2, j + 2)
                        act.wait_ge(made, j * SUB + 1)
                        nc.scalar.activation(cT[:], pS[:, 0], ACT.Copy).then_inc(cT_ok, 1)

                @block.vector
                def _(dve):
                    dve.nop().then_inc(left, 2)
                    with dve.Fori(0, BLOCKS) as j:
                        for s in range(SUB):
                            dve.wait_ge(made, j * SUB + s + 2)
                            row = res[:, bass.ds(j * SUB + s, 1), :].rearrange("p a n -> p (a n)")
                            nc.vector.tensor_tensor(row, row, pM[:, s % 2, 0:D], ALU.add).then_inc(left, 1)


def moe(nc, sem, inp, res, weight, gather_at, moe_in, moe_out, ident, out):
    HC = CT * P // 2
    with ExitStack() as c:
        def sb(name, shape, dt=F32):
            return c.enter_context(nc.sbuf_tensor("me_" + name, shape, dt))
        w1 = [sb(f"w1_{s}", [P, DC, FF]) for s in range(2)]
        w2 = [sb(f"w2_{s}", [P, FC, D]) for s in range(2)]
        xe = [sb(f"xe_{s}", [P, CT, D]) for s in range(2)]
        b1 = sb("b1", [P, EXPERTS, FC])
        b1e = sb("b1e", [P, FC])
        b2 = sb("b2", [P, EXPERTS, D])
        xT = sb("xT", [P, DC, CT * P])
        h = sb("h", [P, FC, CT * P])
        eo = [sb(f"eo_{s}", [P, CT, D]) for s in range(2)]
        y = sb("y", [P, SUB, 2, D])
        pX = c.enter_context(nc.psum_tensor("me_pX", [P, 2, BLK], F32))
        pH = c.enter_context(nc.psum_tensor("me_pH", [P, 4, BLK], F32))
        pO = c.enter_context(nc.psum_tensor("me_pO", [P, 2, BLK], F32))
        stored, b_ok, b1_ok, relay = sem("me_rows_stored"), sem("me_b_ok"), sem("me_b1_ok"), sem("me_relay")
        e_in = [sem(f"me_e_in{s}") for s in range(2)]
        e_out = [sem(f"me_e_out{s}") for s in range(2)]
        x_turn, x_left, h_made, h_left, o_made, o_left = (
            sem("me_" + n) for n in ("x_turn", "x_left", "h_made", "h_left", "o_made", "o_left"))
        with nc.Block() as block:
            @block.sync
            def _(sp):
                sp.nop().then_inc(o_made, 1)
                sp.dma_start(b1[:], inp["b1"]).then_inc(b_ok, 16)
                sp.dma_start(b2[:].rearrange("p e d -> p (e d)"), inp["b2"].broadcast_to((P, EXPERTS * D))).then_inc(b_ok, 16)
                with sp.Fori(0, EXPERTS // 2) as pair:
                    for s in range(2):
                        e = pair * 2 + s
                        sp.wait_ge(o_made, pair * 2 * CT + 1)
                        sp.dma_start(xe[s][:], moe_in[bass.ds(e * CAP, CAP), :].rearrange("(t p) d -> p t d", p=P)).then_inc(e_in[s], 16)
                        sp.dma_start(w1[s][:], inp["w1"][:, bass.ds(e, 1), :, :].rearrange("p a c f -> p (a c) f")).then_inc(e_in[s], 16)
                        sp.dma_start(w2[s][:], inp["w2"][:, bass.ds(e, 1), :, :].rearrange("p a c f -> p (a c) f")).then_inc(e_in[s], 16)

            @block.tensor
            def _(pe):
                with pe.Fori(0, EXPERTS // 2) as pair:
                    for s in range(2):
                        e = pair * 2 + s
                        pe.wait_ge(e_in[s], pair * 48 + 48)
                        for t in range(CT):
                            pe.wait_ge(x_left, e * CT + t + 1)
                            for d in range(DC):
                                last = nc.tensor.transpose(pX[:, t % 2, d * P:(d + 1) * P], xe[s][:, t, d * P:(d + 1) * P], ident[:])
                            last.then_inc(x_turn, 1)
                        pe.wait_ge(x_left, e * CT + CT + 2)
                        for f in range(FC):
                            for k in range(2):
                                n = f * 2 + k
                                pe.wait_ge(h_left, e * FC * 2 + n + 1)
                                for d in range(DC):
                                    last = nc.tensor.matmul(pH[:, n % 4, 0:HC], w1[s][:, d, f * P:(f + 1) * P],
                                                            xT[:, d, k * HC:(k + 1) * HC], start=d == 0, stop=d == DC - 1)
                                last.then_inc(h_made, 1)
                        pe.wait_ge(h_left, (e + 1) * FC * 2 + 4)
                        for t in range(CT):
                            pe.wait_ge(o_left, e * CT + t + 1)
                            for f in range(FC):
                                last = nc.tensor.matmul(pO[:, t % 2, 0:D], h[:, f, t * P:(t + 1) * P], w2[s][:, f, :],
                                                        start=f == 0, stop=f == FC - 1)
                            last.then_inc(o_made, 1)

            @block.scalar
            def _(act):
                act.nop().then_inc(h_left, 4)
                act.wait_ge(b_ok, 32)
                with act.Fori(0, EXPERTS) as e:
                    act.wait_ge(o_made, e * CT + 1)
                    act.wait_ge(h_left, e * FC * 2 + 4)
                    act.nop().then_inc(relay, 1)
                    nc.scalar.activation(b1e[:], b1[:, bass.ds(e, 1), :].rearrange("p a b -> p (a b)"), ACT.Copy).then_inc(b1_ok, 1)
                    act.wait_ge(b1_ok, e + 1)
                    for n in range(FC * 2):
                        act.wait_ge(h_made, e * FC * 2 + n + 2)
                        nc.scalar.activation(h[:, n // 2, (n % 2) * HC:(n % 2 + 1) * HC], pH[:, n % 4, 0:HC], ACT.Relu,
                                             bias=b1e[:, n // 2:n // 2 + 1]).then_inc(h_left, 1)

            @block.vector
            def _(dve):
                dve.nop().then_inc(h_made, 1)
                dve.nop().then_inc(stored, 2)
                dve.nop().then_inc(x_left, 2)
                dve.nop().then_inc(o_left, 2)
                dve.wait_ge(b_ok, 32)
                with dve.Fori(0, EXPERTS // 2) as pair:
                    for s in range(2):
                        e = pair * 2 + s
                        dve.wait_ge(h_made, e * FC * 2 + 1)
                        for t in range(CT):
                            dve.wait_ge(x_turn, e * CT + t + 1)
                            nc.vector.tensor_copy(xT[:, :, t * P:(t + 1) * P],
                                                  pX[:, t % 2, 0:D].rearrange("p (c n) -> p c n", c=DC)).then_inc(x_left, 1)
                        dve.wait_ge(stored, e + 1)
                        for t in range(CT):
                            dve.wait_ge(o_made, e * CT + t + 2)
                            nc.vector.tensor_tensor(eo[s][:, t, :], pO[:, t % 2, 0:D],
                                                    b2[:, bass.ds(e, 1), :].rearrange("p a d -> p (a d)"), ALU.add).then_inc(o_left, 1)

            @block.gpsimd
            def _(pool):
                with pool.Fori(0, EXPERTS // 2) as pair:
                    for s in range(2):
                        e = pair * 2 + s
                        pool.wait_ge(o_left, (e + 1) * CT + 2)
                        pool.dma_start(moe_out[bass.ds(e * CAP, CAP), :].rearrange("(t p) d -> p t d", p=P), eo[s][:]).then_inc(e_out[s], 16)
                        pool.wait_ge(e_out[s], (pair + 1) * 16)
                        pool.nop().then_inc(stored, 1)

        got = [sem(f"me_got{j}") for j in range(BLOCKS)]
        done, stored = sem("me_done"), sem("me_stored")
        rows_out = out.rearrange("b (t p) d -> p (b t) d", p=P)
        y2 = [y[:, :, s, :] for s in range(2)]
        with nc.Block() as block:
            @block.gpsimd
            def _(pool):
                for j in range(BLOCKS):
                    if j >= 2:
                        pool.wait_ge(done, (j - 1) * SUB)
                    for t in range(SUB):
                        at = j * SUB + t
                        pool.indirect_dma_start(y2[j % 2][:, t, :], None, moe_out,
                                                bass.IndirectOffsetOnAxis(ap=gather_at[:, at:at + 1], axis=0)).then_inc(got[j], 16)

            @block.vector
            def _(dve):
                for j in range(BLOCKS):
                    dve.wait_ge(got[j], 16 * SUB)
                    for t in range(SUB):
                        at = j * SUB + t
                        nc.vector.scalar_tensor_tensor(res[:, at, :], y2[j % 2][:, t, :], weight[:, at:at + 1], res[:, at, :],
                                                       ALU.mult, ALU.add).then_inc(done, 1)

            @block.sync
            def _(sp):
                for j in range(BLOCKS):
                    sp.wait_ge(done, (j + 1) * SUB)
                    sp.dma_start(rows_out[:, j * SUB:(j + 1) * SUB, :], res[:, j * SUB:(j + 1) * SUB, :]).then_inc(stored, 16)
                sp.wait_ge(stored, 16 * BLOCKS)


def rows_on_partitions(w, chunks):
    return w.reshape(chunks, P, -1).transpose(1, 0, 2)


def arrays_for(i):
    a = {"x": i["L0_attn_x"]}
    ar = np.arange(P)
    a["c_ident"] = np.eye(P, dtype=np.float32)
    a["gb"] = np.stack([i["L0_attn_ln_gamma"].reshape(DC, P).T, i["L0_attn_ln_beta"].reshape(DC, P).T], 1)
    w_in = i["L0_attn_W_in"]
    a["W_inT"] = rows_on_partitions(w_in.T, DC)
    a["W_inE"] = rows_on_partitions(w_in[:INNER], IC)
    a["W_outT"] = rows_on_partitions(i["L0_attn_W_out"].T, IC)
    a["A"], a["A_T"] = i["L0_attn_A"], i["L0_attn_A"].T
    a["BmT"] = rows_on_partitions(i["L0_attn_Bm"].T, IC)
    a["Cm"] = i["L0_attn_Cm"]
    a["c_own"] = (ar[:, None] // STATE == np.arange(GROUPS)[None]).astype(np.float32)
    a["conv"] = rows_on_partitions(np.concatenate([i["L0_attn_conv_w"][:, 0], i["L0_attn_conv_b"][:, None]], 1), IC)
    a["Wq0"] = rows_on_partitions(i["L0_ffn_Wq"], DC)
    chan = np.stack([np.tile(i["L0_ffn_" + n], 2) for n in ("bn_gamma", "bn_beta")], 1)
    a["pk_vec"] = np.concatenate([i["L0_ffn_bq"].reshape(QCH, P).T, chan], 1)
    a["key0T"], a["key1T"] = i["L0_ffn_sub_key0"].T, i["L0_ffn_sub_key1"].T
    a["downT"] = rows_on_partitions(i["L0_ffn_expert_down"].T, DC)
    a["up"] = rows_on_partitions(i["L0_ffn_expert_up"], DC)
    a["c_heads"] = (ar[:, None] % QD == ar[None] % QD).astype(np.float32) / PK_HEADS
    a["c_halves"] = (ar[:, None] // HALF == np.arange(P // HALF)[None]).astype(np.float32)
    even_odd = np.concatenate([np.arange(0, D, 2), np.arange(1, D, 2)])
    for n in "qk":
        a["W" + n] = rows_on_partitions(i["L1_attn_W" + n][:, even_odd], DC)
        a["b" + n] = i["L1_attn_b" + n][even_odd].reshape(2, P).T
    a["Wv"], a["Wo"] = (rows_on_partitions(i["L1_attn_W" + n], DC) for n in "vo")
    a["bv"], a["bo"] = i["L1_attn_bv"][None], i["L1_attn_bo"][None]
    freq = np.power(10000.0, -2.0 * np.arange(P) / D).astype(np.float32)
    angle = (freq[:, None] * np.arange(SEQ, dtype=np.float32)[None]).astype(np.float64)
    a["c_cos"], a["c_sin"] = np.cos(angle).astype(np.float32), np.sin(angle).astype(np.float32)
    later = np.where(ar[None] > ar[:, None], -1e30, 0.0).astype(np.float32)
    a["c_masks"] = np.stack([later, later.T], 1)
    a["gate"] = rows_on_partitions(i["L1_ffn_gate_w"].T, DC)
    a["gate_b"] = i["L1_ffn_gate_b"][None]
    a["w1"] = i["L1_ffn_w1"].reshape(EXPERTS, DC, P, FF).transpose(2, 0, 1, 3)
    a["b1"] = i["L1_ffn_b1"].reshape(EXPERTS, FC, P).transpose(2, 0, 1)
    a["w2"] = i["L1_ffn_w2"].reshape(EXPERTS, FC, P, D).transpose(2, 0, 1, 3)
    a["b2"] = i["L1_ffn_b2"].reshape(1, EXPERTS * D)
    a["c_before"] = (ar[:, None] <= ar[None]).astype(np.float32)
    a["c_ones"] = np.ones((P, P), np.float32)
    a["c_trash"] = (SLOTS + ar[:, None] + P * np.arange(TILES)[None]).astype(np.float32)
    a["c_expert"] = np.tile(np.arange(EXPERTS, dtype=np.float32), (P, 1))
    return {n: np.ascontiguousarray(x) for n, x in a.items()}


def kernel(**inputs):
    import concourse.bacc as bacc
    from concourse.bass_utils import run_bass_kernel_spmd

    nc = bacc.Bacc("TRN2", target_bir_lowering=False, num_devices=1)
    arrays, aps = {}, {}
    for name, a in arrays_for({n: np.asarray(v) for n, v in inputs.items()}).items():
        arrays["in_" + name] = a
        aps[name] = nc.dram_tensor("in_" + name, a.shape, mybir.dt.from_np(a.dtype), kind="ExternalInput").ap()
    out = nc.dram_tensor("out_0", (BATCH, SEQ, D), F32, kind="ExternalOutput").ap()
    program(nc, aps, out)
    return run_bass_kernel_spmd(nc, [arrays], core_ids=[0]).results[0]["out_0"]
```

```python
from contextlib import ExitStack

import numpy as np

import concourse.bass as bass
from concourse import mybir

F32 = mybir.dt.float32
BF16 = mybir.dt.bfloat16
I32 = mybir.dt.int32
U32 = mybir.dt.uint32
ALU = mybir.AluOpType
ACT = mybir.ActivationFunctionType
AX_X = mybir.AxisListType.X

P = 128
BATCH, SEQ, D = 2, 2048, 256
TOK = BATCH * SEQ
TILES = TOK // P
BLK = 512
BLOCKS = TOK // BLK
SUB = BLK // P
DC = D // P
EPS = 1e-5

INNER, STATE, TAPS = 512, 16, 4
IC = INNER // P
GROUPS = P // STATE

PK_HEADS, QD, NKEY, TOPK_DIM = 8, 64, 32, 4
HALF = QD // 2
SETS = 2 * PK_HEADS
PK_EXP = 256
ROWS_IN = PK_EXP // NKEY
QCH = PK_HEADS * QD // P

HEADS, HD = 16, 16
HPG = 4
HG = HEADS // HPG
QT = SEQ // BLK
KT = SEQ // P
PADV = 32
TERMS = 6
MROW = TERMS * HD

EXPERTS, FF, CAP = 8, 1024, 640
CT = CAP // P
FC = FF // P
SLOTS = EXPERTS * CAP

PARTS_Q = (0, 0, 1, 1, 0, 2)
PARTS_K = (0, 1, 0, 1, 2, 0)


def program(nc, inp, out):
    ctx = ExitStack()
    with ctx:
        def sem(name):
            return ctx.enter_context(nc.semaphore(name))

        def keep(name, shape, dt=F32):
            return ctx.enter_context(nc.sbuf_tensor(name, shape, dt))

        res = keep("res", [P, TILES, D])
        ident = keep("ident", [P, P])
        identb = keep("identb", [P, P], BF16)
        rowsT = nc.dram_tensor("split_rows", (2, 3, BATCH * D, SEQ), BF16, kind="Internal").ap()
        v_pad = nc.dram_tensor("v_padded", (BATCH * HG, P, KT, HPG * PADV), F32, kind="Internal").ap()
        moe_in = nc.dram_tensor("moe_in", (SLOTS + TOK, D), F32, kind="Internal").ap()
        moe_out = nc.dram_tensor("moe_out", (SLOTS, D), F32, kind="Internal").ap()

        weight = keep("weight", [P, TILES])
        gather_at = keep("gather_at", [P, TILES], I32)
        ahead = ctx.enter_context(ExitStack())
        early = ctx.enter_context(ExitStack())
        weights = Weights(nc, sem, early, inp)
        keys = KeyStats(nc, sem, early)
        with ExitStack() as c0:
            normT = c0.enter_context(nc.sbuf_tensor("normT", [P, DC, TOK], F32))
            with ExitStack() as c1:
                ssmT = c1.enter_context(nc.sbuf_tensor("ssmT", [P, DC, TOK], F32))
                norm_first(nc, sem, inp, res, normT, ssmT, ident, identb, weights)
                ssm(nc, sem, res, normT, ssmT, weights, keys, moe_in)
            product_keys(nc, sem, res, normT, ident, weights, keys)
        early.close()
        with ExitStack() as c2:
            rows = c2.enter_context(nc.sbuf_tensor("rows", [P, TILES, D], F32))
            logits = c2.enter_context(nc.sbuf_tensor("logits", [P, TILES, EXPERTS], F32))
            norm_project(nc, sem, inp, res, rows, ident, rowsT, v_pad, logits)
            operands = Operands(nc, sem, ahead, rowsT, v_pad)
            route(nc, sem, inp, rows, logits, weight, gather_at, moe_in, operands)
        with ExitStack() as c3:
            ctxt = c3.enter_context(nc.sbuf_tensor("ctxt", [P, BATCH * HG, KT, HPG * HD], F32))
            wo = c3.enter_context(nc.sbuf_tensor("wo", [P, DC, D], F32))
            attention(nc, sem, inp, res, operands, ctxt, wo, ident, identb)
            ahead.close()
            experts = Experts(nc, sem, inp, ahead, moe_in)
            attention_out(nc, sem, res, ctxt, wo, ident, experts)
        moe(nc, sem, inp, res, weight, gather_at, moe_out, ident, out, experts)


class Steps:

    def __init__(self, sem, per_round, i=0):
        self.sem, self.per, self.i, self.n = sem, per_round, i, 0

    def inc(self, instruction):
        instruction.then_inc(self.sem, 1)
        self.n += 1
        assert self.n <= self.per
        return self.n

    def at(self, n):
        return self.i * self.per + n


class Weights:

    def __init__(self, nc, sem, stack, inp):
        def sb(name, shape):
            return stack.enter_context(nc.sbuf_tensor("w_" + name, shape, F32, side="right"))
        self.inp = inp
        self.w_in = sb("w_in", [P, DC, 2 * INNER])
        self.w_ine = sb("w_ine", [P, IC, D])
        self.w_out = sb("w_out", [P, IC, D])
        self.bmT = sb("bmT", [P, IC, STATE])
        self.cm = sb("cm", [P, INNER])
        self.own = sb("own", [P, GROUPS])
        self.inner = sb("inner", [P, BLOCKS + 1])
        self.cw = sb("cw", [P, IC, TAPS + 1])
        self.pw = sb("pw", [P, 2, 2, P + STATE])
        self.wq = sb("wq", [P, DC, PK_HEADS * QD])
        self.vec = sb("vec", [P, QCH + 2])
        self.keys = sb("keys", [P, P])
        self.ones = sb("ones", [P, P])
        self.heads = sb("heads", [P, P])
        self.halves = sb("halves", [P, P // HALF])
        self.down = sb("down", [P, DC, PK_EXP])
        self.upw = sb("upw", [P, DC, PK_EXP])
        self.ok, self.zero = sem("w_ok"), sem("w_zero")

    def clear(self, engine):
        engine.memset(self.pw[:], 0.0).then_inc(self.zero, 1)
        engine.memset(self.keys[:], 0.0).then_inc(self.zero, 1)

    def load(self, sp):
        inp = self.inp
        moves = []
        for g in range(GROUPS):
            at = slice(g * STATE, (g + 1) * STATE)
            moves.append((self.cm[at, :], inp["Cm"]))
            for q in range(2):
                moves.append((self.pw[at, 0, q, STATE + g * STATE:STATE + (g + 1) * STATE], inp["A_T"] if q == 0 else inp["A"]))
        for k in range(P // HALF):
            at = slice(k * HALF, (k + 1) * HALF)
            moves.append((self.keys[at, at], inp[f"key{k % 2}T"]))
        for t, name in ((self.w_in, "W_inT"), (self.w_ine, "W_inE"), (self.w_out, "W_outT"), (self.bmT, "BmT"),
                        (self.cw, "conv"), (self.own, "c_own"), (self.inner, "c_inner"), (self.wq, "Wq0"), (self.vec, "pk_vec"), (self.ones, "c_ones"),
                        (self.heads, "c_heads"), (self.halves, "c_halves"), (self.down, "downT"), (self.upw, "up")):
            moves.append((t[:], inp[name]))
        sp.wait_ge(self.zero, 2)
        for dst, src in moves:
            sp.dma_start(dst, src).then_inc(self.ok, 16)
        self.all = 16 * len(moves)


def norm_first(nc, sem, inp, res, normT, ssmT, ident, identb, weights):
    x = inp["x"].rearrange("b (t p) d -> p (b t) d", p=P)
    with ExitStack() as c:
        def sb(name, shape, dt=F32):
            return c.enter_context(nc.sbuf_tensor("n1_" + name, shape, dt))
        xn = sb("xn", [P, 2, SUB, D])
        x2 = sb("x2", [P, 2, SUB, D])
        stats = sb("stats", [P, SUB, 6])
        mv = sb("mv", [P, 2, SUB, 2])
        inv = sb("inv", [P, SUB])
        std = sb("std", [P, 2, 2, SUB])
        rstd = sb("rstd", [P, 2, 2, SUB])
        gb = sb("gb", [P, 2, DC])
        ps = c.enter_context(nc.psum_tensor("n1_ps", [P, 2, 2 * DC, BLK], F32))
        const_in = sem("n1_const_in")
        x_in = [sem(f"n1_x_in{h}") for h in range(2)]
        (step, std_ok, inv_ok, xn_ok, x2_ok, res_ok, turned1, turned2, out1, out2, relay) = (sem("n1_" + n) for n in (
            "step", "std_ok", "inv_ok", "xn_ok", "x2_ok", "res_ok", "turned1", "turned2", "out1", "out2", "relay"))
        PER = 2 * SUB + 4
        with nc.Block() as block:
            @block.sync
            def _(sp):
                for h in range(2):
                    sp.dma_start(res[:, h * SUB:(h + 1) * SUB, :], x[:, h * SUB:(h + 1) * SUB, :]).then_inc(x_in[h], 16)
                for t, src in ((ident, inp["c_ident"]), (gb, inp["gb"])):
                    sp.dma_start(t[:], src).then_inc(const_in, 16)
                with sp.Fori(1, BLOCKS // 2) as jj:
                    for h in range(2):
                        sp.wait_ge(x_in[h], jj * 16)
                        at = bass.ds((jj * 2 + h) * SUB, SUB)
                        sp.dma_start(res[:, at, :], x[:, at, :]).then_inc(x_in[h], 16)
                weights.load(sp)

            @block.gpsimd
            def _(pool):
                weights.clear(nc.gpsimd)
                with pool.Fori(0, BLOCKS // 2) as jj:
                    for h in range(2):
                        j = jj * 2 + h
                        pool.wait_ge(xn_ok, j * SUB + SUB)
                        at = bass.ds(j * SUB, SUB)
                        nc.gpsimd.tensor_tensor(res[:, at, :], res[:, at, :], xn[:, h], ALU.add).then_inc(res_ok, 1)

            @block.vector
            def _(dve):
                dve.nop().then_inc(turned1, 2)
                dve.nop().then_inc(turned2, 2)
                dve.nop().then_inc(res_ok, 2)
                dve.nop().then_inc(x2_ok, 1)

                def statistics(j, h, jj):
                    st = Steps(step, PER, j)

                    def then(ins):
                        dve.wait_ge(step, st.at(st.inc(ins)))

                    dve.wait_ge(x_in[h], jj * 16 + 16)
                    if not isinstance(j, int) or j > 0:
                        dve.wait_ge(x2_ok, (j - 1) * SUB + 1)
                    for s in range(SUB):
                        st.inc(nc.vector.bn_stats(stats[:, s, :], res[:, bass.ds(j * SUB + s, 1), :].rearrange("p a n -> p (a n)")))
                    dve.wait_ge(step, st.at(st.n))
                    dve.nop().then_inc(relay, 1)
                    for s in range(SUB):
                        st.inc(nc.vector.bn_aggr(mv[:, h, s, :], stats[:, s, :]))
                    dve.wait_ge(step, st.at(st.n))
                    then(nc.vector.tensor_scalar(std[:, h, 0, :], mv[:, h, :, 1], EPS, None, ALU.add))
                    then(nc.vector.reciprocal(inv[:], std[:, h, 0, :]))
                    then(nc.vector.tensor_tensor(std[:, h, 1, :], mv[:, h, :, 1], inv[:], ALU.mult))
                    st.inc(nc.vector.tensor_scalar(std[:, h, 1, :], std[:, h, 1, :], EPS, None, ALU.add))
                    assert st.n == PER

                def normalise(j, h):
                    dve.wait_ge(std_ok, j + 1)
                    nc.vector.reciprocal(rstd[:, h], std[:, h]).then_inc(inv_ok, 1)
                    dve.wait_ge(turned1, j + 1)
                    dve.wait_ge(res_ok, j + 1)
                    dve.wait_ge(inv_ok, j + 1)
                    for s in range(SUB):
                        row = res[:, bass.ds(j * SUB + s, 1), :].rearrange("p a n -> p (a n)")
                        nc.vector.tensor_scalar(xn[:, h, s, :], row, mv[:, h, s, 0:1], rstd[:, h, 0, s:s + 1],
                                                ALU.subtract, ALU.mult).then_inc(xn_ok, 1)
                    dve.wait_ge(turned2, j + 1)
                    for s in range(SUB):
                        dve.wait_ge(xn_ok, j * SUB + s + 1)
                        nc.vector.tensor_scalar(x2[:, h, s, :], xn[:, h, s, :], rstd[:, h, 1, s:s + 1], None,
                                                ALU.mult).then_inc(x2_ok, 1)

                def two_blocks(jj, final):
                    for h in range(2):
                        j = jj * 2 + h
                        if not (final and h):
                            statistics(j + 1, 1 - h, jj + h)
                        normalise(j, h)

                statistics(0, 0, 0)
                with dve.Fori(0, BLOCKS // 2 - 1) as jj:
                    two_blocks(jj, False)
                two_blocks(BLOCKS // 2 - 1, True)

            @block.tensor
            def _(pe):
                pe.wait_ge(const_in, 32)
                pe.nop().then_inc(out1, 2)
                pe.nop().then_inc(out2, 3)
                with pe.Fori(0, BLOCKS // 2) as jj:
                    for h in range(2):
                        j = jj * 2 + h
                        pe.wait_ge(xn_ok, j * SUB + SUB)
                        pe.wait_ge(out1, j + 1)
                        for d in range(DC):
                            for s in range(SUB):
                                last = nc.tensor.transpose(ps[:, h, d, s * P:(s + 1) * P], xn[:, h, s, d * P:(d + 1) * P], ident[:])
                        last.then_inc(turned1, 1)
                        pe.wait_ge(x2_ok, j * SUB + SUB + 1)
                        pe.wait_ge(out2, j * DC + 1)
                        for d in range(DC):
                            for s in range(SUB):
                                last = nc.tensor.transpose(ps[:, h, DC + d, s * P:(s + 1) * P], x2[:, h, s, d * P:(d + 1) * P], ident[:])
                        last.then_inc(turned2, 1)

            @block.scalar
            def _(act):
                act.wait_ge(const_in, 32)
                nc.scalar.activation(identb[:], ident[:], ACT.Copy)

                def root(j, h):
                    act.wait_ge(step, j * PER + PER)
                    nc.scalar.activation(std[:, h], std[:, h], ACT.Sqrt).then_inc(std_ok, 1)

                def two_blocks(jj, final):
                    for h in range(2):
                        j = jj * 2 + h
                        if not (final and h):
                            root(j + 1, 1 - h)
                        act.wait_ge(turned1, j + 3)
                        nc.scalar.activation(normT[:, :, bass.ds(j * BLK, BLK)], ps[:, h, 0:DC], ACT.Copy).then_inc(out1, 1)
                        act.wait_ge(turned2, j + 3)
                        for d in range(DC):
                            nc.scalar.activation(ssmT[:, d, bass.ds(j * BLK, BLK)], ps[:, h, DC + d, :], ACT.Identity,
                                                 scale=gb[:, 0, d:d + 1], bias=gb[:, 1, d:d + 1]).then_inc(out2, 1)

                root(0, 0)
                with act.Fori(0, BLOCKS // 2 - 1) as jj:
                    two_blocks(jj, False)
                two_blocks(BLOCKS // 2 - 1, True)


class KeyStats:

    def __init__(self, nc, sem, stack):
        def sb(name, shape):
            return stack.enter_context(nc.sbuf_tensor("ks_" + name, shape, F32, side="right"))
        self.nc = nc
        self.keysq = sb("keysq", [P, P])
        self.knorm = sb("knorm", [P, P])
        self.stats = sb("stats", [P, QCH, BLOCKS, 6])
        self.mv = sb("mv", [P, QCH, 2])
        self.sq = sb("sq", [P, QCH])
        self.mom = sb("mom", [P, 4])
        self.gain = sb("gain", [P, 1])
        self.shift = sb("shift", [P, QCH + 1])
        self.made, self.stat, self.kn1, self.kn2, self.prods, self.moment, self.vstep, self.vstd = (
            sem("ks_" + n) for n in ("made", "stat", "kn1", "kn2", "prods", "moment", "vstep", "vstd"))

    def moments_pe(self, pe, weights, bank):
        nc = self.nc
        pe.wait_ge(self.kn1, 1)
        nc.tensor.matmul(bank[:, 0:P], weights.ones[:], self.keysq[:], start=True, stop=True).then_inc(self.prods, 1)
        pe.wait_ge(self.moment, 4)
        pe.wait_ge(self.kn2, 1)
        for m in range(QCH):
            last = nc.tensor.matmul(bank[:, P:P + 2], weights.heads[:], self.mv[:, m, :], start=m == 0, stop=m == QCH - 1)
        last.then_inc(self.prods, 1)

    def act(self, act, weights, bank):
        nc = self.nc
        act.wait_ge(weights.ok, weights.all)
        nc.scalar.activation(self.keysq[:], weights.keys[:], ACT.Square).then_inc(self.kn1, 1)
        act.wait_ge(self.prods, 1)
        nc.scalar.activation(self.knorm[:], bank[:, 0:P], ACT.Sqrt).then_inc(self.kn2, 1)
        act.wait_ge(self.vstep, 6)
        nc.scalar.activation(self.mom[:, 3:4], self.mom[:, 2:3], ACT.Sqrt).then_inc(self.vstd, 1)

    def dve(self, dve, weights, bank):
        nc, knorm, keys, stats, mv, sq, mom = self.nc, self.knorm, weights.keys, self.stats, self.mv, self.sq, self.mom
        vec, moment, vstep = weights.vec, self.moment, self.vstep
        dve.wait_ge(self.stat, BLOCKS * QCH)
        for m in range(QCH):
            nc.vector.bn_aggr(mv[:, m, :], stats[:, m, :, :].rearrange("p a n -> p (a n)")).then_inc(self.stat, 1)
        dve.wait_ge(self.stat, BLOCKS * QCH + QCH)
        nc.vector.tensor_tensor(mv[:, :, 0], mv[:, :, 0], vec[:, 0:QCH], ALU.add).then_inc(moment, 1)
        dve.wait_ge(moment, 1)
        nc.vector.tensor_tensor(sq[:], mv[:, :, 0], mv[:, :, 0], ALU.mult).then_inc(moment, 1)
        dve.wait_ge(moment, 2)
        nc.vector.tensor_tensor(mv[:, :, 1], mv[:, :, 1], sq[:], ALU.add).then_inc(moment, 1)
        dve.wait_ge(moment, 3)
        dve.nop().then_inc(moment, 1)
        dve.wait_ge(self.kn2, 1)
        nc.vector.tensor_scalar(knorm[:], knorm[:], 1e-12, None, ALU.max).then_inc(vstep, 1)
        dve.wait_ge(vstep, 1)
        nc.vector.reciprocal(knorm[:], knorm[:]).then_inc(vstep, 1)
        dve.wait_ge(vstep, 2)
        nc.vector.tensor_tensor(keys[:], keys[:], knorm[:], ALU.mult).then_inc(vstep, 1)
        dve.wait_ge(self.prods, 2)
        nc.vector.tensor_copy(mom[:, 0:2], bank[:, P:P + 2]).then_inc(vstep, 1)
        dve.wait_ge(vstep, 4)
        nc.vector.scalar_tensor_tensor(mom[:, 2:3], mom[:, 0:1], mom[:, 0:1], mom[:, 1:2], ALU.mult,
                                       ALU.subtract).then_inc(vstep, 1)
        dve.wait_ge(vstep, 5)
        nc.vector.tensor_scalar(mom[:, 2:3], mom[:, 2:3], -1.0, EPS, ALU.mult, ALU.add).then_inc(vstep, 1)
        dve.wait_ge(self.vstd, 1)
        nc.vector.reciprocal(mom[:, 3:4], mom[:, 3:4]).then_inc(vstep, 1)
        dve.wait_ge(vstep, 7)
        nc.vector.tensor_tensor(self.gain[:], mom[:, 3:4], vec[:, QCH:QCH + 1], ALU.mult).then_inc(vstep, 1)
        dve.wait_ge(vstep, 8)
        nc.vector.tensor_tensor(mom[:, 1:2], mom[:, 0:1], self.gain[:], ALU.mult).then_inc(vstep, 1)
        dve.wait_ge(vstep, 9)
        nc.vector.tensor_tensor(self.shift[:, QCH:], vec[:, QCH + 1:QCH + 2], mom[:, 1:2], ALU.subtract).then_inc(vstep, 1)
        dve.wait_ge(vstep, 10)
        nc.vector.tensor_scalar(self.shift[:, 0:QCH], vec[:, 0:QCH], self.gain[:], self.shift[:, QCH:],
                                ALU.mult, ALU.add).then_inc(vstep, 1)


def ssm(nc, sem, res, normT, ssmT, weights, keys, moe_in):
    w_in, w_ine, w_out, bmT = weights.w_in, weights.w_ine, weights.w_out, weights.bmT
    cm, own, cw, pw, inner = weights.cm, weights.own, weights.cw, weights.pw, weights.inner
    with ExitStack() as c:
        def sb(name, shape, dt=F32):
            return c.enter_context(nc.sbuf_tensor("ss_" + name, shape, dt))
        stj = sb("stj", [P, BLK])
        vw = sb("vw", [P, DC, 2 * P])
        zeros = sb("zeros", [P, 2 * D])
        sh = sb("sh", [P, 2, P])
        st = sb("st", [P, BLK])
        halo = TAPS - 1
        u = sb("u", [P, IC, halo + BLK])
        sz = sb("sz", [P, IC, BLK])
        cv = sb("cv", [P, IC, BLK])
        sg = sb("sg", [P, IC, BLK])
        y = sb("y", [P, IC, BLK])
        pU = c.enter_context(nc.psum_tensor("ss_pU", [P, 2, BLK], F32))
        pZ = c.enter_context(nc.psum_tensor("ss_pZ", [P, 2, BLK], F32))
        pB = c.enter_context(nc.psum_tensor("ss_pB", [P, 2, BLK], F32))
        pC = c.enter_context(nc.psum_tensor("ss_pC", [P, 2, BLK], F32))
        vw_zero, zero_ok, zeroed = sem("ss_vw_zero"), sem("ss_zero_ok"), sem("ss_zeroed")
        fold, folded, scanp, scanv = sem("ss_fold"), sem("ss_folded"), sem("ss_scanp"), sem("ss_scanv")
        powp, powv, shv, sh_zero = sem("ss_powp"), sem("ss_powv"), sem("ss_shv"), sem("ss_sh_zero")
        STEPS = (BLK - 1).bit_length()
        LEVELS = STEPS + (SEQ // BLK - 1).bit_length()
        CHUNKS = BLOCKS * QCH
        banks = [pU[:, 0, :], pU[:, 1, :], pZ[:, 0, :], pZ[:, 1, :]]

        def chunks_of(k):
            return range(k * CHUNKS // LEVELS, (k + 1) * CHUNKS // LEVELS)

        with nc.Block() as block:
            @block.sync
            def _(sp):
                sp.wait_ge(zero_ok, 1)
                n = SLOTS // (2 * P)
                for k in range(n):
                    sp.dma_start(moe_in[k * 2 * P:(k + 1) * 2 * P, :].rearrange("(p a) d -> p (a d)", p=P),
                                 zeros[:]).then_inc(zeroed, 16)
                sp.wait_ge(zeroed, 16 * n)

            @block.gpsimd
            def _(pool):
                nc.gpsimd.memset(vw[:], 0.0).then_inc(vw_zero, 1)
                nc.gpsimd.memset(zeros[:], 0.0).then_inc(zero_ok, 1)

            @block.tensor
            def _(pe):
                pe.wait_ge(weights.ok, weights.all)
                for d in range(DC):
                    for k in range(IC):
                        last = nc.tensor.matmul(pC[:, d, 0:STATE], w_ine[:, k, d * P:(d + 1) * P], bmT[:, k, :],
                                                start=k == 0, stop=k == IC - 1)
                last.then_inc(fold, 1)
                pe.wait_ge(folded, DC)
                for j in range(BLOCKS):
                    for d in range(DC):
                        last = nc.tensor.matmul(pB[:, 0, :], vw[:, d, P - STATE * j:2 * P - STATE * j],
                                                ssmT[:, d, j * BLK:(j + 1) * BLK],
                                                start=j == 0 and d == 0, stop=j == BLOCKS - 1 and d == DC - 1)
                last.then_inc(scanp, 1)
                for k in range(LEVELS):
                    cur = k % 2
                    pe.wait_ge(shv, k + 1)
                    pe.wait_ge(scanv, k + 1)
                    if k < STEPS:
                        n = 1 << k
                        nc.tensor.matmul(pB[:, 1, n:BLK], pw[:, cur, 0, STATE:], st[:, 0:BLK - n], start=True, stop=True)
                        last = nc.tensor.matmul(pB[:, 1, 0:n], sh[:, cur, :], st[:, BLK - n:BLK], start=True, stop=True)
                    else:
                        last = nc.tensor.matmul(pB[:, 1, :], sh[:, cur, :], st[:], start=True, stop=True)
                    last.then_inc(scanp, 1)
                    if k < LEVELS - 1:
                        nc.tensor.matmul(pC[:, 0, 0:P], pw[:, cur, 1, STATE:], pw[:, cur, 0, STATE:], start=True, stop=True)
                        nc.tensor.matmul(pC[:, 0, P:2 * P], pw[:, cur, 0, STATE:], pw[:, cur, 1, STATE:],
                                         start=True, stop=True).then_inc(powp, 1)
                    for x in chunks_of(k):
                        j, m = x // QCH, x % QCH
                        if x >= QCH:
                            pe.wait_ge(keys.stat, x - QCH + 1)
                        for d in range(DC):
                            last = nc.tensor.matmul(banks[m], weights.wq[:, d, m * P:(m + 1) * P], normT[:, d, j * BLK:(j + 1) * BLK],
                                                    start=d == 0, stop=d == DC - 1)
                        last.then_inc(keys.made, 1)
                keys.moments_pe(pe, weights, pC[:, 1, :])

            @block.scalar
            def _(act):
                keys.act(act, weights, pC[:, 1, :])

            @block.vector
            def _(dve):
                dve.wait_ge(fold, 1)
                dve.wait_ge(vw_zero, 1)
                for d in range(DC):
                    nc.vector.tensor_copy(vw[:, d, P:P + STATE], pC[:, d, 0:STATE]).then_inc(folded, 1)
                dve.wait_ge(scanp, 1)
                nc.vector.tensor_copy(st[:], pB[:, 0, :]).then_inc(scanv, 1)

                def statistics(k):
                    for x in chunks_of(k):
                        dve.wait_ge(keys.made, x + 1)
                        nc.vector.bn_stats(keys.stats[:, x % QCH, x // QCH, :], banks[x % QCH]).then_inc(keys.stat, 1)

                per = SEQ // BLK * STATE
                dve.wait_ge(weights.ok, weights.all)
                for k in range(LEVELS):
                    cur = k % 2
                    if k:
                        dve.wait_ge(powp, k)
                        dve.wait_ge(scanp, k + 1)
                        for q in range(2):
                            nc.vector.tensor_copy(pw[:, cur, q, STATE:], pC[:, 0, q * P:(q + 1) * P]).then_inc(powv, 1)
                        dve.wait_ge(powv, 2 * k)
                    far = max(0, k - STEPS)
                    w = STATE << far
                    nc.vector.memset(sh[:, cur, :], 0.0).then_inc(sh_zero, 1)
                    dve.wait_ge(sh_zero, 1 + k)
                    for b in range(BATCH):
                        last = nc.vector.tensor_copy(sh[:, cur, b * per + w:(b + 1) * per],
                                                     pw[:, cur, 0, STATE + b * per:STATE + (b + 1) * per - w])
                    last.then_inc(shv, 1)
                    if k:
                        statistics(k - 1)
                    dve.wait_ge(scanp, k + 2)
                    dve.wait_ge(scanv, k + 1)
                    nc.vector.tensor_tensor(st[:], st[:], pB[:, 1, :], ALU.add).then_inc(scanv, 1)
                statistics(LEVELS - 1)
                keys.dve(dve, weights, pC[:, 1, :])

        u_made, u_left, z_made, z_left = sem("mx_u_made"), sem("mx_u_left"), sem("mx_z_made"), sem("mx_z_left")
        c_made, c_left, o_made, o_left = sem("mx_c_made"), sem("mx_c_left"), sem("mx_o_made"), sem("mx_o_left")
        own_ok = sem("mx_own_ok")
        halo_ok, conv_ok, gate_ok, silu_ok, y_ok = (sem("mx_" + n) for n in ("halo_ok", "conv_ok", "gate_ok", "silu_ok", "y_ok"))
        with nc.Block() as block:
            @block.tensor
            def _(pe):
                def enter(j):
                    cols = bass.ds(j * BLK, BLK)
                    for m in range(IC):
                        pe.wait_ge(u_left, j * IC + m + 1)
                        for d in range(DC):
                            last = nc.tensor.matmul(pU[:, m % 2, :], w_in[:, d, m * P:(m + 1) * P], ssmT[:, d, cols],
                                                    start=d == 0, stop=d == DC - 1)
                        last.then_inc(u_made, 1)
                        pe.wait_ge(z_left, j * IC + m + 1)
                        for d in range(DC):
                            last = nc.tensor.matmul(pZ[:, m % 2, :], w_in[:, d, INNER + m * P:INNER + (m + 1) * P],
                                                    ssmT[:, d, cols], start=d == 0, stop=d == DC - 1)
                        last.then_inc(z_made, 1)

                def finish(j, more):
                    pe.wait_ge(own_ok, j + 1)
                    for m in range(IC):
                        pe.wait_ge(c_left, j * IC + m + 1)
                        nc.tensor.matmul(pB[:, m % 2, :], cm[:, m * P:(m + 1) * P], stj[:], start=True, stop=True).then_inc(c_made, 1)
                    if more:
                        enter(j + 1)
                    pe.wait_ge(y_ok, j * IC + 2 * IC)
                    for s in range(SUB):
                        pe.wait_ge(o_left, j * SUB + s + 1)
                        for k in range(IC):
                            last = nc.tensor.matmul(pC[:, s % 2, 0:D], y[:, k, s * P:(s + 1) * P], w_out[:, k, :],
                                                    start=k == 0, stop=k == IC - 1)
                        last.then_inc(o_made, 1)

                enter(0)
                with pe.Fori(0, BLOCKS - 1) as j:
                    finish(j, True)
                finish(BLOCKS - 1, False)

            @block.scalar
            def _(act):
                act.nop().then_inc(c_made, 1)
                act.nop().then_inc(y_ok, IC)
                act.nop().then_inc(u_left, 2)
                act.nop().then_inc(z_left, 2)

                def enter(j):
                    act.wait_ge(c_made, j * IC + 1)
                    nc.scalar.activation(stj[:], st[:], ACT.Copy, scale=own[:, bass.ds(j, 1)]).then_inc(own_ok, 1)
                    for m in range(IC):
                        act.wait_ge(u_made, j * IC + m + 1)
                        act.wait_ge(halo_ok, j * IC + m + 1)
                        nc.scalar.activation(u[:, m, halo:], pU[:, m % 2, :], ACT.Copy).then_inc(u_left, 1)
                        act.wait_ge(z_made, j * IC + m + 1)
                        act.wait_ge(y_ok, j * IC + m + 1)
                        nc.scalar.activation(sz[:, m, :], pZ[:, m % 2, :], ACT.Sigmoid).then_inc(z_left, 1)
                    for m in range(IC):
                        act.wait_ge(conv_ok, (j * IC + m) * TAPS + TAPS)
                        nc.scalar.activation(sg[:, m, :], cv[:, m, :], ACT.Sigmoid).then_inc(gate_ok, 1)

                with act.Fori(0, BLOCKS) as j:
                    enter(j)

            @block.vector
            def _(dve):
                dve.nop().then_inc(o_made, 1)
                dve.nop().then_inc(c_left, 2)
                dve.nop().then_inc(o_left, 2)

                def silu_conv(j, more):
                    for m in range(IC):
                        dve.wait_ge(u_left, j * IC + m + 3)
                        n = (j * IC + m) * TAPS
                        nc.vector.tensor_scalar(cv[:, m, :], u[:, m, halo:], cw[:, m, TAPS - 1:TAPS], cw[:, m, TAPS:],
                                                ALU.mult, ALU.add).then_inc(conv_ok, 1)
                        for k in range(TAPS - 1):
                            dve.wait_ge(conv_ok, n + k + 1)
                            nc.vector.scalar_tensor_tensor(cv[:, m, :], u[:, m, k:k + BLK], cw[:, m, k:k + 1], cv[:, m, :],
                                                           ALU.mult, ALU.add).then_inc(conv_ok, 1)
                        if more:
                            dve.wait_ge(conv_ok, n + TAPS)
                            nc.vector.tensor_scalar(u[:, m, 0:halo], u[:, m, BLK:], inner[:, bass.ds(j + 1, 1)], None,
                                                    ALU.mult).then_inc(halo_ok, 1)
                    for m in range(IC):
                        dve.wait_ge(gate_ok, j * IC + m + 1)
                        nc.vector.tensor_tensor(cv[:, m, :], cv[:, m, :], sg[:, m, :], ALU.mult).then_inc(silu_ok, 1)

                def finish(j, more):
                    for m in range(IC):
                        dve.wait_ge(silu_ok, j * IC + m + 1)
                        dve.wait_ge(c_made, j * IC + m + 2)
                        nc.vector.tensor_tensor(sg[:, m, :], cv[:, m, :], pB[:, m % 2, :], ALU.add).then_inc(c_left, 1)
                    dve.wait_ge(z_left, j * IC + IC + 2)
                    dve.wait_ge(o_made, j * SUB + 1)
                    for m in range(IC):
                        dve.wait_ge(c_left, j * IC + m + 3)
                        nc.vector.tensor_tensor(y[:, m, :], sg[:, m, :], sz[:, m, :], ALU.mult).then_inc(y_ok, 1)
                    if more:
                        silu_conv(j + 1, more)
                    for s in range(SUB):
                        dve.wait_ge(o_made, j * SUB + s + 2)
                        row = res[:, bass.ds(j * SUB + s, 1), :].rearrange("p a n -> p (a n)")
                        nc.vector.tensor_tensor(row, row, pC[:, s % 2, 0:D], ALU.add).then_inc(o_left, 1)

                for m in range(IC):
                    nc.vector.memset(u[:, m, 0:halo], 0.0).then_inc(halo_ok, 1)
                silu_conv(0, True)
                with dve.Fori(0, BLOCKS - 1) as j:
                    finish(j, True)
                finish(BLOCKS - 1, False)


def product_keys(nc, sem, res, normT, ident, weights, stats):
    SCORES = SETS * NKEY
    PAIRS = TILES // 2
    PIECES = QCH + DC
    with ExitStack() as c:
        def sb(name, shape, dt=F32):
            return c.enter_context(nc.sbuf_tensor("pk_" + name, shape, dt))
        qn = sb("qn", [P, 2, QCH, BLK])
        qs = sb("qs", [P, QCH, BLK])
        nrm = sb("nrm", [P, 2, SUB * SETS])
        inv = sb("inv", [P, 2, SUB * SETS])
        s_ = sb("s", [P, 2, 2, SCORES])
        ex = sb("ex", [P, 2, 2, SCORES])
        rep = sb("rep", [P, 2, SCORES])
        top = sb("top", [P, 2 * SETS, 8])
        z = sb("z", [P, 2 * SETS])
        far = sb("far", [P, 2, PK_HEADS])
        both = sb("both", [P, 2, PK_HEADS])
        share = sb("share", [P, 2, PK_HEADS])
        a0 = sb("a0", [P, 2, PK_HEADS, ROWS_IN])
        last_w = sb("last_w", [P, 2, 1])
        prod = sb("prod", [P, 2, PK_HEADS, PK_EXP])
        wt = sb("wt", [P, 2, PK_EXP])
        g = sb("g", [P, 2, DC, BLK])
        gw = sb("gw", [P, DC, 2 * P])
        pQ = c.enter_context(nc.psum_tensor("pk_pQ", [P, 2, BLK], F32))
        pN = c.enter_context(nc.psum_tensor("pk_pN", [P, BLK], F32))
        pS = c.enter_context(nc.psum_tensor("pk_pS", [P, 2, BLK], F32))
        pT = c.enter_context(nc.psum_tensor("pk_pT", [P, BLK], F32))
        pO = c.enter_context(nc.psum_tensor("pk_pO", [P, BLK], F32))
        turned = pT[:].rearrange("p (e t) -> p e t", e=DC)
        names = ("relay", "piece", "piece_out", "sq_ok", "n2_ok", "root_ok", "inv_ok", "sc_ok", "s_ok", "ex_ok", "search",
                 "a0_ok", "multiplied", "prod_ok", "summed", "wt_ok", "turn_ok", "gw_ok", "o_ok", "o_left")
        (relay, piece, piece_out, sq_ok, n2_ok, root_ok, inv_ok, sc_ok, s_ok, ex_ok, search,
         a0_ok, multiplied, prod_ok, summed, wt_ok, turn_ok, gw_ok, o_ok, o_left) = (sem("pk_" + n) for n in names)

        def rounds(engine, step):
            with engine.Fori(0, PAIRS // 4 - 1) as jj:
                for i in range(4):
                    step(jj * 4 + i, jj * 2, i, False)
            for i in range(4):
                step(PAIRS - 4 + i, BLOCKS - 2, i, True)

        with nc.Block() as block:
            @block.tensor
            def _(pe):
                pe.nop().then_inc(piece_out, 2)
                pe.nop().then_inc(root_ok, 1)
                pe.nop().then_inc(s_ok, 1)
                pe.nop().then_inc(gw_ok, 1)
                pe.nop().then_inc(o_left, 1)

                def pieces(b, which):
                    for x in which:
                        w, at = (weights.wq, x) if x < QCH else (weights.down, x - QCH)
                        pe.wait_ge(piece_out, b * PIECES + x + 1)
                        for d in range(DC):
                            last = nc.tensor.matmul(pQ[:, x % 2, :], w[:, d, at * P:(at + 1) * P], normT[:, d, bass.ds(b * BLK, BLK)],
                                                    start=d == 0, stop=d == DC - 1)
                        last.then_inc(piece, 1)

                def norms(b):
                    pe.wait_ge(sq_ok, b + 1)
                    pe.wait_ge(root_ok, b + 1)
                    for t in range(SUB):
                        for m in range(QCH):
                            at = t * SETS + m * SETS // QCH
                            last = nc.tensor.matmul(pN[:, at:at + SETS // QCH], qs[:, m, t * P:(t + 1) * P], weights.halves[:],
                                                    start=True, stop=True)
                    last.then_inc(n2_ok, 1)

                def scores(k, b, h, p):
                    pe.wait_ge(piece_out, b * PIECES + QCH + 2)
                    pe.wait_ge(s_ok, k + 1)
                    for t in range(2):
                        for m in range(QCH):
                            last = nc.tensor.matmul(pS[:, t, m * P:(m + 1) * P], qn[:, h, m, (p * 2 + t) * P:(p * 2 + t + 1) * P],
                                                    weights.keys[:], start=True, stop=True)
                    last.then_inc(sc_ok, 1)

                def step(n, b, i, final):
                    if not (final and i >= 2):
                        scores(n + 2, b + (i + 2) // 2, (i + 2) // 2 % 2, i % 2)
                    if i % 2 and not final:
                        norms(b + 2 + i // 2)
                        pieces(b + 2 + i // 2, range(QCH, PIECES))
                    if i % 2 == 0 and not final:
                        pieces(b + 2 + i // 2, range(QCH))
                    pe.wait_ge(wt_ok, n + 1)
                    pe.wait_ge(gw_ok, n + 1)
                    for t in range(2):
                        for e in range(DC):
                            last = nc.tensor.transpose(turned[:, e, t * P:(t + 1) * P], wt[:, t, e * P:(e + 1) * P], ident[:])
                    last.then_inc(turn_ok, 1)
                    pe.wait_ge(gw_ok, n + 2)
                    pe.wait_ge(o_left, n + 1)
                    for t in range(2):
                        for e in range(DC):
                            last = nc.tensor.matmul(pO[:, t * D:(t + 1) * D], gw[:, e, t * P:(t + 1) * P], weights.upw[:, e, :],
                                                    start=e == 0, stop=e == DC - 1)
                    last.then_inc(o_ok, 1)

                for b in range(2):
                    pieces(b, range(QCH))
                    norms(b)
                    scores(b, 0, 0, b)
                    pieces(b, range(QCH, PIECES))
                rounds(pe, step)

            @block.scalar
            def _(act):
                def queries(b, h):
                    if not isinstance(b, int) or b > 1:
                        act.wait_ge(sc_ok, b * 2 - 2)
                    for m in range(QCH):
                        act.wait_ge(piece, b * PIECES + m + 1)
                        nc.scalar.activation(qn[:, h, m, :], pQ[:, m % 2, :], ACT.Identity, scale=stats.gain[:],
                                             bias=stats.shift[:, m:m + 1]).then_inc(piece_out, 1)
                    act.wait_ge(piece_out, b * PIECES + QCH + 2)
                    if not isinstance(b, int) or b > 0:
                        act.wait_ge(n2_ok, b)
                    nc.scalar.activation(qs[:], qn[:, h], ACT.Square).then_inc(sq_ok, 1)

                def roots(b, h):
                    act.wait_ge(n2_ok, b + 1)
                    if not isinstance(b, int) or b > 1:
                        act.wait_ge(inv_ok, b * 2 - 2)
                    nc.scalar.activation(nrm[:, h, :], pN[:, 0:SUB * SETS], ACT.Sqrt).then_inc(root_ok, 1)

                def gates(b, h):
                    if not isinstance(b, int) or b > 1:
                        act.wait_ge(gw_ok, b * 2 - 1)
                    for e in range(DC):
                        act.wait_ge(piece, b * PIECES + QCH + e + 1)
                        nc.scalar.activation(g[:, h, e, :], pQ[:, (QCH + e) % 2, :], ACT.Gelu).then_inc(piece_out, 1)

                def exps(k, slot):
                    act.wait_ge(s_ok, k + 2)
                    if not isinstance(k, int) or k > 1:
                        act.wait_ge(prod_ok, k * 2 - 2)
                    nc.scalar.activation(ex[:, slot], s_[:, slot], ACT.Exp).then_inc(ex_ok, 1)

                def step(n, b, i, final):
                    if i % 2 == 0 and not final:
                        queries(b + 2 + i // 2, i // 2)
                    if not (final and i >= 2):
                        exps(n + 2, i % 2)
                    if i % 2 and not final:
                        roots(b + 2 + i // 2, i // 2)
                        gates(b + 2 + i // 2, i // 2)

                for b in range(2):
                    queries(b, b)
                    roots(b, b)
                    gates(b, b)
                for k in range(2):
                    exps(k, k)
                rounds(act, step)

            @block.gpsimd
            def _(pool):
                with pool.Fori(0, PAIRS // 2) as kk:
                    for slot in range(2):
                        k = kk * 2 + slot
                        pool.wait_ge(a0_ok, k + 1)
                        for t in range(2):
                            pool.wait_ge(summed, k * 2 + t + 1)
                            first = a0[:, t].unsqueeze(3)
                            second = ex[:, slot, t].rearrange("p (h f b) -> p h f b", h=PK_HEADS, f=2)[:, :, 1:2, :]
                            shape = (P, PK_HEADS, ROWS_IN, NKEY)
                            nc.gpsimd.tensor_tensor(prod[:, t].rearrange("p h (a b) -> p h a b", a=ROWS_IN),
                                                    first.broadcast_to(shape), second.broadcast_to(shape), ALU.mult).then_inc(multiplied, 1)
                            pool.wait_ge(multiplied, k * 2 + t + 1)
                            nc.gpsimd.tensor_tensor(prod[:, t, 0:PK_HEADS // 2], prod[:, t, 0:PK_HEADS // 2],
                                                    prod[:, t, PK_HEADS // 2:], ALU.add).then_inc(prod_ok, 1)

            @block.vector
            def _(dve):
                dve.nop().then_inc(root_ok, 1)
                dve.nop().then_inc(turn_ok, 1)
                dve.nop().then_inc(o_ok, 1)
                dve.nop().then_inc(summed, 2)
                PER_K = 10

                def inverse(b, h):
                    dve.wait_ge(root_ok, b + 3)
                    nc.vector.tensor_scalar(inv[:, h, :], nrm[:, h, :], 1e-12, None, ALU.max).then_inc(inv_ok, 1)
                    dve.wait_ge(inv_ok, b * 2 + 1)
                    nc.vector.reciprocal(inv[:, h, :], inv[:, h, :]).then_inc(inv_ok, 1)

                def scale(k, b, h, slot):
                    dve.wait_ge(sc_ok, k + 1)
                    dve.wait_ge(inv_ok, b * 2 + 2)
                    if not isinstance(k, int) or k > 1:
                        dve.wait_ge(ex_ok, k - 1)
                    nc.vector.tensor_tensor(s_[:, slot].rearrange("p t (a k) -> p (t a) k", k=NKEY),
                                            pS[:].rearrange("p t (a k) -> p (t a) k", k=NKEY),
                                            inv[:, h, slot * 2 * SETS:(slot + 1) * 2 * SETS].unsqueeze(2).broadcast_to((P, 2 * SETS, NKEY)),
                                            ALU.mult).then_inc(s_ok, 1)

                class Search:

                    def __init__(self, k, slot):
                        self.k, self.slot, self.st = k, slot, Steps(search, PER_K, k)
                        self.s3 = s_[:, slot].rearrange("p t (a k) -> p (t a) k", k=NKEY)
                        self.rep3 = rep[:].rearrange("p t (a k) -> p (t a) k", k=NKEY)
                        self.p4 = ex[:, slot].rearrange("p t (h f k) -> p (t h) f k", h=PK_HEADS, f=2)

                    def so_far(self):
                        dve.wait_ge(search, self.st.at(self.st.n))

                    def best(self):
                        dve.wait_ge(s_ok, self.k + 2)
                        dve.nop().then_inc(relay, 1)
                        for a in range(2 * SETS):
                            last = nc.vector.max(top[:, a, :], self.s3[:, a, :])
                        self.st.inc(last)

                    def only_four(self):
                        self.so_far()
                        self.st.inc(nc.vector.memset(top[:, :, TOPK_DIM:], 9.0))

                    def mark(self):
                        self.so_far()
                        dve.nop().then_inc(relay, 1)
                        for a in range(2 * SETS):
                            last = nc.vector.match_replace(self.rep3[:, a, :], top[:, a, :], self.s3[:, a, :], -1000.0)
                        self.st.inc(last)

                    def mask(self):
                        self.so_far()
                        dve.wait_ge(ex_ok, self.k + 1)
                        e = ex[:, self.slot]
                        self.st.inc(nc.vector.scalar_tensor_tensor(e, rep[:], -500.0, e, ALU.is_lt, ALU.mult))

                    def sums(self):
                        self.so_far()
                        self.st.inc(nc.vector.tensor_reduce(z[:], self.p4, AX_X, ALU.add))
                        self.st.inc(nc.vector.tensor_reduce(far[:].rearrange("p t h -> p (t h)"), self.p4[:, :, 0, ROWS_IN:], AX_X, ALU.add))

                    def shares(self):
                        z3 = z[:].rearrange("p (t h f) -> p t h f", t=2, f=2)
                        self.so_far()
                        self.st.inc(nc.vector.tensor_tensor(both[:], z3[:, :, :, 0], z3[:, :, :, 1], ALU.mult))
                        self.so_far()
                        self.st.inc(nc.vector.reciprocal(share[:], both[:]))
                        self.so_far()
                        first = self.p4[:, :, 0, 0:ROWS_IN]
                        inverse_sums = share[:].rearrange("p t h -> p (t h)").unsqueeze(2).broadcast_to((P, 2 * PK_HEADS, ROWS_IN))
                        nc.vector.tensor_tensor(a0[:].rearrange("p t h a -> p (t h) a"), first, inverse_sums,
                                                ALU.mult).then_inc(a0_ok, 1)
                        self.st.inc(nc.vector.tensor_tensor(far[:], far[:], share[:], ALU.mult))

                    def rest(self):
                        z3 = z[:].rearrange("p (t h f) -> p t h f", t=2, f=2)
                        self.so_far()
                        self.st.inc(nc.vector.tensor_tensor(far[:], far[:], z3[:, :, :, 1], ALU.mult))
                        self.so_far()
                        nc.vector.tensor_reduce(last_w[:, :, 0], far[:], AX_X, ALU.add).then_inc(last_ok, 1)
                        assert self.st.n == PER_K

                last_ok = sem("pk_last_ok")

                def add_heads(n, t):
                    dve.wait_ge(prod_ok, n * 2 + t + 1)
                    if t == 0:
                        dve.wait_ge(turn_ok, n + 1)
                    nc.vector.tensor_reduce(wt[:, t, :], prod[:, t, 0:PK_HEADS // 2].rearrange("p h e -> p e h"), AX_X, ALU.add).then_inc(summed, 1)

                def add_last(n):
                    dve.wait_ge(summed, n * 2 + 4)
                    dve.wait_ge(last_ok, n + 1)
                    nc.vector.tensor_tensor(wt[:, :, PK_EXP - 1:], wt[:, :, PK_EXP - 1:], last_w[:], ALU.add).then_inc(wt_ok, 1)

                def leave(n, b, h, p):
                    dve.wait_ge(turn_ok, n + 2)
                    dve.wait_ge(piece_out, b * PIECES + PIECES + 2)
                    dve.wait_ge(o_ok, n + 1)
                    nc.vector.tensor_tensor(gw[:], g[:, h, :, p * 2 * P:(p + 1) * 2 * P], turned, ALU.mult).then_inc(gw_ok, 1)

                def onto_res(n):
                    dve.wait_ge(o_ok, n + 2)
                    rows = res[:, bass.ds(n * 2, 2), :]
                    nc.vector.tensor_tensor(rows, rows, pO[:].rearrange("p (t d) -> p t d", t=2), ALU.add).then_inc(o_left, 1)

                def step(n, b, i, final):
                    after = not (final and i == 3)
                    if after:
                        pair = Search(n + 1, (i + 1) % 2)
                        pair.best()
                    if not (final and i >= 2):
                        if i % 2 == 0:
                            inverse(b + 1 + i // 2, (1 + i // 2) % 2)
                        scale(n + 2, b + (i + 2) // 2, (i + 2) // 2 % 2, i % 2)
                    if i:
                        onto_res(n - 1)
                    if after:
                        pair.only_four()
                    add_heads(n, 0)
                    if after:
                        pair.mark()
                        pair.mask()
                    add_heads(n, 1)
                    add_last(n)
                    if after:
                        pair.sums()
                        pair.shares()
                    leave(n, b + i // 2, i // 2, i % 2)
                    if after:
                        pair.rest()
                    if i == 3:
                        onto_res(n)

                inverse(0, 0)
                scale(0, 0, 0, 0)
                pair = Search(0, 0)
                pair.best()
                scale(1, 0, 0, 1)
                for stage in (pair.only_four, pair.mark, pair.mask, pair.sums, pair.shares, pair.rest):
                    stage()
                rounds(dve, step)


def norm_project(nc, sem, inp, res, rows, ident, rowsT, v_pad, logits):
    with ExitStack() as c:
        def sb(name, shape, dt=F32):
            return c.enter_context(nc.sbuf_tensor("pj_" + name, shape, dt))
        xn = sb("xn", [P, SUB, D])
        stats = sb("stats", [P, SUB, 6])
        mv = sb("mv", [P, SUB, 2])
        std = sb("std", [P, SUB])
        rstd = sb("rstd", [P, SUB])
        xT = sb("xT", [P, 2, DC, BLK])
        w = [sb("w" + n, [P, DC, D]) for n in "qk"]
        wv = sb("wv", [P, DC, D + EXPERTS])
        b = [sb("b" + n, [P, 2]) for n in "qk"]
        bv = sb("bv", [P, D])
        gate_b = sb("gate_b", [P, EXPERTS])
        cos = sb("cos", [P, BATCH, SEQ])
        sin = sb("sin", [P, BATCH, SEQ])
        turn = sb("turn", [P, 4, BLK])
        r = sb("r", [P, 2, 2, BLK])
        rest = sb("rest", [P, 2, 2, BLK])
        parts = sb("parts", [P, 2, 2, 3, 2, BLK], BF16)
        vp = sb("vp", [P, 2, SUB, HEADS, PADV])
        pT = c.enter_context(nc.psum_tensor("pj_pT", [P, DC, BLK], F32))
        pE = c.enter_context(nc.psum_tensor("pj_pE", [P, 4, BLK], F32))
        pV = c.enter_context(nc.psum_tensor("pj_pV", [P, 2, BLK], F32))
        (w_ok, stat, var_ok, std_ok, xn_ok, turned, kept, x_ok, p_ok, p_left, v_ok, v_left, rot, r_ok, part0, part1,
         part2, rest1, padded, store_free, relay) = (sem("pj_" + n) for n in (
             "w_ok", "stat", "var_ok", "std_ok", "xn_ok", "turned", "kept", "x_ok", "p_ok", "p_left", "v_ok", "v_left",
             "rot", "r_ok", "part0", "part1", "part2", "rest1", "padded", "store_free", "relay"))
        stored = [sem(f"pj_stored{h}") for h in range(2)]
        vstored = [sem(f"pj_vstored{h}") for h in range(2)]
        PB = SEQ // BLK
        v_by_batch = v_pad.rearrange("(b g) p t c -> b t p g c", b=BATCH)
        loads = [(w[0][:], inp["Wq"]), (w[1][:], inp["Wk"]), (wv[:, :, 0:D], inp["Wv"]), (wv[:, :, D:], inp["gate"]),
                 (b[0][:], inp["bq"]), (b[1][:], inp["bk"]), (bv[:], inp["bv"].broadcast_to((P, D))),
                 (gate_b[:], inp["gate_b"].broadcast_to((P, EXPERTS)))]
        for bt in range(BATCH):
            loads += [(cos[:, bt], inp["c_cos"]), (sin[:, bt], inp["c_sin"])]
        W_ALL = 16 * len(loads)
        with nc.Block() as block:
            @block.sync
            def _(sp):
                for dst, src in loads:
                    sp.dma_start(dst, src).then_inc(w_ok, 16)
                sp.nop().then_inc(stored[1], 1)
                sp.nop().then_inc(vstored[1], 1)
                with sp.Fori(0, BATCH) as bt:
                    with sp.Fori(0, PB // 2) as ii:
                        for h in range(2):
                            jj = bt * (PB // 2) + ii
                            j, i = jj * 2 + h, ii * 2 + h
                            sp.wait_ge(stored[1 - h], (jj + h) * 64 + 1 - h)
                            sp.wait_ge(vstored[1 - h], (jj + h) * 64 + 1 - h)
                            sp.nop().then_inc(store_free, 1)
                            for qk in range(2):
                                sp.wait_ge(part2, j * 2 + qk + 3)
                                for half in range(2):
                                    sp.dma_start(rowsT[qk, :, bass.ds(bt * D + half * P, P), bass.ds(i * BLK, BLK)]
                                                 .rearrange("a p t -> p a t"),
                                                 parts[:, h, qk, :, half, :]).then_inc(stored[h], 16)
                            sp.wait_ge(v_left, j * SUB * 2 + SUB * 2 + 3)
                            for s in range(SUB):
                                sp.dma_start(v_by_batch[bass.ds(bt, 1), bass.ds(i * SUB + s, 1), :, :, :]
                                             .rearrange("a t p g c -> (a t p) g c"),
                                             vp[:, h, s].rearrange("p (g h) c -> p g (h c)", g=HG)).then_inc(vstored[h], 16)
                for h in range(2):
                    sp.wait_ge(stored[h], BLOCKS // 2 * 64 + h)
                    sp.wait_ge(vstored[h], BLOCKS // 2 * 64 + h)

            @block.gpsimd
            def _(pool):
                for h in range(2):
                    nc.gpsimd.memset(vp[:, h, :, :, HD:], 0.0).then_inc(padded, 1)
                pool.wait_ge(padded, 2)
                for h in range(2):
                    nc.gpsimd.memset(vp[:, h, :, :, HD:HD + 1], 1.0).then_inc(padded, 1)
                pool.nop().then_inc(part2, 2)
                with pool.Fori(0, BLOCKS // 2) as jj:
                    for h in range(2):
                        for qk in range(2):
                            n = (jj * 2 + h) * 2 + qk
                            pool.wait_ge(part0, n + 1)
                            pool.wait_ge(part2, n + 1)
                            nc.gpsimd.tensor_tensor(rest[:, qk], r[:, qk], parts[:, h, qk, 0], ALU.subtract).then_inc(rest1, 1)
                            pool.wait_ge(part1, n + 1)
                            nc.gpsimd.tensor_tensor(parts[:, h, qk, 2], rest[:, qk], parts[:, h, qk, 1], ALU.subtract).then_inc(part2, 1)

            @block.scalar
            def _(act):
                act.nop().then_inc(store_free, 1)
                act.nop().then_inc(v_ok, 1)

                def root(n):
                    act.wait_ge(var_ok, n * 2 + 1)
                    nc.scalar.activation(std[:], std[:], ACT.Sqrt).then_inc(std_ok, 1)

                def keep(n, h):
                    act.wait_ge(xn_ok, n * SUB + SUB)
                    act.nop().then_inc(relay, 1)
                    nc.scalar.activation(rows[:, bass.ds(n * SUB, SUB), :], xn[:], ACT.Copy).then_inc(kept, 1)
                    act.wait_ge(turned, n + 2)
                    if not isinstance(n, int) or n > 1:
                        act.wait_ge(v_ok, (n - 1) * SUB + 1)
                    nc.scalar.activation(xT[:, h], pT[:], ACT.Copy).then_inc(x_ok, 1)

                def split(j, h, qk):
                    act.wait_ge(r_ok, j * 2 + qk + 2)
                    nc.scalar.activation(parts[:, h, qk, 0], r[:, qk], ACT.Copy).then_inc(part0, 1)
                    act.wait_ge(rest1, j * 2 + qk + 3)
                    nc.scalar.activation(parts[:, h, qk, 1], rest[:, qk], ACT.Copy).then_inc(part1, 1)

                def two_blocks(jj, final):
                    for h in range(2):
                        j = jj * 2 + h
                        ahead = not (final and h)
                        if ahead:
                            root(j + 1)
                        act.wait_ge(store_free, j + 1)
                        split(j, h, 0)
                        if ahead:
                            keep(j + 1, 1 - h)
                        split(j, h, 1)

                root(0)
                keep(0, 0)
                with act.Fori(0, BLOCKS // 2 - 1) as jj:
                    two_blocks(jj, False)
                two_blocks(BLOCKS // 2 - 1, True)

            @block.tensor
            def _(pe):
                pe.nop().then_inc(x_ok, 1)

                def transposes(n):
                    pe.wait_ge(xn_ok, n * SUB + SUB)
                    pe.wait_ge(x_ok, n + 1)
                    for d in range(DC):
                        for s in range(SUB):
                            last = nc.tensor.transpose(pT[:, d, s * P:(s + 1) * P], xn[:, s, d * P:(d + 1) * P], ident[:])
                    last.then_inc(turned, 1)

                def two_blocks(jj, final):
                    for h in range(2):
                        j = jj * 2 + h
                        pe.wait_ge(x_ok, j + 2)
                        for qk in range(2):
                            pe.wait_ge(p_left, j * 2 + qk + 1)
                            for eo in range(2):
                                for d in range(DC):
                                    last = nc.tensor.matmul(pE[:, qk * 2 + eo, :], w[qk][:, d, eo * P:(eo + 1) * P], xT[:, h, d, :],
                                                            start=d == 0, stop=d == DC - 1)
                            last.then_inc(p_ok, 1)
                        if not (final and h):
                            transposes(j + 1)
                        for s in range(SUB):
                            pe.wait_ge(v_left, (j * SUB + s) * 2 + 1)
                            for d in range(DC):
                                last = nc.tensor.matmul(pV[:, s % 2, 0:D + EXPERTS], xT[:, h, d, s * P:(s + 1) * P], wv[:, d, :],
                                                        start=d == 0, stop=d == DC - 1)
                            last.then_inc(v_ok, 1)

                transposes(0)
                pe.wait_ge(w_ok, W_ALL)
                with pe.Fori(0, BLOCKS // 2 - 1) as jj:
                    two_blocks(jj, False)
                two_blocks(BLOCKS // 2 - 1, True)

            @block.vector
            def _(dve):
                dve.nop().then_inc(turned, 1)
                dve.nop().then_inc(kept, 1)
                dve.nop().then_inc(r_ok, 1)
                dve.nop().then_inc(rest1, 2)
                dve.nop().then_inc(p_left, 2)
                dve.nop().then_inc(v_left, 3)

                def variance(n):
                    dve.wait_ge(kept, n + 1)
                    for s in range(SUB):
                        row = res[:, bass.ds(n * SUB + s, 1), :].rearrange("p a n -> p (a n)")
                        nc.vector.bn_stats(stats[:, s, :], row).then_inc(stat, 1)
                    dve.wait_ge(stat, n * 2 * SUB + SUB)
                    dve.nop().then_inc(relay, 1)
                    for s in range(SUB):
                        nc.vector.bn_aggr(mv[:, s, :], stats[:, s, :]).then_inc(stat, 1)
                    dve.wait_ge(stat, n * 2 * SUB + 2 * SUB)
                    nc.vector.tensor_scalar(std[:], mv[:, :, 1], EPS, None, ALU.add).then_inc(var_ok, 1)

                def normalise(n):
                    dve.wait_ge(std_ok, n + 1)
                    nc.vector.reciprocal(rstd[:], std[:]).then_inc(var_ok, 1)
                    dve.wait_ge(var_ok, n * 2 + 2)
                    dve.wait_ge(turned, n + 1)
                    for s in range(SUB):
                        row = res[:, bass.ds(n * SUB + s, 1), :].rearrange("p a n -> p (a n)")
                        nc.vector.tensor_scalar(xn[:, s, :], row, mv[:, s, 0:1], rstd[:, s:s + 1],
                                                ALU.subtract, ALU.mult).then_inc(xn_ok, 1)

                def rotate(j, qk):
                    n = j * 2 + qk
                    dve.wait_ge(p_ok, n + 1)
                    dve.wait_ge(r_ok, n + 1)
                    at = bass.ds(j * BLK, BLK)
                    for k, (eo, table) in enumerate(((0, cos), (0, sin), (1, sin), (1, cos))):
                        nc.vector.scalar_tensor_tensor(turn[:, k, :], pE[:, qk * 2 + eo, :], b[qk][:, eo:eo + 1],
                                                       table[:].rearrange("p b t -> p (b t)")[:, at], ALU.add, ALU.mult).then_inc(rot, 1)
                    dve.wait_ge(rot, n * 4 + 4)
                    dve.nop().then_inc(p_left, 1)
                    dve.wait_ge(rest1, n + 1)
                    nc.vector.tensor_tensor(r[:, qk], turn[:, 0:2, :], turn[:, 2:4, :], ALU.subtract).then_inc(r_ok, 1)

                def two_blocks(jj, final):
                    for h in range(2):
                        j = jj * 2 + h
                        ahead = not (final and h)
                        if ahead:
                            variance(j + 1)
                        rotate(j, 0)
                        if ahead:
                            normalise(j + 1)
                        rotate(j, 1)
                        dve.wait_ge(store_free, j + 1)
                        for s in range(SUB):
                            dve.wait_ge(v_ok, j * SUB + s + 2)
                            nc.vector.tensor_tensor(vp[:, h, s, :, 0:HD], pV[:, s % 2, 0:D].rearrange("p (h c) -> p h c", c=HD),
                                                    bv[:].rearrange("p (h c) -> p h c", c=HD), ALU.add).then_inc(v_left, 1)
                            lg = logits[:, bass.ds(j * SUB + s, 1), :].rearrange("p a e -> p (a e)")
                            nc.vector.tensor_tensor(lg, pV[:, s % 2, D:D + EXPERTS], gate_b[:], ALU.add).then_inc(v_left, 1)

                variance(0)
                normalise(0)
                dve.wait_ge(w_ok, W_ALL)
                dve.wait_ge(padded, 4)
                with dve.Fori(0, BLOCKS // 2 - 1) as jj:
                    two_blocks(jj, False)
                two_blocks(BLOCKS // 2 - 1, True)


class Operands:

    def __init__(self, nc, sem, stack, rowsT, v_pad):
        def sb(name, shape, dt):
            return stack.enter_context(nc.sbuf_tensor("op_" + name, shape, dt, side="right"))
        self.rowsT, self.v_pad = rowsT, v_pad
        self.q = sb("q", [P, 2, HPG, SEQ], BF16)
        self.k = sb("k", [P, 2, HPG, SEQ], BF16)
        self.v = sb("v", [P, 2, KT, HPG * PADV], F32)
        self.g_in = [sem(f"op_g_in{s}") for s in range(2)]
        self.ones = sem("op_ones")
        self.per_group = 16 * (2 * TERMS + 1)

    def load(self, sp, g, s):
        for t, parts, dst in ((0, PARTS_Q, self.q), (1, PARTS_K, self.k)):
            for n, part in enumerate(parts):
                src = self.rowsT[t, part, bass.ds(g * HPG * HD, HPG * HD), :].rearrange("(h d) s -> d h s", d=HD)
                sp.dma_start(dst[n * HD:(n + 1) * HD, s], src).then_inc(self.g_in[s], 16)
        sp.dma_start(self.v[:, s], self.v_pad[bass.ds(g, 1), :, :, :].rearrange("a p t c -> p (a t) c")).then_inc(self.g_in[s], 16)


def route(nc, sem, inp, rows, logits, weight, gather_at, moe_in, operands):
    TE = TILES * EXPERTS
    with ExitStack() as c:
        def sb(name, shape, dt=F32):
            return c.enter_context(nc.sbuf_tensor("rt_" + name, shape, dt))
        before = sb("before", [P, P])
        ones = sb("ones", [P, P])
        expert = sb("expert", [P, EXPERTS])
        trash = sb("trash", [P, TILES])
        e = sb("e", [P, TILES, EXPERTS])
        hot = sb("hot", [P, TILES, EXPERTS])
        cand = sb("cand", [P, TILES, EXPERTS])
        sums = sb("sums", [P, 2, TILES, EXPERTS])
        at = sb("at", [P, TILES, EXPERTS])
        v = sb("v", [P, 12, TILES])
        scatter_at = sb("scatter_at", [P, TILES], I32)
        pc = c.enter_context(nc.psum_tensor("rt_pc", [P, 2, BLK], F32))
        w_ok, step, exp_ok, cum, where_ok, sent = (sem("rt_" + n) for n in ("w_ok", "step", "exp_ok", "cum", "where_ok", "sent"))
        MX, SUM, IDX, POS, KEEP, SLOT, FAR, TMP = range(8)
        with nc.Block() as block:
            @block.sync
            def _(sp):
                for t, name in ((before, "c_before"), (ones, "c_ones"), (expert, "c_expert"), (trash, "c_trash")):
                    sp.dma_start(t[:], inp[name]).then_inc(w_ok, 16)
                for s in range(2):
                    operands.load(sp, s, s)

            @block.tensor
            def _(pe):
                pe.wait_ge(w_ok, 64)
                pe.wait_ge(step, 7)
                nc.tensor.matmul(pc[:, 0, 0:TE], before[:], hot[:].rearrange("p t e -> p (t e)"), start=True, stop=True)
                nc.tensor.matmul(pc[:, 1, 0:TE], ones[:], hot[:].rearrange("p t e -> p (t e)"), start=True,
                                 stop=True).then_inc(cum, 1)

            @block.scalar
            def _(act):
                act.wait_ge(step, 2)
                nc.scalar.activation(e[:], e[:], ACT.Exp).then_inc(exp_ok, 1)

            @block.vector
            def _(dve):
                st = Steps(step, 99)

                def then(ins):
                    dve.wait_ge(step, st.at(st.inc(ins)))

                def by_token(k):
                    return v[:, k, :].unsqueeze(2).broadcast_to((P, TILES, EXPERTS))

                per_expert = expert[:].unsqueeze(1).broadcast_to((P, TILES, EXPERTS))
                dve.wait_ge(w_ok, 64)
                then(nc.vector.tensor_reduce(v[:, MX, :], logits[:], AX_X, ALU.max))
                then(nc.vector.tensor_tensor(e[:], logits[:], by_token(MX), ALU.subtract))
                then(nc.vector.tensor_tensor(hot[:], logits[:], by_token(MX), ALU.is_equal))
                then(nc.vector.tensor_scalar(cand[:], hot[:], -float(EXPERTS), None, ALU.mult))
                then(nc.vector.tensor_tensor(cand[:], cand[:], per_expert, ALU.add))
                then(nc.vector.tensor_reduce(v[:, IDX, :], cand[:], AX_X, ALU.min))
                then(nc.vector.tensor_tensor(hot[:], cand[:], by_token(IDX), ALU.is_equal))
                then(nc.vector.tensor_scalar(v[:, IDX, :], v[:, IDX, :], float(EXPERTS), None, ALU.add))
                dve.wait_ge(exp_ok, 1)
                then(nc.vector.tensor_reduce(v[:, SUM, :], e[:], AX_X, ALU.add))
                then(nc.vector.reciprocal(v[:, MX, :], v[:, SUM, :]))
                dve.wait_ge(cum, 1)
                then(nc.vector.memset(sums[:], 0.0))
                then(nc.vector.tensor_copy(sums[:, 0, 1:, :], pc[:, 1, 0:TE].rearrange("p (t e) -> p t e", e=EXPERTS)[:, :TILES - 1]))
                cur, n = 0, 1
                while n < TILES:
                    st.inc(nc.vector.tensor_copy(sums[:, 1 - cur, 0:n, :], sums[:, cur, 0:n, :]))
                    then(nc.vector.tensor_tensor(sums[:, 1 - cur, n:, :], sums[:, cur, n:, :], sums[:, cur, :TILES - n, :], ALU.add))
                    cur, n = 1 - cur, 2 * n
                then(nc.vector.tensor_tensor(at[:], sums[:, cur], pc[:, 0, 0:TE].rearrange("p (t e) -> p t e", e=EXPERTS), ALU.add))
                then(nc.vector.tensor_tensor(at[:], at[:], hot[:], ALU.mult))
                then(nc.vector.tensor_reduce(v[:, POS, :], at[:], AX_X, ALU.add))
                then(nc.vector.tensor_scalar(v[:, KEEP, :], v[:, POS, :], float(CAP), None, ALU.is_le))
                then(nc.vector.tensor_tensor(weight[:], v[:, MX, :], v[:, KEEP, :], ALU.mult))
                then(nc.vector.tensor_scalar(v[:, POS, :], v[:, POS, :], -1.0, None, ALU.add))
                then(nc.vector.tensor_tensor(v[:, POS, :], v[:, POS, :], v[:, KEEP, :], ALU.mult))
                then(nc.vector.scalar_tensor_tensor(v[:, SLOT, :], v[:, IDX, :], float(CAP), v[:, POS, :], ALU.mult, ALU.add))
                then(nc.vector.tensor_tensor(v[:, FAR, :], trash[:], v[:, SLOT, :], ALU.subtract))
                then(nc.vector.tensor_scalar(v[:, TMP, :], v[:, KEEP, :], -1.0, 1.0, ALU.mult, ALU.add))
                then(nc.vector.tensor_tensor(v[:, FAR, :], v[:, FAR, :], v[:, TMP, :], ALU.mult))
                then(nc.vector.tensor_tensor(v[:, FAR, :], v[:, FAR, :], v[:, SLOT, :], ALU.add))
                nc.vector.tensor_copy(gather_at[:], v[:, SLOT, :]).then_inc(where_ok, 1)
                nc.vector.tensor_copy(scatter_at[:], v[:, FAR, :]).then_inc(where_ok, 1)

            @block.gpsimd
            def _(pool):
                for s in range(2):
                    nc.gpsimd.memset(operands.k[MROW:MROW + 1, s], 1.0).then_inc(operands.ones, 1)
                pool.wait_ge(where_ok, 2)
                for t in range(TILES):
                    pool.indirect_dma_start(moe_in, bass.IndirectOffsetOnAxis(ap=scatter_at[:, t:t + 1], axis=0),
                                            rows[:, t, :], None).then_inc(sent, 16)
                pool.wait_ge(sent, 16 * TILES)


def attention_timeline():
    steps = [(s, qt, kt) for s in range(2) for qt in range(QT) for kt in range(4 * qt + SUB)]
    width = [BLK - P * max(0, kt - 4 * qt) for _, qt, kt in steps]
    events = []
    ready, turn = [], None
    for s in range(2):
        mine = [n for n, st in enumerate(steps) if st[0] == s]
        items = [4 * s + 3] + [4 * s + 4 + x for x in range(3)]
        units = [(it, u) for it in items for u in range(HPG * len(attention_units(it % QT)))]
        cost = [0]
        for it, u in units:
            cost.append(cost[-1] + 64 + attention_units(it % QT)[u // HPG][2])
        total, spent, at = sum(width[n] for n in mine), 0, 0
        for n in mine:
            spent += width[n]
            lot = []
            while at < len(units) and cost[at + 1] * total <= cost[-1] * spent:
                lot.append(units[at])
                at += 1
            quarter = (len(lot) + 3) // 4
            for pair in range(2):
                events.append(("S", n + 1, pair))
                for it, u in lot[:quarter]:
                    events.append(("U", it, u))
                    if u + 1 == HPG * len(attention_units(it % QT)):
                        events.append(("N", it))
                        ready.append((n, it))
                lot = lot[quarter:]
            if turn is not None:
                events.append(("T", turn))
                turn = None
            events.append(("V", n))
            if n + 1 == len(steps) or steps[n + 1][:2] != steps[n][:2]:
                turn = 4 * s + steps[n][1]
                events.append(("O", turn))
            for it, u in lot:
                events.append(("U", it, u))
                if u + 1 == HPG * len(attention_units(it % QT)):
                    events.append(("N", it))
                    ready.append((n, it))
            while ready and (ready[0][0] < n or n + 1 == len(steps)):
                events.append(("R", ready.pop(0)[1]))
    events.append(("T", turn))
    return steps, events


def attention_units(qt):
    return [(qs, ch, min(BLK, P * (4 * qt + qs + 1) - BLK * ch)) for qs in range(SUB) for ch in range(qt + 1)]


def attention(nc, sem, inp, res, operands, ctxt, wo, ident, identb):
    G = BATCH * HG
    ROUNDS = G // 2
    ROWS = MROW + 1
    PER = sum(4 * qt + SUB for qt in range(QT))
    ITEMS = 2 * QT
    UNITS = [HPG * len(attention_units(qt)) for qt in range(QT)]
    UPER = sum(UNITS)
    STEPS, EVENTS = attention_timeline()
    AHEAD = 3
    RING = 4
    assert PER % RING == 0

    def unit_number(rnd, it, u):
        return (rnd * 2 + it // QT) * UPER + sum(UNITS[:it % QT]) + u

    def last_round(event):
        return (event[0] == "S" and event[1] == len(STEPS)) or (event[0] in "UNR" and event[1] >= ITEMS)

    with ExitStack() as c:
        def sb(name, shape, dt=F32):
            return c.enter_context(nc.sbuf_tensor("at_" + name, shape, dt))
        q, k, v = operands.q, operands.k, operands.v
        prob = sb("prob", [P, RING, HPG, BLK])
        masks = sb("masks", [P, 2, P])
        masksb = sb("masksb", [P, 2, P], BF16)
        mask_k, mask_q = masksb[:, 0, :], masksb[:, 1, :]
        peak = sb("peak", [P, HPG, SUB, QT])
        neg = sb("neg", [P, 2, HPG, SUB], BF16)
        mrow = sb("mrow", [P, BLK], BF16)
        o = sb("o", [P, BLK])
        inv = sb("inv", [P, SUB, HPG])
        bo = sb("bo", [P, D])
        pS = c.enter_context(nc.psum_tensor("at_pS", [P, 2, 2, BLK], F32))
        pM = c.enter_context(nc.psum_tensor("at_pM", [P, 2, BLK], F32))
        pR = c.enter_context(nc.psum_tensor("at_pR", [P, BLK], F32))
        pO = c.enter_context(nc.psum_tensor("at_pO", [P, BLK], F32))
        names = ("w_ok", "masks_ok", "m_made", "m_left", "neg_ok", "row_made", "row_ok", "row_in",
                 "s_made", "p_ok", "pv", "o_ok", "turned", "inv_ok", "ctx_ok", "relay", "clean")
        (w_ok, masks_ok, m_made, m_left, neg_ok, row_made, row_ok, row_in,
         s_made, p_ok, pv, o_ok, turned, inv_ok, ctx_ok, relay, clean) = (sem("at_" + n) for n in names)
        g_in, G_IN = operands.g_in, operands.per_group
        with nc.Block() as block:
            @block.sync
            def _(sp):
                for t, src in ((masks, inp["c_masks"]), (wo, inp["Wo"]), (bo, inp["bo"].broadcast_to((P, D)))):
                    sp.dma_start(t[:], src).then_inc(w_ok, 16)

                with sp.Fori(1, ROUNDS) as rnd:
                    for s in range(2):
                        sp.wait_ge(pv, (rnd * 2 + s - 1) * PER + RING)
                        operands.load(sp, rnd * 2 + s, s)

            @block.gpsimd
            def _(pool):
                def place(n, it):
                    pool.wait_ge(row_ok, n + 2)
                    pool.nop().then_inc(relay, 1)
                    s, qt = it // QT % 2, it % QT
                    for h in range(HPG):
                        pool.dma_start(q[MROW:MROW + 1, s, h, qt * BLK:(qt + 1) * BLK], mrow[32 * h:32 * h + 1, :]).then_inc(row_in, 16)

                for it in range(AHEAD):
                    place(it, it)
                with pool.Fori(0, ROUNDS - 1) as rnd:
                    for it in range(AHEAD, AHEAD + ITEMS):
                        place(rnd * ITEMS + it, it)
                for it in range(AHEAD, ITEMS):
                    place((ROUNDS - 1) * ITEMS + it, it)
                pool.wait_ge(w_ok, 48)
                pool.wait_ge(clean, 1)
                for t in range(TILES):
                    nc.gpsimd.tensor_tensor(res[:, t, :], res[:, t, :], bo[:], ALU.add)

            @block.tensor
            def _(pe):
                pe.nop().then_inc(row_ok, 1)
                pe.nop().then_inc(ctx_ok, 1)
                pe.nop().then_inc(o_ok, 1)
                pe.wait_ge(w_ok, 48)
                pe.wait_ge(operands.ones, 2)
                pe.wait_ge(masks_ok, 1)
                pe.wait_ge(clean, 1)

                def maxima(rnd, it, u):
                    s, qt = it // QT % 2, it % QT
                    (qs, ch, width), h = attention_units(qt)[u // HPG], u % HPG
                    i = 4 * qt + qs
                    bank = pM[:, u % 2, :]
                    pe.wait_ge(m_left, unit_number(rnd, it, u) + 1)
                    last = nc.tensor.matmul(bank[:, 0:width], q[0:MROW, s, h, i * P:(i + 1) * P],
                                            k[0:MROW, s, h, ch * BLK:ch * BLK + width], start=True, stop=ch < qt)
                    if ch == qt:
                        last = nc.tensor.matmul(bank[:, width - P:width], identb[:], mask_k, start=False, stop=True)
                    last.then_inc(m_made, 1)

                def row(n, it, turns):
                    pe.wait_ge(neg_ok, n + 2)
                    pe.wait_ge(row_ok, n + 1)
                    pe.wait_ge(ctx_ok, turns + 1)
                    for h in range(HPG):
                        for qs in range(SUB):
                            last = nc.tensor.matmul(pR[32 * h:32 * h + 1, qs * P:(qs + 1) * P], neg[:, it % 2, h, qs:qs + 1], identb[:],
                                                    start=True, stop=True, tile_position=(0, 32 * h))
                    last.then_inc(row_made, 1)

                def scores(rnd, step, pair):
                    s, qt, kt = STEPS[step % len(STEPS)]
                    n = rnd * len(STEPS) + step
                    if kt == 0 and pair == 0:
                        it = QT * (step // PER) + qt
                        pe.wait_ge(row_in, (rnd * ITEMS + it + 1) * 16 * HPG)
                    r = max(0, kt - 4 * qt)
                    diag = kt >= 4 * qt
                    pe.wait_ge(p_ok, n * 2 + pair + 1)
                    for x in range(2):
                        h = pair * 2 + x
                        last = nc.tensor.matmul(pS[:, pair, x, r * P:], k[0:ROWS, s, h, kt * P:(kt + 1) * P],
                                                q[0:ROWS, s, h, qt * BLK + r * P:(qt + 1) * BLK], start=True, stop=not diag)
                        if diag:
                            last = nc.tensor.matmul(pS[:, pair, x, r * P:(r + 1) * P], identb[:], mask_q, start=False, stop=True)
                    last.then_inc(s_made, 1)

                def values(rnd, step):
                    s, qt, kt = STEPS[step]
                    n = rnd * len(STEPS) + step
                    r = max(0, kt - 4 * qt)
                    if kt == 0:
                        pe.wait_ge(o_ok, rnd * ITEMS + s * QT + qt + 1)
                    pe.wait_ge(p_ok, n * 2 + 4)
                    for h in range(HPG):
                        last = nc.tensor.matmul(pO[32 * h:32 * (h + 1), r * P:], v[:, s, kt, h * PADV:(h + 1) * PADV],
                                                prob[:, step % RING, h, r * P:], start=kt == 0, stop=kt == 4 * qt + SUB - 1,
                                                tile_position=(0, 32 * h))
                    last.then_inc(pv, 1)

                def turn_out(n, rows):
                    pe.wait_ge(o_ok, n + 2)
                    pe.wait_ge(row_ok, rows + 1)
                    pe.wait_ge(ctx_ok, n + 1)
                    for qs in range(SUB):
                        last = nc.tensor.transpose(pR[:, qs * P:(qs + 1) * P], o[:, qs * P:(qs + 1) * P], ident[:])
                    last.then_inc(turned, 1)

                pe.wait_ge(g_in[0], G_IN)
                for it in range(AHEAD):
                    for u in range(UNITS[it]):
                        maxima(0, it, u)
                    row(it, it, 0)
                for pair in range(2):
                    scores(0, 0, pair)

                def one_round(rnd, final):
                    first = rnd * ITEMS
                    rows, turns, slot1 = AHEAD, 0, False
                    for e in EVENTS:
                        if final and last_round(e):
                            continue
                        if e[0] == "S":
                            scores(rnd, e[1], e[2])
                        elif e[0] == "U":
                            if e[1] == QT and e[2] == 0:
                                pe.wait_ge(g_in[1], (rnd + 1) * G_IN)
                            if e[1] == 2 * QT and e[2] == 0:
                                pe.wait_ge(g_in[0], (rnd + 2) * G_IN)
                            maxima(rnd, e[1], e[2])
                        elif e[0] == "V":
                            values(rnd, e[1])
                        elif e[0] == "R":
                            row(first + e[1], e[1], first + turns)
                            rows += 1
                        elif e[0] == "T":
                            turn_out(first + e[1], first + rows)
                            turns += 1

                with pe.Fori(0, ROUNDS - 1) as rnd:
                    one_round(rnd, False)
                one_round(ROUNDS - 1, True)

            @block.scalar
            def _(act):
                act.wait_ge(w_ok, 48)
                nc.scalar.activation(masksb[:], masks[:], ACT.Copy).then_inc(masks_ok, 1)
                act.nop().then_inc(pv, RING)
                act.nop().then_inc(p_ok, 2)

                def exps(rnd, step, pair):
                    _, qt, kt = STEPS[step % len(STEPS)]
                    n = rnd * len(STEPS) + step
                    r = max(0, kt - 4 * qt)
                    act.wait_ge(s_made, n * 2 + pair + 1)
                    if pair == 0:
                        act.wait_ge(pv, n + 1)
                    nc.scalar.activation(prob[:, step % RING, pair * 2:pair * 2 + 2, r * P:], pS[:, pair, :, r * P:],
                                         ACT.Exp, scale=HD ** -0.5).then_inc(p_ok, 1)

                def row_copy(n):
                    act.wait_ge(row_made, n + 1)
                    if not isinstance(n, int) or n > 0:
                        act.wait_ge(row_in, n * 16 * HPG)
                    nc.scalar.activation(mrow[:], pR[:], ACT.Copy).then_inc(row_ok, 1)

                for it in range(AHEAD):
                    row_copy(it)
                for pair in range(2):
                    exps(0, 0, pair)

                def one_round(rnd, final):
                    for e in EVENTS:
                        if final and last_round(e):
                            continue
                        if e[0] == "S":
                            exps(rnd, e[1], e[2])
                        elif e[0] == "R":
                            row_copy(rnd * ITEMS + e[1])
                        elif e[0] == "O":
                            n = rnd * ITEMS + e[1]
                            steps = sum(4 * x + SUB for x in range(e[1] % QT + 1)) + e[1] // QT * PER
                            act.wait_ge(pv, rnd * len(STEPS) + steps + RING)
                            act.wait_ge(turned, n + 1)
                            nc.scalar.activation(o[:], pO[:], ACT.Copy).then_inc(o_ok, 1)

                with act.Fori(0, ROUNDS - 1) as rnd:
                    one_round(rnd, False)
                one_round(ROUNDS - 1, True)

            @block.vector
            def _(dve):
                nc.vector.memset(pR[:], 0.0).then_inc(clean, 1)
                dve.nop().then_inc(neg_ok, 1)
                dve.nop().then_inc(turned, 1)
                dve.nop().then_inc(m_left, 2)

                def maxima(rnd, it, u):
                    (qs, ch, width), h = attention_units(it % QT)[u // HPG], u % HPG
                    x = unit_number(rnd, it, u)
                    dve.wait_ge(m_made, x + 1)
                    if u == 0:
                        dve.wait_ge(neg_ok, rnd * ITEMS + it + 1)
                    nc.vector.tensor_reduce(peak[:, h, qs, ch:ch + 1], pM[:, u % 2, 0:width], AX_X, ALU.max).then_inc(m_left, 1)

                def negate(rnd, it):
                    dve.wait_ge(m_left, unit_number(rnd, it, UNITS[it % QT] - 1) + 3)
                    if not isinstance(rnd, int) or rnd > 0 or it > 1:
                        dve.wait_ge(row_made, rnd * ITEMS + it - 1)
                    nc.vector.tensor_reduce(neg[:, it % 2], peak[:, :, :, 0:it % QT + 1], AX_X, ALU.max, negate=True).then_inc(neg_ok, 1)

                def outputs(rnd, it):
                    n, s, qt = rnd * ITEMS + it, it // QT, it % QT
                    dve.wait_ge(turned, n + 2)
                    t4 = pR[:].rearrange("p (s h c) -> p s h c", s=SUB, h=HPG)
                    dve.wait_ge(ctx_ok, n + 1)
                    nc.vector.reciprocal(inv[:], t4[:, :, :, HD]).then_inc(inv_ok, 1)
                    dve.wait_ge(inv_ok, n + 1)
                    to = ctxt[:, bass.ds(rnd * 2 + s, 1), qt * SUB:(qt + 1) * SUB, :].rearrange("p a s (h c) -> p (a s) h c", h=HPG)
                    nc.vector.tensor_tensor(to, t4[:, :, :, 0:HD], inv[:].unsqueeze(3).broadcast_to((P, SUB, HPG, HD)),
                                            ALU.mult).then_inc(ctx_ok, 1)

                for it in range(AHEAD):
                    for u in range(UNITS[it]):
                        maxima(0, it, u)
                    negate(0, it)

                def one_round(rnd, final):
                    for e in EVENTS:
                        if final and last_round(e):
                            continue
                        if e[0] == "U":
                            maxima(rnd, e[1], e[2])
                        elif e[0] == "N":
                            negate(rnd, e[1])
                        elif e[0] == "T":
                            outputs(rnd, e[1])

                with dve.Fori(0, ROUNDS - 1) as rnd:
                    one_round(rnd, False)
                one_round(ROUNDS - 1, True)


class Experts:

    def __init__(self, nc, sem, inp, stack, moe_in):
        def sb(name, shape):
            return stack.enter_context(nc.sbuf_tensor("ex_" + name, shape, F32, side="right"))
        self.inp, self.moe_in = inp, moe_in
        self.w1 = [sb(f"w1_{s}", [P, DC, FF]) for s in range(2)]
        self.w2 = [sb(f"w2_{s}", [P, FC, D]) for s in range(2)]
        self.xe = [sb(f"xe_{s}", [P, CT, D]) for s in range(2)]
        self.b1 = sb("b1", [P, EXPERTS, FC])
        self.b2 = sb("b2", [P, EXPERTS, D])
        self.e_in = [sem(f"ex_e_in{s}") for s in range(2)]
        self.b_ok = sem("ex_b_ok")

    def load_biases(self, sp):
        sp.dma_start(self.b1[:], self.inp["b1"]).then_inc(self.b_ok, 16)
        sp.dma_start(self.b2[:].rearrange("p e d -> p (e d)"), self.inp["b2"].broadcast_to((P, EXPERTS * D))).then_inc(self.b_ok, 16)

    def load(self, sp, e, s):
        rows = self.moe_in[bass.ds(e * CAP, CAP), :].rearrange("(t p) d -> p t d", p=P)
        sp.dma_start(self.xe[s][:], rows).then_inc(self.e_in[s], 16)
        for w, name in ((self.w1, "w1"), (self.w2, "w2")):
            sp.dma_start(w[s][:], self.inp[name][:, bass.ds(e, 1), :, :].rearrange("p a c f -> p (a c) f")).then_inc(self.e_in[s], 16)


def attention_out(nc, sem, res, ctxt, wo, ident, experts):
    with ExitStack() as c:
        cx = [c.enter_context(nc.sbuf_tensor(f"ao_cx{h}", [P, SUB, D], F32)) for h in range(2)]
        cT = [c.enter_context(nc.sbuf_tensor(f"ao_cT{h}", [P, DC, BLK], F32)) for h in range(2)]
        pC = c.enter_context(nc.psum_tensor("ao_pC", [P, 2, DC, BLK], F32))
        pW = c.enter_context(nc.psum_tensor("ao_pW", [P, 2, BLK], F32))
        got, turned, cT_ok, made, left = (sem("ao_" + n) for n in ("got", "turned", "cT_ok", "made", "left"))
        with nc.Block() as block:
            @block.sync
            def _(sp):
                experts.load_biases(sp)
                for s in range(2):
                    experts.load(sp, s, s)

            @block.gpsimd
            def _(pool):
                pool.nop().then_inc(turned, 2)
                with pool.Fori(0, BATCH) as b:
                    with pool.Fori(0, QT // 2) as ii:
                        for h in range(2):
                            i = ii * 2 + h
                            pool.wait_ge(turned, b * QT + i + 1)
                            nc.gpsimd.tensor_copy(cx[h][:].rearrange("p s (g c) -> p g s c", g=HG),
                                                  ctxt[:, bass.ds(b * HG, HG), bass.ds(i * SUB, SUB), :]).then_inc(got, 1)

            @block.tensor
            def _(pe):
                pe.nop().then_inc(cT_ok, 2)

                def turn(j, h):
                    pe.wait_ge(got, j + 1)
                    pe.wait_ge(cT_ok, j + 1)
                    for d in range(DC):
                        for s in range(SUB):
                            last = nc.tensor.transpose(pC[:, h, d, s * P:(s + 1) * P], cx[h][:, s, d * P:(d + 1) * P], ident[:])
                    last.then_inc(turned, 1)

                def two_blocks(jj, final):
                    for h in range(2):
                        j = jj * 2 + h
                        if not (final and h):
                            turn(j + 1, 1 - h)
                        pe.wait_ge(cT_ok, j + 3)
                        for s in range(SUB):
                            pe.wait_ge(left, j * SUB + s + 1)
                            for d in range(DC):
                                last = nc.tensor.matmul(pW[:, s % 2, 0:D], cT[h][:, d, s * P:(s + 1) * P], wo[:, d, :],
                                                        start=d == 0, stop=d == DC - 1)
                            last.then_inc(made, 1)

                turn(0, 0)
                with pe.Fori(0, BLOCKS // 2 - 1) as jj:
                    two_blocks(jj, False)
                two_blocks(BLOCKS // 2 - 1, True)

            @block.scalar
            def _(act):
                act.nop().then_inc(made, SUB + 1)
                with act.Fori(0, BLOCKS // 2) as jj:
                    for h in range(2):
                        j = jj * 2 + h
                        act.wait_ge(turned, j + 3)
                        act.wait_ge(made, j * SUB + 1)
                        nc.scalar.activation(cT[h][:], pC[:, h], ACT.Copy).then_inc(cT_ok, 1)

            @block.vector
            def _(dve):
                dve.nop().then_inc(left, 2)
                with dve.Fori(0, BLOCKS) as j:
                    for s in range(SUB):
                        dve.wait_ge(made, j * SUB + s + SUB + 2)
                        row = res[:, bass.ds(j * SUB + s, 1), :].rearrange("p a n -> p (a n)")
                        nc.vector.tensor_tensor(row, row, pW[:, s % 2, 0:D], ALU.add).then_inc(left, 1)


def moe(nc, sem, inp, res, weight, gather_at, moe_out, ident, out, experts):
    HC = CT * P // 2
    with ExitStack() as c:
        def sb(name, shape, dt=F32):
            return c.enter_context(nc.sbuf_tensor("me_" + name, shape, dt))
        w1, w2, xe, b1, b2 = experts.w1, experts.w2, experts.xe, experts.b1, experts.b2
        b_ok, e_in = experts.b_ok, experts.e_in
        b1e = sb("b1e", [P, FC])
        xT = sb("xT", [P, DC, CT * P])
        h = sb("h", [P, FC, CT * P])
        eo = [sb(f"eo_{s}", [P, CT, D]) for s in range(2)]
        y = sb("y", [P, SUB, 2, D])
        pX = c.enter_context(nc.psum_tensor("me_pX", [P, 2, BLK], F32))
        pH = c.enter_context(nc.psum_tensor("me_pH", [P, 4, BLK], F32))
        pO = c.enter_context(nc.psum_tensor("me_pO", [P, 2, BLK], F32))
        stored, b1_ok, relay = sem("me_rows_stored"), sem("me_b1_ok"), sem("me_relay")
        e_out = [sem(f"me_e_out{s}") for s in range(2)]
        x_turn, x_left, h_made, h_left, o_made, o_left = (
            sem("me_" + n) for n in ("x_turn", "x_left", "h_made", "h_left", "o_made", "o_left"))
        with nc.Block() as block:
            @block.sync
            def _(sp):
                sp.nop().then_inc(o_made, 1)

                with sp.Fori(1, EXPERTS // 2) as pair:
                    for s in range(2):
                        sp.wait_ge(o_made, (pair * 2 + s - 1) * CT + 1)
                        experts.load(sp, pair * 2 + s, s)

            @block.tensor
            def _(pe):
                with pe.Fori(0, EXPERTS // 2) as pair:
                    for s in range(2):
                        e = pair * 2 + s
                        pe.wait_ge(e_in[s], pair * 48 + 48)
                        for t in range(CT):
                            pe.wait_ge(x_left, e * CT + t + 1)
                            for d in range(DC):
                                last = nc.tensor.transpose(pX[:, t % 2, d * P:(d + 1) * P], xe[s][:, t, d * P:(d + 1) * P], ident[:])
                            last.then_inc(x_turn, 1)
                        pe.wait_ge(x_left, e * CT + CT + 2)
                        for f in range(FC):
                            for k in range(2):
                                n = f * 2 + k
                                pe.wait_ge(h_left, e * FC * 2 + n + 1)
                                for d in range(DC):
                                    last = nc.tensor.matmul(pH[:, n % 4, 0:HC], w1[s][:, d, f * P:(f + 1) * P],
                                                            xT[:, d, k * HC:(k + 1) * HC], start=d == 0, stop=d == DC - 1)
                                last.then_inc(h_made, 1)
                        pe.wait_ge(h_left, (e + 1) * FC * 2 + 4)
                        for t in range(CT):
                            pe.wait_ge(o_left, e * CT + t + 1)
                            for f in range(FC):
                                last = nc.tensor.matmul(pO[:, t % 2, 0:D], h[:, f, t * P:(t + 1) * P], w2[s][:, f, :],
                                                        start=f == 0, stop=f == FC - 1)
                            last.then_inc(o_made, 1)

            @block.scalar
            def _(act):
                act.nop().then_inc(h_left, 4)
                act.wait_ge(b_ok, 32)
                with act.Fori(0, EXPERTS) as e:
                    act.wait_ge(o_made, e * CT + 1)
                    act.wait_ge(h_left, e * FC * 2 + 4)
                    act.nop().then_inc(relay, 1)
                    nc.scalar.activation(b1e[:], b1[:, bass.ds(e, 1), :].rearrange("p a b -> p (a b)"), ACT.Copy).then_inc(b1_ok, 1)
                    act.wait_ge(b1_ok, e + 1)
                    for n in range(FC * 2):
                        act.wait_ge(h_made, e * FC * 2 + n + 2)
                        nc.scalar.activation(h[:, n // 2, (n % 2) * HC:(n % 2 + 1) * HC], pH[:, n % 4, 0:HC], ACT.Relu,
                                             bias=b1e[:, n // 2:n // 2 + 1]).then_inc(h_left, 1)

            @block.vector
            def _(dve):
                dve.nop().then_inc(h_made, 1)
                dve.nop().then_inc(stored, 2)
                dve.nop().then_inc(x_left, 2)
                dve.nop().then_inc(o_left, 2)
                dve.wait_ge(b_ok, 32)
                with dve.Fori(0, EXPERTS // 2) as pair:
                    for s in range(2):
                        e = pair * 2 + s
                        dve.wait_ge(h_made, e * FC * 2 + 1)
                        for t in range(CT):
                            dve.wait_ge(x_turn, e * CT + t + 1)
                            nc.vector.tensor_copy(xT[:, :, t * P:(t + 1) * P],
                                                  pX[:, t % 2, 0:D].rearrange("p (c n) -> p c n", c=DC)).then_inc(x_left, 1)
                        dve.wait_ge(stored, e + 1)
                        for t in range(CT):
                            dve.wait_ge(o_made, e * CT + t + 2)
                            nc.vector.tensor_tensor(eo[s][:, t, :], pO[:, t % 2, 0:D],
                                                    b2[:, bass.ds(e, 1), :].rearrange("p a d -> p (a d)"), ALU.add).then_inc(o_left, 1)

            @block.gpsimd
            def _(pool):
                with pool.Fori(0, EXPERTS // 2) as pair:
                    for s in range(2):
                        e = pair * 2 + s
                        pool.wait_ge(o_left, (e + 1) * CT + 2)
                        pool.dma_start(moe_out[bass.ds(e * CAP, CAP), :].rearrange("(t p) d -> p t d", p=P), eo[s][:]).then_inc(e_out[s], 16)
                        pool.wait_ge(e_out[s], (pair + 1) * 16)
                        pool.nop().then_inc(stored, 1)

        got = [sem(f"me_got{j}") for j in range(BLOCKS)]
        done, stored = sem("me_done"), sem("me_stored")
        rows_out = out.rearrange("b (t p) d -> p (b t) d", p=P)
        y2 = [y[:, :, s, :] for s in range(2)]
        with nc.Block() as block:
            @block.gpsimd
            def _(pool):
                for j in range(BLOCKS):
                    if j >= 2:
                        pool.wait_ge(done, (j - 1) * SUB)
                    for t in range(SUB):
                        at = j * SUB + t
                        pool.indirect_dma_start(y2[j % 2][:, t, :], None, moe_out,
                                                bass.IndirectOffsetOnAxis(ap=gather_at[:, at:at + 1], axis=0)).then_inc(got[j], 16)

            @block.vector
            def _(dve):
                for j in range(BLOCKS):
                    dve.wait_ge(got[j], 16 * SUB)
                    for t in range(SUB):
                        at = j * SUB + t
                        nc.vector.scalar_tensor_tensor(res[:, at, :], y2[j % 2][:, t, :], weight[:, at:at + 1], res[:, at, :],
                                                       ALU.mult, ALU.add).then_inc(done, 1)

            @block.sync
            def _(sp):
                for j in range(BLOCKS):
                    sp.wait_ge(done, (j + 1) * SUB)
                    sp.dma_start(rows_out[:, j * SUB:(j + 1) * SUB, :], res[:, j * SUB:(j + 1) * SUB, :]).then_inc(stored, 16)
                sp.wait_ge(stored, 16 * BLOCKS)


def rows_on_partitions(w, chunks):
    return w.reshape(chunks, P, -1).transpose(1, 0, 2)


def arrays_for(i):
    a = {"x": i["L0_attn_x"]}
    ar = np.arange(P)
    a["c_ident"] = np.eye(P, dtype=np.float32)
    a["gb"] = np.stack([i["L0_attn_ln_gamma"].reshape(DC, P).T, i["L0_attn_ln_beta"].reshape(DC, P).T], 1)
    w_in = i["L0_attn_W_in"]
    a["W_inT"] = rows_on_partitions(w_in.T, DC)
    a["W_inE"] = rows_on_partitions(w_in[:INNER], IC)
    a["W_outT"] = rows_on_partitions(i["L0_attn_W_out"].T, IC)
    a["A"], a["A_T"] = i["L0_attn_A"], i["L0_attn_A"].T
    a["BmT"] = rows_on_partitions(i["L0_attn_Bm"].T, IC)
    a["Cm"] = i["L0_attn_Cm"]
    a["c_own"] = (ar[:, None] // STATE == np.arange(GROUPS)[None]).astype(np.float32)
    starts = np.arange(BLOCKS + 1) % (SEQ // BLK) == 0
    a["c_inner"] = np.tile(1.0 - starts.astype(np.float32), (P, 1))
    a["conv"] = rows_on_partitions(np.concatenate([i["L0_attn_conv_w"][:, 0], i["L0_attn_conv_b"][:, None]], 1), IC)
    a["Wq0"] = rows_on_partitions(i["L0_ffn_Wq"], DC)
    chan = np.stack([np.tile(i["L0_ffn_" + n], 2) for n in ("bn_gamma", "bn_beta")], 1)
    a["pk_vec"] = np.concatenate([i["L0_ffn_bq"].reshape(QCH, P).T, chan], 1)
    a["key0T"], a["key1T"] = i["L0_ffn_sub_key0"].T, i["L0_ffn_sub_key1"].T
    a["downT"] = rows_on_partitions(i["L0_ffn_expert_down"].T, DC)
    a["up"] = rows_on_partitions(i["L0_ffn_expert_up"], DC)
    a["c_heads"] = (ar[:, None] % QD == ar[None] % QD).astype(np.float32) / PK_HEADS
    a["c_halves"] = (ar[:, None] // HALF == np.arange(P // HALF)[None]).astype(np.float32)
    even_odd = np.concatenate([np.arange(0, D, 2), np.arange(1, D, 2)])
    for n in "qk":
        a["W" + n] = rows_on_partitions(i["L1_attn_W" + n][:, even_odd], DC)
        a["b" + n] = i["L1_attn_b" + n][even_odd].reshape(2, P).T
    a["Wv"], a["Wo"] = (rows_on_partitions(i["L1_attn_W" + n], DC) for n in "vo")
    a["bv"], a["bo"] = i["L1_attn_bv"][None], i["L1_attn_bo"][None]
    freq = np.power(10000.0, -2.0 * np.arange(P) / D).astype(np.float32)
    angle = (freq[:, None] * np.arange(SEQ, dtype=np.float32)[None]).astype(np.float64)
    a["c_cos"], a["c_sin"] = np.cos(angle).astype(np.float32), np.sin(angle).astype(np.float32)
    later = np.where(ar[None] > ar[:, None], -1e30, 0.0).astype(np.float32)
    a["c_masks"] = np.stack([later, later.T], 1)
    a["gate"] = rows_on_partitions(i["L1_ffn_gate_w"].T, DC)
    a["gate_b"] = i["L1_ffn_gate_b"][None]
    a["w1"] = i["L1_ffn_w1"].reshape(EXPERTS, DC, P, FF).transpose(2, 0, 1, 3)
    a["b1"] = i["L1_ffn_b1"].reshape(EXPERTS, FC, P).transpose(2, 0, 1)
    a["w2"] = i["L1_ffn_w2"].reshape(EXPERTS, FC, P, D).transpose(2, 0, 1, 3)
    a["b2"] = i["L1_ffn_b2"].reshape(1, EXPERTS * D)
    a["c_before"] = (ar[:, None] <= ar[None]).astype(np.float32)
    a["c_ones"] = np.ones((P, P), np.float32)
    a["c_trash"] = (SLOTS + ar[:, None] + P * np.arange(TILES)[None]).astype(np.float32)
    a["c_expert"] = np.tile(np.arange(EXPERTS, dtype=np.float32), (P, 1))
    return {n: np.ascontiguousarray(x) for n, x in a.items()}


def kernel(**inputs):
    import concourse.bacc as bacc
    from concourse.bass_utils import run_bass_kernel_spmd

    nc = bacc.Bacc("TRN2", target_bir_lowering=False, num_devices=1)
    arrays, aps = {}, {}
    for name, a in arrays_for({n: np.asarray(v) for n, v in inputs.items()}).items():
        arrays["in_" + name] = a
        aps[name] = nc.dram_tensor("in_" + name, a.shape, mybir.dt.from_np(a.dtype), kind="ExternalInput").ap()
    out = nc.dram_tensor("out_0", (BATCH, SEQ, D), F32, kind="ExternalOutput").ap()
    program(nc, aps, out)
    return run_bass_kernel_spmd(nc, [arrays], core_ids=[0]).results[0]["out_0"]
```

```python
from contextlib import ExitStack

import numpy as np

import concourse.bass as bass
from concourse import mybir

F32 = mybir.dt.float32
BF16 = mybir.dt.bfloat16
I32 = mybir.dt.int32
U32 = mybir.dt.uint32
ALU = mybir.AluOpType
ACT = mybir.ActivationFunctionType
AX_X = mybir.AxisListType.X

P = 128
BATCH, SEQ, D = 2, 2048, 256
TOK = BATCH * SEQ
TILES = TOK // P
BLK = 512
BLOCKS = TOK // BLK
SUB = BLK // P
DC = D // P
EPS = 1e-5

INNER, STATE, TAPS = 512, 16, 4
IC = INNER // P
GROUPS = P // STATE

PK_HEADS, QD, NKEY, TOPK_DIM = 8, 64, 32, 4
HALF = QD // 2
SETS = 2 * PK_HEADS
PK_EXP = 256
ROWS_IN = PK_EXP // NKEY
QCH = PK_HEADS * QD // P

HEADS, HD = 16, 16
HPG = 4
HG = HEADS // HPG
QT = SEQ // BLK
KT = SEQ // P
VCOLS = HD + 1
TERMS = 6
MROW = TERMS * HD

EXPERTS, FF, CAP = 8, 1024, 640
CT = CAP // P
FC = FF // P
SLOTS = EXPERTS * CAP

PARTS_Q = (0, 0, 1, 1, 0, 2)
PARTS_K = (0, 1, 0, 1, 2, 0)


def program(nc, inp, out):
    ctx = ExitStack()
    with ctx:
        def sem(name):
            return ctx.enter_context(nc.semaphore(name))

        def keep(name, shape, dt=F32):
            return ctx.enter_context(nc.sbuf_tensor(name, shape, dt))

        res = keep("res", [P, TILES, D])
        ident = keep("ident", [P, P])
        identb = keep("identb", [P, P], BF16)
        rowsT = nc.dram_tensor("split_rows", (2, 3, BATCH * D, SEQ), BF16, kind="Internal").ap()
        v_pad = nc.dram_tensor("v_padded", (BATCH * HG, P, KT, HPG * VCOLS), F32, kind="Internal").ap()
        moe_in = nc.dram_tensor("moe_in", (SLOTS + TOK, D), F32, kind="Internal").ap()
        moe_out = nc.dram_tensor("moe_out", (SLOTS, D), F32, kind="Internal").ap()

        weight = keep("weight", [P, TILES])
        gather_at = keep("gather_at", [P, TILES], I32)
        ahead = ctx.enter_context(ExitStack())
        early = ctx.enter_context(ExitStack())
        weights = Weights(nc, sem, early, inp)
        keys = KeyStats(nc, sem, early)
        with ExitStack() as c0:
            normT = c0.enter_context(nc.sbuf_tensor("normT", [P, DC, TOK], F32))
            with ExitStack() as c1:
                ssmT = c1.enter_context(nc.sbuf_tensor("ssmT", [P, DC, TOK], F32))
                norm_first(nc, sem, inp, res, normT, ssmT, ident, identb, weights)
                ssm(nc, sem, res, normT, ssmT, weights, keys, moe_in)
            product_keys(nc, sem, res, normT, ident, weights, keys)
        early.close()
        rows = ctx.enter_context(nc.sbuf_tensor("rows", [P, TILES, D], F32))
        scatter_at = ctx.enter_context(nc.sbuf_tensor("scatter_at", [P, TILES], I32))
        with ExitStack() as c2:
            logits = c2.enter_context(nc.sbuf_tensor("logits", [P, TILES, EXPERTS], F32))
            places = Places(nc, sem, inp, c2)
            norm_project(nc, sem, inp, res, rows, ident, rowsT, v_pad, logits, places)
            operands = Operands(nc, sem, ahead, rowsT, v_pad)
            route(nc, sem, logits, weight, gather_at, scatter_at, places, operands, identb)
        with ExitStack() as c3:
            wo = c3.enter_context(nc.sbuf_tensor("wo", [P, DC, D], F32))
            attention(nc, sem, inp, res, operands, rows, scatter_at, moe_in, wo, ident, identb)
            ahead.close()
            ctxt = rows[:].rearrange("p t d -> p (t d)").rearrange("p (g t c) -> p g t c", g=BATCH * HG, c=HPG * HD)
            experts = Experts(nc, sem, inp, ahead, moe_in)
            attention_out(nc, sem, res, ctxt, wo, ident, experts)
        moe(nc, sem, res, weight, gather_at, moe_out, ident, out, experts)


class Steps:

    def __init__(self, sem, per_round, i=0):
        self.sem, self.per, self.i, self.n = sem, per_round, i, 0

    def inc(self, instruction):
        instruction.then_inc(self.sem, 1)
        self.n += 1
        assert self.n <= self.per
        return self.n

    def at(self, n):
        return self.i * self.per + n


class Weights:

    def __init__(self, nc, sem, stack, inp):
        def sb(name, shape):
            return stack.enter_context(nc.sbuf_tensor("w_" + name, shape, F32, side="right"))
        self.inp = inp
        self.w_in = sb("w_in", [P, DC, 2 * INNER])
        self.w_ine = sb("w_ine", [P, IC, D])
        self.w_out = sb("w_out", [P, IC, D])
        self.bmT = sb("bmT", [P, IC, STATE])
        self.cm = sb("cm", [P, INNER])
        self.own = sb("own", [P, GROUPS])
        self.inner = sb("inner", [P, BLOCKS + 1])
        self.cw = sb("cw", [P, IC, TAPS + 1])
        self.pw = sb("pw", [P, 2, 2, P + STATE])
        self.wq = sb("wq", [P, DC, PK_HEADS * QD])
        self.vec = sb("vec", [P, QCH + 2])
        self.keys = sb("keys", [P, P])
        self.ones = sb("ones", [P, P])
        self.heads = sb("heads", [P, P])
        self.halves = sb("halves", [P, 32])
        self.down = sb("down", [P, DC, PK_EXP])
        self.upw = sb("upw", [P, DC, PK_EXP])
        self.ok, self.zero = sem("w_ok"), sem("w_zero")

    def clear(self, engine):
        engine.memset(self.pw[:], 0.0).then_inc(self.zero, 1)
        engine.memset(self.keys[:], 0.0).then_inc(self.zero, 1)

    def load(self, sp):
        inp = self.inp
        moves = []
        for g in range(GROUPS):
            at = slice(g * STATE, (g + 1) * STATE)
            moves.append((self.cm[at, :], inp["Cm"]))
            for q in range(2):
                moves.append((self.pw[at, 0, q, STATE + g * STATE:STATE + (g + 1) * STATE], inp["A_T"] if q == 0 else inp["A"]))
        for k in range(P // HALF):
            at = slice(k * HALF, (k + 1) * HALF)
            moves.append((self.keys[at, at], inp[f"key{k % 2}T"]))
        for t, name in ((self.w_in, "W_inT"), (self.w_ine, "W_inE"), (self.w_out, "W_outT"), (self.bmT, "BmT"),
                        (self.cw, "conv"), (self.own, "c_own"), (self.inner, "c_inner"), (self.wq, "Wq0"), (self.vec, "pk_vec"), (self.ones, "c_ones"),
                        (self.heads, "c_heads"), (self.halves, "c_halves"), (self.down, "downT"), (self.upw, "up")):
            moves.append((t[:], inp[name]))
        sp.wait_ge(self.zero, 2)
        for dst, src in moves:
            sp.dma_start(dst, src).then_inc(self.ok, 16)
        self.all = 16 * len(moves)


def norm_first(nc, sem, inp, res, normT, ssmT, ident, identb, weights):
    x = inp["x"].rearrange("b (t p) d -> p (b t) d", p=P)
    with ExitStack() as c:
        def sb(name, shape, dt=F32):
            return c.enter_context(nc.sbuf_tensor("n1_" + name, shape, dt))
        xn = sb("xn", [P, 2, SUB, D])
        x2 = sb("x2", [P, 2, SUB, D])
        stats = sb("stats", [P, SUB, 6])
        mv = sb("mv", [P, 2, SUB, 2])
        inv = sb("inv", [P, SUB])
        std = sb("std", [P, 2, 2, SUB])
        rstd = sb("rstd", [P, 2, 2, SUB])
        gb = sb("gb", [P, 2, DC])
        ps = c.enter_context(nc.psum_tensor("n1_ps", [P, 2, 2 * DC, BLK], F32))
        const_in = sem("n1_const_in")
        x_in = [sem(f"n1_x_in{h}") for h in range(2)]
        (step, std_ok, inv_ok, xn_ok, x2_ok, res_ok, turned1, turned2, out1, out2, relay) = (sem("n1_" + n) for n in (
            "step", "std_ok", "inv_ok", "xn_ok", "x2_ok", "res_ok", "turned1", "turned2", "out1", "out2", "relay"))
        PER = 2 * SUB + 4
        with nc.Block() as block:
            @block.sync
            def _(sp):
                for h in range(2):
                    sp.dma_start(res[:, h * SUB:(h + 1) * SUB, :], x[:, h * SUB:(h + 1) * SUB, :]).then_inc(x_in[h], 16)
                for t, src in ((ident, inp["c_ident"]), (gb, inp["gb"])):
                    sp.dma_start(t[:], src).then_inc(const_in, 16)
                with sp.Fori(1, BLOCKS // 2) as jj:
                    for h in range(2):
                        sp.wait_ge(x_in[h], jj * 16)
                        at = bass.ds((jj * 2 + h) * SUB, SUB)
                        sp.dma_start(res[:, at, :], x[:, at, :]).then_inc(x_in[h], 16)
                weights.load(sp)

            @block.gpsimd
            def _(pool):
                weights.clear(nc.gpsimd)
                with pool.Fori(0, BLOCKS // 2) as jj:
                    for h in range(2):
                        j = jj * 2 + h
                        pool.wait_ge(xn_ok, j * SUB + SUB)
                        at = bass.ds(j * SUB, SUB)
                        nc.gpsimd.tensor_tensor(res[:, at, :], res[:, at, :], xn[:, h], ALU.add).then_inc(res_ok, 1)

            @block.vector
            def _(dve):
                dve.nop().then_inc(turned1, 2)
                dve.nop().then_inc(turned2, 2)
                dve.nop().then_inc(res_ok, 2)
                dve.nop().then_inc(x2_ok, 1)

                def statistics(j, h, jj):
                    st = Steps(step, PER, j)

                    def then(ins):
                        dve.wait_ge(step, st.at(st.inc(ins)))

                    dve.wait_ge(x_in[h], jj * 16 + 16)
                    if not isinstance(j, int) or j > 0:
                        dve.wait_ge(x2_ok, (j - 1) * SUB + 1)
                    for s in range(SUB):
                        st.inc(nc.vector.bn_stats(stats[:, s, :], res[:, bass.ds(j * SUB + s, 1), :].rearrange("p a n -> p (a n)")))
                    dve.wait_ge(step, st.at(st.n))
                    dve.nop().then_inc(relay, 1)
                    for s in range(SUB):
                        st.inc(nc.vector.bn_aggr(mv[:, h, s, :], stats[:, s, :]))
                    dve.wait_ge(step, st.at(st.n))
                    then(nc.vector.tensor_scalar(std[:, h, 0, :], mv[:, h, :, 1], EPS, None, ALU.add))
                    then(nc.vector.reciprocal(inv[:], std[:, h, 0, :]))
                    then(nc.vector.tensor_tensor(std[:, h, 1, :], mv[:, h, :, 1], inv[:], ALU.mult))
                    st.inc(nc.vector.tensor_scalar(std[:, h, 1, :], std[:, h, 1, :], EPS, None, ALU.add))
                    assert st.n == PER

                def normalise(j, h):
                    dve.wait_ge(std_ok, j + 1)
                    nc.vector.reciprocal(rstd[:, h], std[:, h]).then_inc(inv_ok, 1)
                    dve.wait_ge(turned1, j + 1)
                    dve.wait_ge(res_ok, j + 1)
                    dve.wait_ge(inv_ok, j + 1)
                    for s in range(SUB):
                        row = res[:, bass.ds(j * SUB + s, 1), :].rearrange("p a n -> p (a n)")
                        nc.vector.tensor_scalar(xn[:, h, s, :], row, mv[:, h, s, 0:1], rstd[:, h, 0, s:s + 1],
                                                ALU.subtract, ALU.mult).then_inc(xn_ok, 1)
                    dve.wait_ge(turned2, j + 1)
                    for s in range(SUB):
                        dve.wait_ge(xn_ok, j * SUB + s + 1)
                        nc.vector.tensor_scalar(x2[:, h, s, :], xn[:, h, s, :], rstd[:, h, 1, s:s + 1], None,
                                                ALU.mult).then_inc(x2_ok, 1)

                def two_blocks(jj, final):
                    for h in range(2):
                        j = jj * 2 + h
                        if not (final and h):
                            statistics(j + 1, 1 - h, jj + h)
                        normalise(j, h)

                statistics(0, 0, 0)
                with dve.Fori(0, BLOCKS // 2 - 1) as jj:
                    two_blocks(jj, False)
                two_blocks(BLOCKS // 2 - 1, True)

            @block.tensor
            def _(pe):
                pe.wait_ge(const_in, 32)
                pe.nop().then_inc(out1, 2)
                pe.nop().then_inc(out2, 3)
                with pe.Fori(0, BLOCKS // 2) as jj:
                    for h in range(2):
                        j = jj * 2 + h
                        pe.wait_ge(xn_ok, j * SUB + SUB)
                        pe.wait_ge(out1, j + 1)
                        for d in range(DC):
                            for s in range(SUB):
                                last = nc.tensor.transpose(ps[:, h, d, s * P:(s + 1) * P], xn[:, h, s, d * P:(d + 1) * P], ident[:])
                        last.then_inc(turned1, 1)
                        pe.wait_ge(x2_ok, j * SUB + SUB + 1)
                        pe.wait_ge(out2, j * DC + 1)
                        for d in range(DC):
                            for s in range(SUB):
                                last = nc.tensor.transpose(ps[:, h, DC + d, s * P:(s + 1) * P], x2[:, h, s, d * P:(d + 1) * P], ident[:])
                        last.then_inc(turned2, 1)

            @block.scalar
            def _(act):
                act.wait_ge(const_in, 32)
                nc.scalar.activation(identb[:], ident[:], ACT.Copy)

                def root(j, h):
                    act.wait_ge(step, j * PER + PER)
                    nc.scalar.activation(std[:, h], std[:, h], ACT.Sqrt).then_inc(std_ok, 1)

                def two_blocks(jj, final):
                    for h in range(2):
                        j = jj * 2 + h
                        if not (final and h):
                            root(j + 1, 1 - h)
                        act.wait_ge(turned1, j + 3)
                        nc.scalar.activation(normT[:, :, bass.ds(j * BLK, BLK)], ps[:, h, 0:DC], ACT.Copy).then_inc(out1, 1)
                        act.wait_ge(turned2, j + 3)
                        for d in range(DC):
                            nc.scalar.activation(ssmT[:, d, bass.ds(j * BLK, BLK)], ps[:, h, DC + d, :], ACT.Identity,
                                                 scale=gb[:, 0, d:d + 1], bias=gb[:, 1, d:d + 1]).then_inc(out2, 1)

                root(0, 0)
                with act.Fori(0, BLOCKS // 2 - 1) as jj:
                    two_blocks(jj, False)
                two_blocks(BLOCKS // 2 - 1, True)


class KeyStats:

    def __init__(self, nc, sem, stack):
        def sb(name, shape):
            return stack.enter_context(nc.sbuf_tensor("ks_" + name, shape, F32, side="right"))
        self.nc = nc
        self.keysq = sb("keysq", [P, P])
        self.knorm = sb("knorm", [P, P])
        self.stats = sb("stats", [P, QCH, BLOCKS, 6])
        self.mv = sb("mv", [P, QCH, 2])
        self.sq = sb("sq", [P, QCH])
        self.mom = sb("mom", [P, 4])
        self.gain = sb("gain", [P, 1])
        self.shift = sb("shift", [P, QCH + 1])
        self.made, self.stat, self.kn1, self.kn2, self.prods, self.moment, self.vstep, self.vstd = (
            sem("ks_" + n) for n in ("made", "stat", "kn1", "kn2", "prods", "moment", "vstep", "vstd"))

    def moments_pe(self, pe, weights, bank):
        nc = self.nc
        pe.wait_ge(self.kn1, 1)
        nc.tensor.matmul(bank[:, 0:P], weights.ones[:], self.keysq[:], start=True, stop=True).then_inc(self.prods, 1)
        pe.wait_ge(self.moment, 4)
        pe.wait_ge(self.kn2, 1)
        for m in range(QCH):
            last = nc.tensor.matmul(bank[:, P:P + 2], weights.heads[:], self.mv[:, m, :], start=m == 0, stop=m == QCH - 1)
        last.then_inc(self.prods, 1)

    def act(self, act, weights, bank):
        nc = self.nc
        act.wait_ge(weights.ok, weights.all)
        nc.scalar.activation(self.keysq[:], weights.keys[:], ACT.Square).then_inc(self.kn1, 1)
        act.wait_ge(self.prods, 1)
        nc.scalar.activation(self.knorm[:], bank[:, 0:P], ACT.Sqrt).then_inc(self.kn2, 1)
        act.wait_ge(self.vstep, 6)
        nc.scalar.activation(self.mom[:, 3:4], self.mom[:, 2:3], ACT.Sqrt).then_inc(self.vstd, 1)

    def dve(self, dve, weights, bank):
        nc, knorm, keys, stats, mv, sq, mom = self.nc, self.knorm, weights.keys, self.stats, self.mv, self.sq, self.mom
        vec, moment, vstep = weights.vec, self.moment, self.vstep
        dve.wait_ge(self.stat, BLOCKS * QCH)
        for m in range(QCH):
            nc.vector.bn_aggr(mv[:, m, :], stats[:, m, :, :].rearrange("p a n -> p (a n)")).then_inc(self.stat, 1)
        dve.wait_ge(self.stat, BLOCKS * QCH + QCH)
        nc.vector.tensor_tensor(mv[:, :, 0], mv[:, :, 0], vec[:, 0:QCH], ALU.add).then_inc(moment, 1)
        dve.wait_ge(moment, 1)
        nc.vector.tensor_tensor(sq[:], mv[:, :, 0], mv[:, :, 0], ALU.mult).then_inc(moment, 1)
        dve.wait_ge(moment, 2)
        nc.vector.tensor_tensor(mv[:, :, 1], mv[:, :, 1], sq[:], ALU.add).then_inc(moment, 1)
        dve.wait_ge(moment, 3)
        dve.nop().then_inc(moment, 1)
        dve.wait_ge(self.kn2, 1)
        nc.vector.tensor_scalar(knorm[:], knorm[:], 1e-12, None, ALU.max).then_inc(vstep, 1)
        dve.wait_ge(vstep, 1)
        nc.vector.reciprocal(knorm[:], knorm[:]).then_inc(vstep, 1)
        dve.wait_ge(vstep, 2)
        nc.vector.tensor_tensor(keys[:], keys[:], knorm[:], ALU.mult).then_inc(vstep, 1)
        dve.wait_ge(self.prods, 2)
        nc.vector.tensor_copy(mom[:, 0:2], bank[:, P:P + 2]).then_inc(vstep, 1)
        dve.wait_ge(vstep, 4)
        nc.vector.scalar_tensor_tensor(mom[:, 2:3], mom[:, 0:1], mom[:, 0:1], mom[:, 1:2], ALU.mult,
                                       ALU.subtract).then_inc(vstep, 1)
        dve.wait_ge(vstep, 5)
        nc.vector.tensor_scalar(mom[:, 2:3], mom[:, 2:3], -1.0, EPS, ALU.mult, ALU.add).then_inc(vstep, 1)
        dve.wait_ge(self.vstd, 1)
        nc.vector.reciprocal(mom[:, 3:4], mom[:, 3:4]).then_inc(vstep, 1)
        dve.wait_ge(vstep, 7)
        nc.vector.tensor_tensor(self.gain[:], mom[:, 3:4], vec[:, QCH:QCH + 1], ALU.mult).then_inc(vstep, 1)
        dve.wait_ge(vstep, 8)
        nc.vector.tensor_tensor(mom[:, 1:2], mom[:, 0:1], self.gain[:], ALU.mult).then_inc(vstep, 1)
        dve.wait_ge(vstep, 9)
        nc.vector.tensor_tensor(self.shift[:, QCH:], vec[:, QCH + 1:QCH + 2], mom[:, 1:2], ALU.subtract).then_inc(vstep, 1)
        dve.wait_ge(vstep, 10)
        nc.vector.tensor_scalar(self.shift[:, 0:QCH], vec[:, 0:QCH], self.gain[:], self.shift[:, QCH:],
                                ALU.mult, ALU.add).then_inc(vstep, 1)


def ssm(nc, sem, res, normT, ssmT, weights, keys, moe_in):
    w_in, w_ine, w_out, bmT = weights.w_in, weights.w_ine, weights.w_out, weights.bmT
    cm, own, cw, pw, inner = weights.cm, weights.own, weights.cw, weights.pw, weights.inner
    with ExitStack() as c:
        def sb(name, shape, dt=F32):
            return c.enter_context(nc.sbuf_tensor("ss_" + name, shape, dt))
        stj = sb("stj", [P, BLK])
        vw = sb("vw", [P, DC, 3 * STATE])
        zeros = sb("zeros", [P, 2 * D])
        sh = sb("sh", [P, 2, P])
        st = sb("st", [P, BLK])
        halo = TAPS - 1
        u = sb("u", [P, IC, halo + BLK])
        sz = sb("sz", [P, IC, BLK])
        cv = sb("cv", [P, IC, BLK])
        sg = sb("sg", [P, IC, BLK])
        y = sb("y", [P, IC, BLK])
        pU = c.enter_context(nc.psum_tensor("ss_pU", [P, 2, BLK], F32))
        pZ = c.enter_context(nc.psum_tensor("ss_pZ", [P, 2, BLK], F32))
        pB = c.enter_context(nc.psum_tensor("ss_pB", [P, 2, BLK], F32))
        pC = c.enter_context(nc.psum_tensor("ss_pC", [P, 2, BLK], F32))
        vw_zero, zero_ok, zeroed = sem("ss_vw_zero"), sem("ss_zero_ok"), sem("ss_zeroed")
        fold, folded, scanp, scanv = sem("ss_fold"), sem("ss_folded"), sem("ss_scanp"), sem("ss_scanv")
        powp, powv, shv, sh_zero = sem("ss_powp"), sem("ss_powv"), sem("ss_shv"), sem("ss_sh_zero")
        STEPS = (BLK - 1).bit_length()
        LEVELS = STEPS + (SEQ // BLK - 1).bit_length()
        CHUNKS = BLOCKS * QCH
        banks = [pU[:, 0, :], pU[:, 1, :], pZ[:, 0, :], pZ[:, 1, :]]

        def chunks_of(k):
            return range(k * CHUNKS // LEVELS, (k + 1) * CHUNKS // LEVELS)

        with nc.Block() as block:
            @block.sync
            def _(sp):
                sp.wait_ge(zero_ok, 1)
                n = SLOTS // (2 * P)
                for k in range(n):
                    sp.dma_start(moe_in[k * 2 * P:(k + 1) * 2 * P, :].rearrange("(p a) d -> p (a d)", p=P),
                                 zeros[:]).then_inc(zeroed, 16)
                sp.wait_ge(zeroed, 16 * n)

            @block.gpsimd
            def _(pool):
                nc.gpsimd.memset(vw[:], 0.0).then_inc(vw_zero, 1)
                nc.gpsimd.memset(zeros[:], 0.0).then_inc(zero_ok, 1)

            @block.tensor
            def _(pe):
                pe.wait_ge(weights.ok, weights.all)
                for d in range(DC):
                    for k in range(IC):
                        last = nc.tensor.matmul(pC[:, d, 0:STATE], w_ine[:, k, d * P:(d + 1) * P], bmT[:, k, :],
                                                start=k == 0, stop=k == IC - 1)
                last.then_inc(fold, 1)
                pe.wait_ge(folded, DC)
                for odd in range(2):
                    for d in range(DC):
                        for quarter in range(4):
                            j = quarter * 2 + odd
                            last = nc.tensor.matmul(pB[32 * quarter:32 * (quarter + 1), 0, :],
                                                    vw[:, d, STATE * (1 - odd):STATE * (1 - odd) + 32], ssmT[:, d, j * BLK:(j + 1) * BLK],
                                                    start=odd == 0 and d == 0, stop=odd == 1 and d == DC - 1,
                                                    tile_position=(0, 32 * quarter))
                last.then_inc(scanp, 1)
                for k in range(LEVELS):
                    cur = k % 2
                    pe.wait_ge(shv, k + 1)
                    pe.wait_ge(scanv, k + 1)
                    if k < STEPS:
                        n = 1 << k
                        nc.tensor.matmul(pB[:, 1, n:BLK], pw[:, cur, 0, STATE:], st[:, 0:BLK - n], start=True, stop=True)
                        last = nc.tensor.matmul(pB[:, 1, 0:n], sh[:, cur, :], st[:, BLK - n:BLK], start=True, stop=True)
                    else:
                        last = nc.tensor.matmul(pB[:, 1, :], sh[:, cur, :], st[:], start=True, stop=True)
                    last.then_inc(scanp, 1)
                    if k < LEVELS - 1:
                        nc.tensor.matmul(pC[:, 0, 0:P], pw[:, cur, 1, STATE:], pw[:, cur, 0, STATE:], start=True, stop=True)
                        nc.tensor.matmul(pC[:, 0, P:2 * P], pw[:, cur, 0, STATE:], pw[:, cur, 1, STATE:],
                                         start=True, stop=True).then_inc(powp, 1)
                    for x in chunks_of(k):
                        j, m = x // QCH, x % QCH
                        if x >= QCH:
                            pe.wait_ge(keys.stat, x - QCH + 1)
                        for d in range(DC):
                            last = nc.tensor.matmul(banks[m], weights.wq[:, d, m * P:(m + 1) * P], normT[:, d, j * BLK:(j + 1) * BLK],
                                                    start=d == 0, stop=d == DC - 1)
                        last.then_inc(keys.made, 1)
                keys.moments_pe(pe, weights, pC[:, 1, :])

            @block.scalar
            def _(act):
                keys.act(act, weights, pC[:, 1, :])

            @block.vector
            def _(dve):
                dve.wait_ge(fold, 1)
                dve.wait_ge(vw_zero, 1)
                for d in range(DC):
                    nc.vector.tensor_copy(vw[:, d, STATE:2 * STATE], pC[:, d, 0:STATE]).then_inc(folded, 1)
                dve.wait_ge(scanp, 1)
                nc.vector.tensor_copy(st[:], pB[:, 0, :]).then_inc(scanv, 1)

                def statistics(k):
                    for x in chunks_of(k):
                        dve.wait_ge(keys.made, x + 1)
                        nc.vector.bn_stats(keys.stats[:, x % QCH, x // QCH, :], banks[x % QCH]).then_inc(keys.stat, 1)

                per = SEQ // BLK * STATE
                dve.wait_ge(weights.ok, weights.all)
                for k in range(LEVELS):
                    cur = k % 2
                    if k:
                        dve.wait_ge(powp, k)
                        dve.wait_ge(scanp, k + 1)
                        for q in range(2):
                            nc.vector.tensor_copy(pw[:, cur, q, STATE:], pC[:, 0, q * P:(q + 1) * P]).then_inc(powv, 1)
                        dve.wait_ge(powv, 2 * k)
                    far = max(0, k - STEPS)
                    w = STATE << far
                    nc.vector.memset(sh[:, cur, :], 0.0).then_inc(sh_zero, 1)
                    dve.wait_ge(sh_zero, 1 + k)
                    for b in range(BATCH):
                        last = nc.vector.tensor_copy(sh[:, cur, b * per + w:(b + 1) * per],
                                                     pw[:, cur, 0, STATE + b * per:STATE + (b + 1) * per - w])
                    last.then_inc(shv, 1)
                    if k:
                        statistics(k - 1)
                    dve.wait_ge(scanp, k + 2)
                    dve.wait_ge(scanv, k + 1)
                    nc.vector.tensor_tensor(st[:], st[:], pB[:, 1, :], ALU.add).then_inc(scanv, 1)
                statistics(LEVELS - 1)
                keys.dve(dve, weights, pC[:, 1, :])

        u_made, u_left, z_made, z_left = sem("mx_u_made"), sem("mx_u_left"), sem("mx_z_made"), sem("mx_z_left")
        c_made, c_left, o_made, o_left = sem("mx_c_made"), sem("mx_c_left"), sem("mx_o_made"), sem("mx_o_left")
        own_ok = sem("mx_own_ok")
        halo_ok, conv_ok, gate_ok, silu_ok, y_ok = (sem("mx_" + n) for n in ("halo_ok", "conv_ok", "gate_ok", "silu_ok", "y_ok"))
        with nc.Block() as block:
            @block.tensor
            def _(pe):
                def enter(j):
                    cols = bass.ds(j * BLK, BLK)
                    for m in range(IC):
                        pe.wait_ge(u_left, j * IC + m + 1)
                        for d in range(DC):
                            last = nc.tensor.matmul(pU[:, m % 2, :], w_in[:, d, m * P:(m + 1) * P], ssmT[:, d, cols],
                                                    start=d == 0, stop=d == DC - 1)
                        last.then_inc(u_made, 1)
                        pe.wait_ge(z_left, j * IC + m + 1)
                        for d in range(DC):
                            last = nc.tensor.matmul(pZ[:, m % 2, :], w_in[:, d, INNER + m * P:INNER + (m + 1) * P],
                                                    ssmT[:, d, cols], start=d == 0, stop=d == DC - 1)
                        last.then_inc(z_made, 1)

                def finish(j, more):
                    pe.wait_ge(own_ok, j + 1)
                    for m in range(IC):
                        pe.wait_ge(c_left, j * IC + m + 1)
                        nc.tensor.matmul(pB[:, m % 2, :], cm[:, m * P:(m + 1) * P], stj[:], start=True, stop=True).then_inc(c_made, 1)
                    if more:
                        enter(j + 1)
                    pe.wait_ge(y_ok, j * IC + 2 * IC)
                    for s in range(SUB):
                        pe.wait_ge(o_left, j * SUB + s + 1)
                        for k in range(IC):
                            last = nc.tensor.matmul(pC[:, s % 2, 0:D], y[:, k, s * P:(s + 1) * P], w_out[:, k, :],
                                                    start=k == 0, stop=k == IC - 1)
                        last.then_inc(o_made, 1)

                enter(0)
                with pe.Fori(0, BLOCKS - 1) as j:
                    finish(j, True)
                finish(BLOCKS - 1, False)

            @block.scalar
            def _(act):
                act.nop().then_inc(c_made, 1)
                act.nop().then_inc(y_ok, IC)
                act.nop().then_inc(u_left, 2)
                act.nop().then_inc(z_left, 2)

                def enter(j):
                    act.wait_ge(c_made, j * IC + 1)
                    nc.scalar.activation(stj[:], st[:], ACT.Copy, scale=own[:, bass.ds(j, 1)]).then_inc(own_ok, 1)
                    for m in range(IC):
                        act.wait_ge(u_made, j * IC + m + 1)
                        act.wait_ge(halo_ok, j * IC + m + 1)
                        nc.scalar.activation(u[:, m, halo:], pU[:, m % 2, :], ACT.Copy).then_inc(u_left, 1)
                        act.wait_ge(z_made, j * IC + m + 1)
                        act.wait_ge(y_ok, j * IC + m + 1)
                        nc.scalar.activation(sz[:, m, :], pZ[:, m % 2, :], ACT.Sigmoid).then_inc(z_left, 1)
                    for m in range(IC):
                        act.wait_ge(conv_ok, (j * IC + m) * TAPS + TAPS)
                        nc.scalar.activation(sg[:, m, :], cv[:, m, :], ACT.Sigmoid).then_inc(gate_ok, 1)

                with act.Fori(0, BLOCKS) as j:
                    enter(j)

            @block.vector
            def _(dve):
                dve.nop().then_inc(o_made, 1)
                dve.nop().then_inc(c_left, 2)
                dve.nop().then_inc(o_left, 2)

                def silu_conv(j, more):
                    for m in range(IC):
                        dve.wait_ge(u_left, j * IC + m + 3)
                        n = (j * IC + m) * TAPS
                        nc.vector.tensor_scalar(cv[:, m, :], u[:, m, halo:], cw[:, m, TAPS - 1:TAPS], cw[:, m, TAPS:],
                                                ALU.mult, ALU.add).then_inc(conv_ok, 1)
                        for k in range(TAPS - 1):
                            dve.wait_ge(conv_ok, n + k + 1)
                            nc.vector.scalar_tensor_tensor(cv[:, m, :], u[:, m, k:k + BLK], cw[:, m, k:k + 1], cv[:, m, :],
                                                           ALU.mult, ALU.add).then_inc(conv_ok, 1)
                        if more:
                            dve.wait_ge(conv_ok, n + TAPS)
                            nc.vector.tensor_scalar(u[:, m, 0:halo], u[:, m, BLK:], inner[:, bass.ds(j + 1, 1)], None,
                                                    ALU.mult).then_inc(halo_ok, 1)
                    for m in range(IC):
                        dve.wait_ge(gate_ok, j * IC + m + 1)
                        nc.vector.tensor_tensor(cv[:, m, :], cv[:, m, :], sg[:, m, :], ALU.mult).then_inc(silu_ok, 1)

                def finish(j, more):
                    for m in range(IC):
                        dve.wait_ge(silu_ok, j * IC + m + 1)
                        dve.wait_ge(c_made, j * IC + m + 2)
                        nc.vector.tensor_tensor(sg[:, m, :], cv[:, m, :], pB[:, m % 2, :], ALU.add).then_inc(c_left, 1)
                    dve.wait_ge(z_left, j * IC + IC + 2)
                    dve.wait_ge(o_made, j * SUB + 1)
                    for m in range(IC):
                        dve.wait_ge(c_left, j * IC + m + 3)
                        nc.vector.tensor_tensor(y[:, m, :], sg[:, m, :], sz[:, m, :], ALU.mult).then_inc(y_ok, 1)
                    if more:
                        silu_conv(j + 1, more)
                    for s in range(SUB):
                        dve.wait_ge(o_made, j * SUB + s + 2)
                        row = res[:, bass.ds(j * SUB + s, 1), :].rearrange("p a n -> p (a n)")
                        nc.vector.tensor_tensor(row, row, pC[:, s % 2, 0:D], ALU.add).then_inc(o_left, 1)

                for m in range(IC):
                    nc.vector.memset(u[:, m, 0:halo], 0.0).then_inc(halo_ok, 1)
                silu_conv(0, True)
                with dve.Fori(0, BLOCKS - 1) as j:
                    finish(j, True)
                finish(BLOCKS - 1, False)


def product_keys(nc, sem, res, normT, ident, weights, stats):
    SCORES = SETS * NKEY
    PAIRS = TILES // 2
    PIECES = QCH + DC
    with ExitStack() as c:
        def sb(name, shape, dt=F32):
            return c.enter_context(nc.sbuf_tensor("pk_" + name, shape, dt))
        qn = sb("qn", [P, 2, QCH, BLK])
        qs = sb("qs", [P, QCH, BLK])
        nrm = sb("nrm", [P, BLK])
        inv = sb("inv", [P, 2, SUB * SETS])
        s_ = sb("s", [P, 2, 2, SCORES])
        ex = sb("ex", [P, 2, 2, SCORES])
        rep = sb("rep", [P, 2, SCORES])
        top = sb("top", [P, 2 * SETS, 8])
        z = sb("z", [P, 2 * SETS])
        far = sb("far", [P, 2, PK_HEADS])
        both = sb("both", [P, 2, PK_HEADS])
        share = sb("share", [P, 2, PK_HEADS])
        a0 = sb("a0", [P, 2, 2, PK_HEADS, ROWS_IN])
        last_w = sb("last_w", [P, 2, 1])
        prod = sb("prod", [P, 2, PK_HEADS, PK_EXP])
        wt = sb("wt", [P, 2, PK_EXP])
        g = sb("g", [P, 2, DC, BLK])
        gw = sb("gw", [P, DC, 2 * P])
        pQ = c.enter_context(nc.psum_tensor("pk_pQ", [P, 2, BLK], F32))
        pN = c.enter_context(nc.psum_tensor("pk_pN", [P, BLK], F32))
        pI = c.enter_context(nc.psum_tensor("pk_pI", [P, BLK], F32))
        pS = c.enter_context(nc.psum_tensor("pk_pS", [P, 2, BLK], F32))
        pT = c.enter_context(nc.psum_tensor("pk_pT", [P, BLK], F32))
        pO = c.enter_context(nc.psum_tensor("pk_pO", [P, BLK], F32))
        turned = pT[:].rearrange("p (e t) -> p e t", e=DC)
        names = ("relay", "piece", "piece_out", "sq_ok", "n2_ok", "root_ok", "norm_turned", "inv_ok", "sc_ok", "s_ok", "ex_ok", "search",
                 "a0_ok", "multiplied", "prod_ok", "summed", "wt_ok", "turn_ok", "gw_ok", "o_ok", "o_left")
        (relay, piece, piece_out, sq_ok, n2_ok, root_ok, norm_turned, inv_ok, sc_ok, s_ok, ex_ok, search,
         a0_ok, multiplied, prod_ok, summed, wt_ok, turn_ok, gw_ok, o_ok, o_left) = (sem("pk_" + n) for n in names)

        def rounds(engine, step, first=0):
            for i in range(4 * first):
                step(i, 0, i, False)
            with engine.Fori(first, PAIRS // 4 - 1) as jj:
                for i in range(4):
                    step(jj * 4 + i, jj * 2, i, False)
            for i in range(4):
                step(PAIRS - 4 + i, BLOCKS - 2, i, True)

        with nc.Block() as block:
            @block.tensor
            def _(pe):
                pe.nop().then_inc(piece_out, 2)
                pe.nop().then_inc(root_ok, 1)
                pe.nop().then_inc(inv_ok, 1)
                pe.nop().then_inc(s_ok, 1)
                pe.nop().then_inc(gw_ok, 1)
                pe.nop().then_inc(o_left, 1)

                def pieces(b, which):
                    for x in which:
                        w, at = (weights.wq, x) if x < QCH else (weights.down, x - QCH)
                        pe.wait_ge(piece_out, b * PIECES + x + 1)
                        for d in range(DC):
                            last = nc.tensor.matmul(pQ[:, x % 2, :], w[:, d, at * P:(at + 1) * P], normT[:, d, bass.ds(b * BLK, BLK)],
                                                    start=d == 0, stop=d == DC - 1)
                        last.then_inc(piece, 1)

                def norms(b):
                    pe.wait_ge(sq_ok, b + 1)
                    pe.wait_ge(root_ok, b + 1)
                    for m in range(QCH):
                        last = nc.tensor.matmul(pN[32 * m:32 * (m + 1), :], weights.halves[:], qs[:, m, :], start=True, stop=True,
                                                tile_position=(0, 32 * m))
                    last.then_inc(n2_ok, 1)

                def turn_norms(b):
                    pe.wait_ge(root_ok, b + 2)
                    pe.wait_ge(inv_ok, b * 2 + 1)
                    for t in range(SUB):
                        last = nc.tensor.transpose(pI[:, t * P:(t + 1) * P], nrm[:, t * P:(t + 1) * P], ident[:])
                    last.then_inc(norm_turned, 1)

                def scores(k, b, h, p):
                    pe.wait_ge(piece_out, b * PIECES + QCH + 2)
                    pe.wait_ge(s_ok, k + 1)
                    for t in range(2):
                        for m in range(QCH):
                            last = nc.tensor.matmul(pS[:, t, m * P:(m + 1) * P], qn[:, h, m, (p * 2 + t) * P:(p * 2 + t + 1) * P],
                                                    weights.keys[:], start=True, stop=True)
                    last.then_inc(sc_ok, 1)

                def step(n, b, i, final):
                    if i % 2 and not final:
                        norms(b + 2 + i // 2)
                    if i % 2 == 0 and not final:
                        pieces(b + 2 + i // 2, range(QCH))
                    if not (final and i >= 1):
                        scores(n + 3, b + (i + 3) // 2, (i + 3) // 2 % 2, (i + 3) % 2)
                    pe.wait_ge(wt_ok, n + 1)
                    pe.wait_ge(gw_ok, n + 1)
                    for t in range(2):
                        for e in range(DC):
                            last = nc.tensor.transpose(turned[:, e, t * P:(t + 1) * P], wt[:, t, e * P:(e + 1) * P], ident[:])
                    last.then_inc(turn_ok, 1)
                    if i % 2 and not final:
                        turn_norms(b + 2 + i // 2)
                    pe.wait_ge(gw_ok, n + 2)
                    pe.wait_ge(o_left, n + 1)
                    for t in range(2):
                        for e in range(DC):
                            last = nc.tensor.matmul(pO[:, t * D:(t + 1) * D], gw[:, e, t * P:(t + 1) * P], weights.upw[:, e, :],
                                                    start=e == 0, stop=e == DC - 1)
                    last.then_inc(o_ok, 1)
                    if i % 2 == 0 and not final:
                        pieces(b + 2 + i // 2, range(QCH, PIECES))

                for b in range(2):
                    pieces(b, range(QCH))
                    norms(b)
                    turn_norms(b)
                    if b == 0:
                        for k in range(2):
                            scores(k, 0, 0, k)
                    else:
                        scores(2, 1, 1, 0)
                    pieces(b, range(QCH, PIECES))
                rounds(pe, step)

            @block.scalar
            def _(act):
                def queries(b, h):
                    if not isinstance(b, int) or b > 1:
                        act.wait_ge(sc_ok, b * 2 - 2)
                    for m in range(QCH):
                        act.wait_ge(piece, b * PIECES + m + 1)
                        nc.scalar.activation(qn[:, h, m, :], pQ[:, m % 2, :], ACT.Identity, scale=stats.gain[:],
                                             bias=stats.shift[:, m:m + 1]).then_inc(piece_out, 1)
                    act.wait_ge(piece_out, b * PIECES + QCH + 2)
                    if not isinstance(b, int) or b > 0:
                        act.wait_ge(n2_ok, b)
                    nc.scalar.activation(qs[:], qn[:, h], ACT.Square).then_inc(sq_ok, 1)

                def roots(b):
                    act.wait_ge(n2_ok, b + 1)
                    if not isinstance(b, int) or b > 0:
                        act.wait_ge(norm_turned, b)
                    nc.scalar.activation(nrm[:], pN[:], ACT.Sqrt).then_inc(root_ok, 1)

                def gates(b, h):
                    if not isinstance(b, int) or b > 1:
                        act.wait_ge(gw_ok, b * 2 - 1)
                    for e in range(DC):
                        act.wait_ge(piece, b * PIECES + QCH + e + 1)
                        nc.scalar.activation(g[:, h, e, :], pQ[:, (QCH + e) % 2, :], ACT.Gelu).then_inc(piece_out, 1)

                def exps(k, slot):
                    act.wait_ge(s_ok, k + 2)
                    if not isinstance(k, int) or k > 1:
                        act.wait_ge(prod_ok, k * 2 - 2)
                    nc.scalar.activation(ex[:, slot], s_[:, slot], ACT.Exp).then_inc(ex_ok, 1)

                def step(n, b, i, final):
                    if i % 2 == 0 and not final:
                        queries(b + 2 + i // 2, i // 2)
                    if not (final and i >= 2):
                        exps(n + 2, i % 2)
                    if i % 2 and not final:
                        roots(b + 2 + i // 2)
                        gates(b + 2 + i // 2, i // 2)

                for b in range(2):
                    queries(b, b)
                    roots(b)
                    if b == 0:
                        exps(0, 0)
                    gates(b, b)
                    if b == 0:
                        exps(1, 1)
                rounds(act, step)

            @block.gpsimd
            def _(pool):
                with pool.Fori(0, PAIRS // 2) as kk:
                    for slot in range(2):
                        k = kk * 2 + slot
                        pool.wait_ge(a0_ok, k + 1)
                        for t in range(2):
                            pool.wait_ge(summed, k * 2 + t + 1)
                            first = a0[:, slot, t].unsqueeze(3)
                            second = ex[:, slot, t].rearrange("p (h f b) -> p h f b", h=PK_HEADS, f=2)[:, :, 1:2, :]
                            shape = (P, PK_HEADS, ROWS_IN, NKEY)
                            nc.gpsimd.tensor_tensor(prod[:, t].rearrange("p h (a b) -> p h a b", a=ROWS_IN),
                                                    first.broadcast_to(shape), second.broadcast_to(shape), ALU.mult).then_inc(multiplied, 1)
                            pool.wait_ge(multiplied, (k * 2 + t) * 2 + 1)
                            nc.gpsimd.tensor_tensor(prod[:, t, 0:PK_HEADS // 2], prod[:, t, 0:PK_HEADS // 2],
                                                    prod[:, t, PK_HEADS // 2:], ALU.add).then_inc(multiplied, 1)
                            pool.wait_ge(multiplied, (k * 2 + t) * 2 + 2)
                            nc.gpsimd.tensor_tensor(prod[:, t, 0:PK_HEADS // 4], prod[:, t, 0:PK_HEADS // 4],
                                                    prod[:, t, PK_HEADS // 4:PK_HEADS // 2], ALU.add).then_inc(prod_ok, 1)

            @block.vector
            def _(dve):
                dve.nop().then_inc(turn_ok, 1)
                dve.nop().then_inc(o_ok, 1)
                dve.nop().then_inc(summed, 2)
                PER_K = 10

                def inverse(b, h):
                    dve.wait_ge(norm_turned, b + 1)
                    if not isinstance(b, int) or b > 1:
                        dve.wait_ge(s_ok, b * 2 - 1)
                    nc.vector.tensor_scalar(inv[:, h, :].rearrange("p (t m c) -> p t m c", t=SUB, m=QCH),
                                            pI[:].rearrange("p (t m c) -> p t m c", t=SUB, m=QCH)[:, :, :, 0:SETS // QCH],
                                            1e-12, None, ALU.max).then_inc(inv_ok, 1)
                    dve.wait_ge(inv_ok, b * 2 + 2)
                    nc.vector.reciprocal(inv[:, h, :], inv[:, h, :]).then_inc(inv_ok, 1)

                def scale(k, b, h, slot):
                    dve.wait_ge(sc_ok, k + 1)
                    dve.wait_ge(inv_ok, b * 2 + 3)
                    if not isinstance(k, int) or k > 1:
                        dve.wait_ge(ex_ok, k - 1)
                    nc.vector.tensor_tensor(s_[:, slot].rearrange("p t (a k) -> p (t a) k", k=NKEY),
                                            pS[:].rearrange("p t (a k) -> p (t a) k", k=NKEY),
                                            inv[:, h, slot * 2 * SETS:(slot + 1) * 2 * SETS].unsqueeze(2).broadcast_to((P, 2 * SETS, NKEY)),
                                            ALU.mult).then_inc(s_ok, 1)

                class Search:

                    def __init__(self, k, slot):
                        self.k, self.slot, self.st = k, slot, Steps(search, PER_K, k)
                        self.s3 = s_[:, slot].rearrange("p t (a k) -> p (t a) k", k=NKEY)
                        self.rep3 = rep[:].rearrange("p t (a k) -> p (t a) k", k=NKEY)
                        self.p4 = ex[:, slot].rearrange("p t (h f k) -> p (t h) f k", h=PK_HEADS, f=2)

                    def so_far(self):
                        dve.wait_ge(search, self.st.at(self.st.n))

                    def best(self):
                        dve.wait_ge(s_ok, self.k + 2)
                        dve.nop().then_inc(relay, 1)
                        for a in range(2 * SETS):
                            last = nc.vector.max(top[:, a, :], self.s3[:, a, :])
                        self.st.inc(last)

                    def only_four(self):
                        self.so_far()
                        self.st.inc(nc.vector.memset(top[:, :, TOPK_DIM:], 9.0))

                    def mark(self):
                        self.so_far()
                        dve.nop().then_inc(relay, 1)
                        for a in range(2 * SETS):
                            last = nc.vector.match_replace(self.rep3[:, a, :], top[:, a, :], self.s3[:, a, :], -1000.0)
                        self.st.inc(last)

                    def mask(self):
                        self.so_far()
                        dve.wait_ge(ex_ok, self.k + 1)
                        e = ex[:, self.slot]
                        self.st.inc(nc.vector.scalar_tensor_tensor(e, rep[:], -500.0, e, ALU.is_lt, ALU.mult))

                    def sums(self):
                        self.so_far()
                        self.st.inc(nc.vector.tensor_reduce(z[:], self.p4, AX_X, ALU.add))
                        self.st.inc(nc.vector.tensor_reduce(far[:].rearrange("p t h -> p (t h)"), self.p4[:, :, 0, ROWS_IN:], AX_X, ALU.add))

                    def shares(self):
                        z3 = z[:].rearrange("p (t h f) -> p t h f", t=2, f=2)
                        self.so_far()
                        self.st.inc(nc.vector.tensor_tensor(both[:], z3[:, :, :, 0], z3[:, :, :, 1], ALU.mult))
                        self.so_far()
                        self.st.inc(nc.vector.reciprocal(share[:], both[:]))
                        self.so_far()
                        first = self.p4[:, :, 0, 0:ROWS_IN]
                        inverse_sums = share[:].rearrange("p t h -> p (t h)").unsqueeze(2).broadcast_to((P, 2 * PK_HEADS, ROWS_IN))
                        nc.vector.tensor_tensor(a0[:, self.slot].rearrange("p t h a -> p (t h) a"), first, inverse_sums,
                                                ALU.mult).then_inc(a0_ok, 1)
                        self.st.inc(nc.vector.tensor_tensor(far[:], far[:], share[:], ALU.mult))

                    def rest(self):
                        z3 = z[:].rearrange("p (t h f) -> p t h f", t=2, f=2)
                        self.so_far()
                        self.st.inc(nc.vector.tensor_tensor(far[:], far[:], z3[:, :, :, 1], ALU.mult))
                        self.so_far()
                        nc.vector.tensor_reduce(last_w[:, :, 0], far[:], AX_X, ALU.add).then_inc(last_ok, 1)
                        assert self.st.n == PER_K

                last_ok = sem("pk_last_ok")

                def add_heads(n, t):
                    dve.wait_ge(prod_ok, n * 2 + t + 1)
                    if t == 0:
                        dve.wait_ge(turn_ok, n + 1)
                    nc.vector.tensor_tensor(wt[:, t, :], prod[:, t, 0, :], prod[:, t, 1, :], ALU.add).then_inc(summed, 1)

                def add_last(n):
                    dve.wait_ge(summed, n * 2 + 4)
                    dve.wait_ge(last_ok, n + 1)
                    nc.vector.tensor_tensor(wt[:, :, PK_EXP - 1:], wt[:, :, PK_EXP - 1:], last_w[:], ALU.add).then_inc(wt_ok, 1)

                def leave(n, b, h, p):
                    dve.wait_ge(turn_ok, n + 2)
                    dve.wait_ge(piece_out, b * PIECES + PIECES + 2)
                    dve.wait_ge(o_ok, n + 1)
                    nc.vector.tensor_tensor(gw[:], g[:, h, :, p * 2 * P:(p + 1) * 2 * P], turned, ALU.mult).then_inc(gw_ok, 1)

                def onto_res(n):
                    dve.wait_ge(o_ok, n + 2)
                    rows = res[:, bass.ds(n * 2, 2), :]
                    nc.vector.tensor_tensor(rows, rows, pO[:].rearrange("p (t d) -> p t d", t=2), ALU.add).then_inc(o_left, 1)

                def step(n, b, i, final):
                    after = not (final and i == 3)
                    if after:
                        pair = Search(n + 1, (i + 1) % 2)
                        pair.best()
                    if not (final and i >= 2):
                        if i % 2 == 0:
                            inverse(b + 1 + i // 2, (1 + i // 2) % 2)
                        scale(n + 2, b + (i + 2) // 2, (i + 2) // 2 % 2, i % 2)
                    if not isinstance(n, int) or n > 0:
                        onto_res(n - 1)
                    if after:
                        pair.only_four()
                    add_heads(n, 0)
                    if after:
                        pair.mark()
                        pair.mask()
                        pair.sums()
                        pair.shares()
                    add_heads(n, 1)
                    add_last(n)
                    if after:
                        pair.rest()
                    leave(n, b + i // 2, i // 2, i % 2)
                    if final and i == 3:
                        onto_res(n)

                inverse(0, 0)
                scale(0, 0, 0, 0)
                pair = Search(0, 0)
                pair.best()
                scale(1, 0, 0, 1)
                for stage in (pair.only_four, pair.mark, pair.mask, pair.sums, pair.shares, pair.rest):
                    stage()
                rounds(dve, step, first=1)


def norm_project(nc, sem, inp, res, rows, ident, rowsT, v_pad, logits, places):
    with ExitStack() as c:
        def sb(name, shape, dt=F32):
            return c.enter_context(nc.sbuf_tensor("pj_" + name, shape, dt))
        xn = sb("xn", [P, SUB, D])
        stats = sb("stats", [P, SUB, 6])
        mv = sb("mv", [P, SUB, 2])
        std = sb("std", [P, SUB])
        rstd = sb("rstd", [P, SUB])
        xT = sb("xT", [P, 2, DC, BLK])
        w = [sb("w" + n, [P, DC, D]) for n in "qk"]
        wv = sb("wv", [P, DC, D + EXPERTS])
        b = [sb("b" + n, [P, 2]) for n in "qk"]
        bv = sb("bv", [P, D])
        gate_b = sb("gate_b", [P, EXPERTS])
        cos = sb("cos", [P, BATCH, SEQ])
        sin = sb("sin", [P, BATCH, SEQ])
        turn = sb("turn", [P, 4, BLK])
        r = sb("r", [P, 2, 2, BLK])
        rest = sb("rest", [P, 2, 2, BLK])
        parts = sb("parts", [P, 2, 2, 3, 2, BLK], BF16)
        vp = sb("vp", [P, 2, HG, SUB, HPG, VCOLS])
        pT = c.enter_context(nc.psum_tensor("pj_pT", [P, DC, BLK], F32))
        pE = c.enter_context(nc.psum_tensor("pj_pE", [P, 4, BLK], F32))
        pV = c.enter_context(nc.psum_tensor("pj_pV", [P, 2, BLK], F32))
        (w_ok, stat, var_ok, std_ok, xn_ok, turned, kept, x_ok, p_ok, p_left, v_ok, v_left, rot, r_ok, part0, part1,
         part2, rest1, padded, store_free, relay) = (sem("pj_" + n) for n in (
             "w_ok", "stat", "var_ok", "std_ok", "xn_ok", "turned", "kept", "x_ok", "p_ok", "p_left", "v_ok", "v_left",
             "rot", "r_ok", "part0", "part1", "part2", "rest1", "padded", "store_free", "relay"))
        table_in, tables = sem("pj_table_in"), sem("pj_tables")
        stored = [sem(f"pj_stored{h}") for h in range(2)]
        vstored = [sem(f"pj_vstored{h}") for h in range(2)]
        PB = SEQ // BLK
        v_by_batch = v_pad.rearrange("(b g) p t c -> b g p t c", b=BATCH)
        loads = [(w[0][:], inp["Wq"]), (w[1][:], inp["Wk"]), (wv[:, :, 0:D], inp["Wv"]), (wv[:, :, D:], inp["gate"]),
                 (b[0][:], inp["bq"]), (b[1][:], inp["bk"]), (bv[:], inp["bv"].broadcast_to((P, D))),
                 (gate_b[:], inp["gate_b"].broadcast_to((P, EXPERTS)))]
        assert BATCH == 2 and BLOCKS == 8
        W_ALL = 16 * len(loads)
        with nc.Block() as block:
            @block.sync
            def _(sp):
                for dst, src in loads:
                    sp.dma_start(dst, src).then_inc(w_ok, 16)
                for bt in range(BATCH):
                    for t, name in ((cos, "c_cos"), (sin, "c_sin")):
                        sp.dma_start(t[:, bt], inp[name]).then_inc(table_in, 16)
                    sp.wait_ge(table_in, (bt + 1) * 32)
                    sp.nop().then_inc(tables, PB // 2)
                places.load(sp)
                sp.nop().then_inc(stored[1], 1)
                sp.nop().then_inc(vstored[1], 1)
                with sp.Fori(0, BATCH) as bt:
                    with sp.Fori(0, PB // 2) as ii:
                        for h in range(2):
                            jj = bt * (PB // 2) + ii
                            j, i = jj * 2 + h, ii * 2 + h
                            sp.wait_ge(stored[1 - h], (jj + h) * 64 + 1 - h)
                            sp.wait_ge(vstored[1 - h], (jj + h) * 64 + 1 - h)
                            sp.nop().then_inc(store_free, 1)
                            for qk in range(2):
                                sp.wait_ge(part2, j * 2 + qk + 3)
                                for half in range(2):
                                    sp.dma_start(rowsT[qk, :, bass.ds(bt * D + half * P, P), bass.ds(i * BLK, BLK)]
                                                 .rearrange("a p t -> p a t"),
                                                 parts[:, h, qk, :, half, :]).then_inc(stored[h], 16)
                            sp.wait_ge(v_left, j * SUB * 2 + SUB * 2 + 3)
                            for g in range(HG):
                                sp.dma_start(v_by_batch[bass.ds(bt, 1), g, :, bass.ds(i * SUB, SUB), :]
                                             .rearrange("a p t c -> (a p) t c"),
                                             vp[:, h, g].rearrange("p s h c -> p s (h c)")).then_inc(vstored[h], 16)
                places.stores += [(t[h], BLOCKS // 2 * 64 + h) for t in (stored, vstored) for h in range(2)]

            @block.gpsimd
            def _(pool):
                for h in range(2):
                    nc.gpsimd.memset(vp[:, h], 1.0).then_inc(padded, 1)
                pool.nop().then_inc(part2, 2)
                with pool.Fori(0, BLOCKS // 2) as jj:
                    for h in range(2):
                        for qk in range(2):
                            n = (jj * 2 + h) * 2 + qk
                            pool.wait_ge(part0, n + 1)
                            pool.wait_ge(part2, n + 1)
                            nc.gpsimd.tensor_tensor(rest[:, qk], r[:, qk], parts[:, h, qk, 0], ALU.subtract).then_inc(rest1, 1)
                            pool.wait_ge(part1, n + 1)
                            nc.gpsimd.tensor_tensor(parts[:, h, qk, 2], rest[:, qk], parts[:, h, qk, 1], ALU.subtract).then_inc(part2, 1)

            @block.scalar
            def _(act):
                act.nop().then_inc(store_free, 1)
                act.nop().then_inc(v_ok, 1)

                def root(n):
                    act.wait_ge(var_ok, n * 2 + 1)
                    nc.scalar.activation(std[:], std[:], ACT.Sqrt).then_inc(std_ok, 1)

                def keep(n):
                    act.wait_ge(xn_ok, n * SUB + SUB)
                    act.nop().then_inc(relay, 1)
                    nc.scalar.activation(rows[:, bass.ds(n * SUB, SUB), :], xn[:], ACT.Copy).then_inc(kept, 1)

                def turn(n, h):
                    act.wait_ge(turned, n + 2)
                    if not isinstance(n, int) or n > 1:
                        act.wait_ge(v_ok, (n - 1) * SUB + 1)
                    nc.scalar.activation(xT[:, h], pT[:], ACT.Copy).then_inc(x_ok, 1)

                def first_part(j, h, qk):
                    act.wait_ge(r_ok, j * 2 + qk + 2)
                    nc.scalar.activation(parts[:, h, qk, 0], r[:, qk], ACT.Copy).then_inc(part0, 1)

                def second_part(j, h, qk):
                    act.wait_ge(rest1, j * 2 + qk + 3)
                    nc.scalar.activation(parts[:, h, qk, 1], rest[:, qk], ACT.Copy).then_inc(part1, 1)

                def two_blocks(jj, final):
                    for h in range(2):
                        j = jj * 2 + h
                        more = not (final and h)
                        if more:
                            keep(j + 1)
                            turn(j + 1, 1 - h)
                        act.wait_ge(store_free, j + 1)
                        first_part(j, h, 0)
                        second_part(j, h, 0)
                        if not final:
                            root(j + 2)
                        first_part(j, h, 1)
                        second_part(j, h, 1)

                root(0)
                keep(0)
                turn(0, 0)
                root(1)
                with act.Fori(0, BLOCKS // 2 - 1) as jj:
                    two_blocks(jj, False)
                two_blocks(BLOCKS // 2 - 1, True)

            @block.tensor
            def _(pe):
                pe.nop().then_inc(x_ok, 1)

                def transposes(n):
                    pe.wait_ge(xn_ok, n * SUB + SUB)
                    pe.wait_ge(x_ok, n + 1)
                    for d in range(DC):
                        for s in range(SUB):
                            last = nc.tensor.transpose(pT[:, d, s * P:(s + 1) * P], xn[:, s, d * P:(d + 1) * P], ident[:])
                    last.then_inc(turned, 1)

                def two_blocks(jj, final):
                    for h in range(2):
                        j = jj * 2 + h
                        pe.wait_ge(x_ok, j + 2)
                        for qk in range(2):
                            pe.wait_ge(p_left, j * 2 + qk + 1)
                            for eo in range(2):
                                for d in range(DC):
                                    last = nc.tensor.matmul(pE[:, qk * 2 + eo, :], w[qk][:, d, eo * P:(eo + 1) * P], xT[:, h, d, :],
                                                            start=d == 0, stop=d == DC - 1)
                            last.then_inc(p_ok, 1)
                            if qk == 0 and not (final and h):
                                transposes(j + 1)
                            for s in range(qk * 2, qk * 2 + 2):
                                pe.wait_ge(v_left, (j * SUB + s) * 2 + 1)
                                for d in range(DC):
                                    last = nc.tensor.matmul(pV[:, s % 2, 0:D + EXPERTS], xT[:, h, d, s * P:(s + 1) * P], wv[:, d, :],
                                                            start=d == 0, stop=d == DC - 1)
                                last.then_inc(v_ok, 1)

                transposes(0)
                pe.wait_ge(w_ok, W_ALL)
                with pe.Fori(0, BLOCKS // 2 - 1) as jj:
                    two_blocks(jj, False)
                two_blocks(BLOCKS // 2 - 1, True)

            @block.vector
            def _(dve):
                dve.nop().then_inc(turned, 1)
                dve.nop().then_inc(kept, 1)
                dve.nop().then_inc(r_ok, 1)
                dve.nop().then_inc(rest1, 2)
                dve.nop().then_inc(p_left, 2)
                dve.nop().then_inc(v_left, 3)

                def variance(n):
                    if not isinstance(n, int) or n > 0:
                        dve.wait_ge(xn_ok, n * SUB)
                    for s in range(SUB):
                        row = res[:, bass.ds(n * SUB + s, 1), :].rearrange("p a n -> p (a n)")
                        nc.vector.bn_stats(stats[:, s, :], row).then_inc(stat, 1)
                    dve.wait_ge(stat, n * 2 * SUB + SUB)
                    dve.nop().then_inc(relay, 1)
                    for s in range(SUB):
                        nc.vector.bn_aggr(mv[:, s, :], stats[:, s, :]).then_inc(stat, 1)
                    dve.wait_ge(stat, n * 2 * SUB + 2 * SUB)
                    nc.vector.tensor_scalar(std[:], mv[:, :, 1], EPS, None, ALU.add).then_inc(var_ok, 1)

                def normalise(n):
                    dve.wait_ge(std_ok, n + 1)
                    nc.vector.reciprocal(rstd[:], std[:]).then_inc(var_ok, 1)
                    dve.wait_ge(var_ok, n * 2 + 2)
                    dve.wait_ge(turned, n + 1)
                    dve.wait_ge(kept, n + 1)
                    for s in range(SUB):
                        row = res[:, bass.ds(n * SUB + s, 1), :].rearrange("p a n -> p (a n)")
                        nc.vector.tensor_scalar(xn[:, s, :], row, mv[:, s, 0:1], rstd[:, s:s + 1],
                                                ALU.subtract, ALU.mult).then_inc(xn_ok, 1)

                def rotate(j, qk):
                    n = j * 2 + qk
                    dve.wait_ge(p_ok, n + 1)
                    dve.wait_ge(r_ok, n + 1)
                    at = bass.ds(j * BLK, BLK)
                    for k, (eo, table) in enumerate(((0, cos), (0, sin), (1, sin), (1, cos))):
                        nc.vector.scalar_tensor_tensor(turn[:, k, :], pE[:, qk * 2 + eo, :], b[qk][:, eo:eo + 1],
                                                       table[:].rearrange("p b t -> p (b t)")[:, at], ALU.add, ALU.mult).then_inc(rot, 1)
                    dve.wait_ge(rot, n * 4 + 4)
                    dve.nop().then_inc(p_left, 1)
                    dve.wait_ge(rest1, n + 1)
                    nc.vector.tensor_tensor(r[:, qk], turn[:, 0:2, :], turn[:, 2:4, :], ALU.subtract).then_inc(r_ok, 1)

                def two_blocks(jj, final):
                    dve.wait_ge(tables, jj + 1)
                    for h in range(2):
                        j = jj * 2 + h
                        if not (final and h):
                            normalise(j + 1)
                        for qk in range(2):
                            rotate(j, qk)
                            dve.wait_ge(store_free, j + 1)
                            for s in range(qk * 2, qk * 2 + 2):
                                dve.wait_ge(v_ok, j * SUB + s + 2)
                                nc.vector.tensor_tensor(vp[:, h, :, s, :, 0:HD], pV[:, s % 2, 0:D].rearrange("p (g h c) -> p g h c", g=HG, c=HD),
                                                        bv[:].rearrange("p (g h c) -> p g h c", g=HG, c=HD), ALU.add).then_inc(v_left, 1)
                                lg = logits[:, bass.ds(j * SUB + s, 1), :].rearrange("p a e -> p (a e)")
                                nc.vector.tensor_tensor(lg, pV[:, s % 2, D:D + EXPERTS], gate_b[:], ALU.add).then_inc(v_left, 1)
                            if qk == 0 and not final:
                                variance(j + 2)

                variance(0)
                normalise(0)
                variance(1)
                dve.wait_ge(w_ok, W_ALL)
                dve.wait_ge(padded, 2)
                with dve.Fori(0, BLOCKS // 2 - 1) as jj:
                    two_blocks(jj, False)
                two_blocks(BLOCKS // 2 - 1, True)


class Operands:

    def __init__(self, nc, sem, stack, rowsT, v_pad):
        def sb(name, shape, dt):
            return stack.enter_context(nc.sbuf_tensor("op_" + name, shape, dt, side="right"))
        self.rowsT, self.v_pad = rowsT, v_pad
        self.q = sb("q", [P, 2, HPG, SEQ], BF16)
        self.k = sb("k", [P, 2, HPG, SEQ], BF16)
        self.v = sb("v", [P, 2, KT, HPG * VCOLS], F32)
        self.g_in = [sem(f"op_g_in{s}") for s in range(2)]
        self.ones = sem("op_ones")
        self.per_group = 16 * (2 * TERMS + 1)

    def load(self, sp, g, s):
        for t, parts, dst in ((0, PARTS_Q, self.q), (1, PARTS_K, self.k)):
            for n, part in enumerate(parts):
                src = self.rowsT[t, part, bass.ds(g * HPG * HD, HPG * HD), :].rearrange("(h d) s -> d h s", d=HD)
                sp.dma_start(dst[n * HD:(n + 1) * HD, s], src).then_inc(self.g_in[s], 16)
        sp.dma_start(self.v[:, s], self.v_pad[bass.ds(g, 1), :, :, :].rearrange("a p t c -> p (a t) c")).then_inc(self.g_in[s], 16)


class Places:

    def __init__(self, nc, sem, inp, stack):
        def sb(name, shape):
            return stack.enter_context(nc.sbuf_tensor("pl_" + name, shape, F32))
        self.inp = inp
        self.before = sb("before", [P, P])
        self.ones = sb("ones", [P, P])
        self.expert = sb("expert", [P, EXPERTS])
        self.trash = sb("trash", [P, TILES])
        self.ok = sem("pl_ok")
        self.stores = []

    def load(self, sp):
        for t, name in ((self.before, "c_before"), (self.ones, "c_ones"), (self.expert, "c_expert"), (self.trash, "c_trash")):
            sp.dma_start(t[:], self.inp[name]).then_inc(self.ok, 16)


def route(nc, sem, logits, weight, gather_at, scatter_at, places, operands, identb):
    TE = TILES * EXPERTS
    with ExitStack() as c:
        def sb(name, shape, dt=F32):
            return c.enter_context(nc.sbuf_tensor("rt_" + name, shape, dt))
        before, ones, expert, trash, w_ok = places.before, places.ones, places.expert, places.trash, places.ok
        e = sb("e", [P, TILES, EXPERTS])
        hot = sb("hot", [P, TILES, EXPERTS])
        cand = sb("cand", [P, TILES, EXPERTS])
        sums = sb("sums", [P, 2, TILES, EXPERTS])
        at = sb("at", [P, TILES, EXPERTS])
        v = sb("v", [P, 12, TILES])
        pc = c.enter_context(nc.psum_tensor("rt_pc", [P, 2, BLK], F32))
        step, exp_ok, cum, free = (sem("rt_" + n) for n in ("step", "exp_ok", "cum", "free"))
        MX, SUM, IDX, POS, KEEP, SLOT, FAR, TMP = range(8)
        with nc.Block() as block:
            @block.sync
            def _(sp):
                for stored, value in places.stores:
                    sp.wait_ge(stored, value)
                sp.nop().then_inc(free, 1)
                operands.load(sp, 0, 0)

            @block.tensor
            def _(pe):
                pe.wait_ge(w_ok, 64)
                pe.wait_ge(step, 7)
                nc.tensor.matmul(pc[:, 0, 0:TE], before[:], hot[:].rearrange("p t e -> p (t e)"), start=True, stop=True)
                nc.tensor.matmul(pc[:, 1, 0:TE], ones[:], hot[:].rearrange("p t e -> p (t e)"), start=True,
                                 stop=True).then_inc(cum, 1)

            @block.scalar
            def _(act):
                act.wait_ge(step, 2)
                nc.scalar.activation(e[:], e[:], ACT.Exp).then_inc(exp_ok, 1)
                act.wait_ge(free, 1)
                nc.scalar.activation(operands.k[MROW:MROW + 1, 1].rearrange("p h s -> p (h s)"),
                                     identb[MROW:MROW + 1, MROW:MROW + 1].broadcast_to((1, HPG * SEQ)), ACT.Copy).then_inc(operands.ones, 1)

            @block.vector
            def _(dve):
                st = Steps(step, 99)

                def then(ins):
                    dve.wait_ge(step, st.at(st.inc(ins)))

                def by_token(k):
                    return v[:, k, :].unsqueeze(2).broadcast_to((P, TILES, EXPERTS))

                per_expert = expert[:].unsqueeze(1).broadcast_to((P, TILES, EXPERTS))
                dve.wait_ge(w_ok, 64)
                then(nc.vector.tensor_reduce(v[:, MX, :], logits[:], AX_X, ALU.max))
                then(nc.vector.tensor_tensor(e[:], logits[:], by_token(MX), ALU.subtract))
                then(nc.vector.tensor_tensor(hot[:], logits[:], by_token(MX), ALU.is_equal))
                then(nc.vector.tensor_scalar(cand[:], hot[:], -float(EXPERTS), None, ALU.mult))
                then(nc.vector.tensor_tensor(cand[:], cand[:], per_expert, ALU.add))
                then(nc.vector.tensor_reduce(v[:, IDX, :], cand[:], AX_X, ALU.min))
                then(nc.vector.tensor_tensor(hot[:], cand[:], by_token(IDX), ALU.is_equal))
                then(nc.vector.tensor_scalar(v[:, IDX, :], v[:, IDX, :], float(EXPERTS), None, ALU.add))
                dve.wait_ge(exp_ok, 1)
                then(nc.vector.tensor_reduce(v[:, SUM, :], e[:], AX_X, ALU.add))
                then(nc.vector.reciprocal(v[:, MX, :], v[:, SUM, :]))
                dve.wait_ge(cum, 1)
                then(nc.vector.memset(sums[:], 0.0))
                then(nc.vector.tensor_copy(sums[:, 0, 1:, :], pc[:, 1, 0:TE].rearrange("p (t e) -> p t e", e=EXPERTS)[:, :TILES - 1]))
                cur, n = 0, 1
                while n < TILES:
                    st.inc(nc.vector.tensor_copy(sums[:, 1 - cur, 0:n, :], sums[:, cur, 0:n, :]))
                    then(nc.vector.tensor_tensor(sums[:, 1 - cur, n:, :], sums[:, cur, n:, :], sums[:, cur, :TILES - n, :], ALU.add))
                    cur, n = 1 - cur, 2 * n
                then(nc.vector.tensor_tensor(at[:], sums[:, cur], pc[:, 0, 0:TE].rearrange("p (t e) -> p t e", e=EXPERTS), ALU.add))
                then(nc.vector.tensor_tensor(at[:], at[:], hot[:], ALU.mult))
                then(nc.vector.tensor_reduce(v[:, POS, :], at[:], AX_X, ALU.add))
                then(nc.vector.tensor_scalar(v[:, KEEP, :], v[:, POS, :], float(CAP), None, ALU.is_le))
                then(nc.vector.tensor_tensor(weight[:], v[:, MX, :], v[:, KEEP, :], ALU.mult))
                then(nc.vector.tensor_scalar(v[:, POS, :], v[:, POS, :], -1.0, None, ALU.add))
                then(nc.vector.tensor_tensor(v[:, POS, :], v[:, POS, :], v[:, KEEP, :], ALU.mult))
                then(nc.vector.scalar_tensor_tensor(v[:, SLOT, :], v[:, IDX, :], float(CAP), v[:, POS, :], ALU.mult, ALU.add))
                then(nc.vector.tensor_tensor(v[:, FAR, :], trash[:], v[:, SLOT, :], ALU.subtract))
                then(nc.vector.tensor_scalar(v[:, TMP, :], v[:, KEEP, :], -1.0, 1.0, ALU.mult, ALU.add))
                then(nc.vector.tensor_tensor(v[:, FAR, :], v[:, FAR, :], v[:, TMP, :], ALU.mult))
                then(nc.vector.tensor_tensor(v[:, FAR, :], v[:, FAR, :], v[:, SLOT, :], ALU.add))
                nc.vector.tensor_copy(gather_at[:], v[:, SLOT, :])
                nc.vector.tensor_copy(scatter_at[:], v[:, FAR, :])

            @block.gpsimd
            def _(pool):
                pool.wait_ge(free, 1)
                nc.gpsimd.memset(operands.k[MROW:MROW + 1, 0], 1.0).then_inc(operands.ones, 1)


def attention_timeline():
    STEP_COST = 200
    steps = [(s, qt, kt) for s in range(2) for qt in range(QT) for kt in range(4 * qt + SUB)]
    width = [STEP_COST + BLK - P * max(0, kt - 4 * qt) for _, qt, kt in steps]
    events = []
    ready, turn = [], None

    def maxima(lot, n):
        for it, u in lot:
            events.append(("U", it, u))
            if u + 1 == len(attention_units(it % QT)):
                events.append(("N", it))
                ready.append((n, it))

    for s in range(2):
        mine = [n for n, st in enumerate(steps) if st[0] == s]
        items = [4 * s + 3] + [4 * s + 4 + x for x in range(3)]
        units = [(it, u) for it in items for u in range(len(attention_units(it % QT)))]
        cost = [0]
        for it, u in units:
            cost.append(cost[-1] + attention_units(it % QT)[u][2] * len(attention_units(it % QT)[u][3]))
        total, spent, at = sum(width[n] for n in mine), 0, 0
        for n in mine:
            spent += width[n]
            lot = []
            while at < len(units) and cost[at + 1] * total <= cost[-1] * spent:
                lot.append(units[at])
                at += 1
            quarter = (len(lot) + 3) // 4
            for pair in range(2):
                events.append(("S", n + 1, pair))
                maxima(lot[:quarter], n)
                lot = lot[quarter:]
            if turn is not None:
                events.append(("T", turn))
                turn = None
            events.append(("V", n))
            if n + 1 == len(steps) or steps[n + 1][:2] != steps[n][:2]:
                turn = 4 * s + steps[n][1]
                events.append(("O", turn))
            maxima(lot, n)
            while ready and (ready[0][0] < n or n + 1 == len(steps)):
                events.append(("R", ready.pop(0)[1]))
    events.append(("T", turn))
    return steps, events


def attention_units(qt):
    units = []
    for qs in range(SUB):
        for ch in range(qt + 1):
            width = min(BLK, P * (4 * qt + qs + 1) - BLK * ch)
            n = 1 << (BLK // width).bit_length() - 1
            units += [(qs, ch, width, range(h, h + n)) for h in range(0, HPG, n)]
    return units


def attention(nc, sem, inp, res, operands, rows, scatter_at, moe_in, wo, ident, identb):
    G = BATCH * HG
    ROUNDS = G // 2
    ROWS = MROW + 1
    PER = sum(4 * qt + SUB for qt in range(QT))
    ITEMS = 2 * QT
    UNITS = [len(attention_units(qt)) for qt in range(QT)]
    UPER = sum(UNITS)
    assert UPER % 2 == 0
    STEPS, EVENTS = attention_timeline()
    AHEAD = 3
    RING = 4
    assert PER % RING == 0

    def unit_number(rnd, it, u):
        return (rnd * 2 + it // QT) * UPER + sum(UNITS[:it % QT]) + u

    def bank_of(it, u):
        return (sum(UNITS[:it % QT]) + u) % 2

    def last_round(event):
        return (event[0] == "S" and event[1] == len(STEPS)) or (event[0] in "UNR" and event[1] >= ITEMS)

    with ExitStack() as c:
        def sb(name, shape, dt=F32):
            return c.enter_context(nc.sbuf_tensor("at_" + name, shape, dt))
        ctxt = rows[:].rearrange("p t d -> p (t d)").rearrange("p (g t c) -> p g t c", g=G, c=HPG * HD)
        q, k, v = operands.q, operands.k, operands.v
        prob = sb("prob", [P, RING, HPG, BLK])
        masks = sb("masks", [P, 2, P])
        masksb = sb("masksb", [P, 2, P], BF16)
        mask_k, mask_q = masksb[:, 0, :], masksb[:, 1, :]
        peak = sb("peak", [P, HPG, SUB, QT])
        neg = sb("neg", [P, 2, SUB, P], BF16)
        mrow = sb("mrow", [P, BLK], BF16)
        o = sb("o", [P, BLK])
        inv = sb("inv", [P, SUB, HPG])
        bo = sb("bo", [P, D])
        pS = c.enter_context(nc.psum_tensor("at_pS", [P, 2, 2, BLK], F32))
        pM = c.enter_context(nc.psum_tensor("at_pM", [P, 2, BLK], F32))
        pR = c.enter_context(nc.psum_tensor("at_pR", [P, BLK], F32))
        pO = c.enter_context(nc.psum_tensor("at_pO", [P, BLK], F32))
        names = ("w_ok", "masks_ok", "m_made", "m_left", "neg_ok", "row_made", "row_ok", "row_in",
                 "s_made", "p_ok", "pv", "o_ok", "turned", "inv_ok", "ctx_ok", "relay", "clean", "sent")
        (w_ok, masks_ok, m_made, m_left, neg_ok, row_made, row_ok, row_in,
         s_made, p_ok, pv, o_ok, turned, inv_ok, ctx_ok, relay, clean, sent) = (sem("at_" + n) for n in names)
        g_in, G_IN = operands.g_in, operands.per_group
        with nc.Block() as block:
            @block.sync
            def _(sp):
                for t, src in ((masks, inp["c_masks"]), (wo, inp["Wo"]), (bo, inp["bo"].broadcast_to((P, D)))):
                    sp.dma_start(t[:], src).then_inc(w_ok, 16)
                sp.wait_ge(g_in[0], G_IN)
                operands.load(sp, 1, 1)
                with sp.Fori(1, ROUNDS) as rnd:
                    for s in range(2):
                        sp.wait_ge(pv, (rnd * 2 + s - 1) * PER + RING)
                        operands.load(sp, rnd * 2 + s, s)

            @block.gpsimd
            def _(pool):
                def place(n, it):
                    pool.wait_ge(row_ok, n + 2)
                    pool.nop().then_inc(relay, 1)
                    s, qt = it // QT % 2, it % QT
                    for h in range(HPG):
                        pool.dma_start(q[MROW:MROW + 1, s, h, qt * BLK:(qt + 1) * BLK], mrow[32 * h:32 * h + 1, :]).then_inc(row_in, 16)

                for t in range(TILES):
                    pool.indirect_dma_start(moe_in, bass.IndirectOffsetOnAxis(ap=scatter_at[:, t:t + 1], axis=0),
                                            rows[:, t, :], None).then_inc(sent, 16)
                for it in range(AHEAD):
                    place(it, it)
                with pool.Fori(0, ROUNDS - 1) as rnd:
                    for it in range(AHEAD, AHEAD + ITEMS):
                        place(rnd * ITEMS + it, it)
                for it in range(AHEAD, ITEMS):
                    place((ROUNDS - 1) * ITEMS + it, it)
                pool.wait_ge(w_ok, 48)
                for t in range(TILES):
                    nc.gpsimd.tensor_tensor(res[:, t, :], res[:, t, :], bo[:], ALU.add)

            @block.tensor
            def _(pe):
                pe.nop().then_inc(row_ok, 1)
                pe.nop().then_inc(ctx_ok, 1)
                pe.nop().then_inc(o_ok, 1)
                pe.wait_ge(w_ok, 48)
                pe.wait_ge(operands.ones, 2)
                pe.wait_ge(masks_ok, 1)
                pe.wait_ge(clean, 2)

                def maxima(rnd, it, u):
                    s, qt = it // QT % 2, it % QT
                    qs, ch, width, heads = attention_units(qt)[u]
                    i = 4 * qt + qs
                    pe.wait_ge(m_left, unit_number(rnd, it, u) + 1)
                    for x, h in enumerate(heads):
                        bank = pM[:, bank_of(it, u), x * width:(x + 1) * width]
                        last = nc.tensor.matmul(bank, q[0:MROW, s, h, i * P:(i + 1) * P],
                                                k[0:MROW, s, h, ch * BLK:ch * BLK + width], start=True, stop=ch < qt)
                        if ch == qt:
                            last = nc.tensor.matmul(bank[:, width - P:width], identb[:], mask_k, start=False, stop=True)
                    last.then_inc(m_made, 1)

                def row(n, it, turns):
                    pe.wait_ge(neg_ok, n + 2)
                    pe.wait_ge(row_ok, n + 1)
                    pe.wait_ge(ctx_ok, turns + 1)
                    for qs in range(SUB):
                        last = nc.tensor.matmul(pR[:, qs * P:(qs + 1) * P], neg[:, it % 2, qs, :], identb[:], start=True, stop=True)
                    last.then_inc(row_made, 1)

                def scores(rnd, step, pair):
                    s, qt, kt = STEPS[step % len(STEPS)]
                    n = rnd * len(STEPS) + step
                    if kt == 0 and pair == 0:
                        it = QT * (step // PER) + qt
                        pe.wait_ge(row_in, (rnd * ITEMS + it + 1) * 16 * HPG)
                    r = max(0, kt - 4 * qt)
                    diag = kt >= 4 * qt
                    pe.wait_ge(p_ok, n * 2 + pair + 1)
                    for x in range(2):
                        h = pair * 2 + x
                        last = nc.tensor.matmul(pS[:, pair, x, r * P:], k[0:ROWS, s, h, kt * P:(kt + 1) * P],
                                                q[0:ROWS, s, h, qt * BLK + r * P:(qt + 1) * BLK], start=True, stop=not diag)
                        if diag:
                            last = nc.tensor.matmul(pS[:, pair, x, r * P:(r + 1) * P], identb[:], mask_q, start=False, stop=True)
                    last.then_inc(s_made, 1)

                def values(rnd, step):
                    s, qt, kt = STEPS[step]
                    n = rnd * len(STEPS) + step
                    r = max(0, kt - 4 * qt)
                    if kt == 0:
                        pe.wait_ge(o_ok, rnd * ITEMS + s * QT + qt + 1)
                    pe.wait_ge(p_ok, n * 2 + 4)
                    for h in range(HPG):
                        last = nc.tensor.matmul(pO[32 * h:32 * h + VCOLS, r * P:], v[:, s, kt, h * VCOLS:(h + 1) * VCOLS],
                                                prob[:, step % RING, h, r * P:], start=kt == 0, stop=kt == 4 * qt + SUB - 1,
                                                tile_position=(0, 32 * h))
                    last.then_inc(pv, 1)

                def turn_out(n, rows):
                    pe.wait_ge(o_ok, n + 2)
                    pe.wait_ge(row_ok, rows + 1)
                    pe.wait_ge(ctx_ok, n + 1)
                    for qs in range(SUB):
                        last = nc.tensor.transpose(pR[:, qs * P:(qs + 1) * P], o[:, qs * P:(qs + 1) * P], ident[:])
                    last.then_inc(turned, 1)

                pe.wait_ge(g_in[0], G_IN)
                for it in range(AHEAD):
                    for u in range(UNITS[it]):
                        maxima(0, it, u)
                    row(it, it, 0)
                for pair in range(2):
                    scores(0, 0, pair)

                def one_round(rnd, final):
                    first = rnd * ITEMS
                    rows, turns = AHEAD, 0
                    for e in EVENTS:
                        if final and last_round(e):
                            continue
                        if e[0] == "S":
                            scores(rnd, e[1], e[2])
                        elif e[0] == "U":
                            if e[1] == QT and e[2] == 0:
                                pe.wait_ge(g_in[1], (rnd + 1) * G_IN)
                            if e[1] == 2 * QT and e[2] == 0:
                                pe.wait_ge(g_in[0], (rnd + 2) * G_IN)
                            maxima(rnd, e[1], e[2])
                        elif e[0] == "V":
                            values(rnd, e[1])
                        elif e[0] == "R":
                            row(first + e[1], e[1], first + turns)
                            rows += 1
                        elif e[0] == "T":
                            turn_out(first + e[1], first + rows)
                            turns += 1

                with pe.Fori(0, ROUNDS - 1) as rnd:
                    one_round(rnd, False)
                one_round(ROUNDS - 1, True)

            @block.scalar
            def _(act):
                act.wait_ge(w_ok, 48)
                nc.scalar.activation(masksb[:], masks[:], ACT.Copy).then_inc(masks_ok, 1)
                act.nop().then_inc(pv, RING)
                act.nop().then_inc(p_ok, 2)

                def exps(rnd, step, pair):
                    _, qt, kt = STEPS[step % len(STEPS)]
                    n = rnd * len(STEPS) + step
                    r = max(0, kt - 4 * qt)
                    act.wait_ge(s_made, n * 2 + pair + 1)
                    if pair == 0:
                        act.wait_ge(pv, n + 1)
                    nc.scalar.activation(prob[:, step % RING, pair * 2:pair * 2 + 2, r * P:], pS[:, pair, :, r * P:],
                                         ACT.Exp, scale=HD ** -0.5).then_inc(p_ok, 1)

                def row_copy(n):
                    act.wait_ge(row_made, n + 1)
                    if not isinstance(n, int) or n > 0:
                        act.wait_ge(row_in, n * 16 * HPG)
                    nc.scalar.activation(mrow[:], pR[:], ACT.Copy).then_inc(row_ok, 1)

                for it in range(AHEAD):
                    row_copy(it)
                for pair in range(2):
                    exps(0, 0, pair)

                def one_round(rnd, final):
                    for e in EVENTS:
                        if final and last_round(e):
                            continue
                        if e[0] == "S":
                            exps(rnd, e[1], e[2])
                        elif e[0] == "R":
                            row_copy(rnd * ITEMS + e[1])
                        elif e[0] == "O":
                            n = rnd * ITEMS + e[1]
                            steps = sum(4 * x + SUB for x in range(e[1] % QT + 1)) + e[1] // QT * PER
                            act.wait_ge(pv, rnd * len(STEPS) + steps + RING)
                            act.wait_ge(turned, n + 1)
                            nc.scalar.activation(o[:], pO[:], ACT.Copy).then_inc(o_ok, 1)

                with act.Fori(0, ROUNDS - 1) as rnd:
                    one_round(rnd, False)
                one_round(ROUNDS - 1, True)

            @block.vector
            def _(dve):
                nc.vector.memset(neg[:], 0.0).then_inc(clean, 1)
                nc.vector.memset(pO[:], 0.0).then_inc(clean, 1)
                dve.nop().then_inc(neg_ok, 1)
                dve.nop().then_inc(turned, 1)
                dve.nop().then_inc(m_left, 2)

                def maxima(rnd, it, u):
                    qs, ch, width, heads = attention_units(it % QT)[u]
                    x = unit_number(rnd, it, u)
                    dve.wait_ge(m_made, x + 1)
                    if u == 0:
                        dve.wait_ge(neg_ok, rnd * ITEMS + it + 1)
                    n = len(heads)
                    nc.vector.tensor_reduce(peak[:, heads[0]:heads[0] + n, qs, ch],
                                            pM[:, bank_of(it, u), 0:n * width].rearrange("p (h k) -> p h k", h=n),
                                            AX_X, ALU.max).then_inc(m_left, 1)

                def negate(rnd, it):
                    dve.wait_ge(m_left, unit_number(rnd, it, UNITS[it % QT] - 1) + 3)
                    if isinstance(rnd, int) and rnd == 0 and it < 2:
                        dve.wait_ge(clean, 1)
                    if not isinstance(rnd, int) or rnd > 0 or it > 1:
                        dve.wait_ge(row_made, rnd * ITEMS + it - 1)
                    nc.vector.tensor_reduce(neg[:, it % 2].rearrange("p s (h c) -> p h s c", h=HPG)[:, :, :, 0],
                                            peak[:, :, :, 0:it % QT + 1], AX_X, ALU.max, negate=True).then_inc(neg_ok, 1)

                def outputs(rnd, it):
                    n, s, qt = rnd * ITEMS + it, it // QT, it % QT
                    dve.wait_ge(turned, n + 2)
                    t4 = pR[:].rearrange("p (s h c) -> p s h c", s=SUB, h=HPG)
                    dve.wait_ge(ctx_ok, n + 1)
                    nc.vector.reciprocal(inv[:], t4[:, :, :, HD]).then_inc(inv_ok, 1)
                    dve.wait_ge(inv_ok, n + 1)
                    to = ctxt[:, bass.ds(rnd * 2 + s, 1), qt * SUB:(qt + 1) * SUB, :].rearrange("p a s (h c) -> p (a s) h c", h=HPG)
                    nc.vector.tensor_tensor(to, t4[:, :, :, 0:HD], inv[:].unsqueeze(3).broadcast_to((P, SUB, HPG, HD)),
                                            ALU.mult).then_inc(ctx_ok, 1)

                for it in range(AHEAD):
                    for u in range(UNITS[it]):
                        maxima(0, it, u)
                    negate(0, it)
                dve.wait_ge(sent, 16 * TILES)

                def one_round(rnd, final):
                    for e in EVENTS:
                        if final and last_round(e):
                            continue
                        if e[0] == "U":
                            maxima(rnd, e[1], e[2])
                        elif e[0] == "N":
                            negate(rnd, e[1])
                        elif e[0] == "T":
                            outputs(rnd, e[1])

                with dve.Fori(0, ROUNDS - 1) as rnd:
                    one_round(rnd, False)
                one_round(ROUNDS - 1, True)


class Experts:

    def __init__(self, nc, sem, inp, stack, moe_in):
        def sb(name, shape):
            return stack.enter_context(nc.sbuf_tensor("ex_" + name, shape, F32, side="right"))
        self.inp, self.moe_in = inp, moe_in
        self.w1 = [sb(f"w1_{s}", [P, DC, FF]) for s in range(2)]
        self.w2 = [sb(f"w2_{s}", [P, FC, D]) for s in range(2)]
        self.xe = [sb(f"xe_{s}", [P, CT, D]) for s in range(2)]
        self.b1 = sb("b1", [P, EXPERTS, FC])
        self.b2 = sb("b2", [P, EXPERTS, D])
        self.e_in = [sem(f"ex_e_in{s}") for s in range(2)]
        self.b_ok = sem("ex_b_ok")

    def load_biases(self, sp):
        sp.dma_start(self.b1[:], self.inp["b1"]).then_inc(self.b_ok, 16)
        sp.dma_start(self.b2[:].rearrange("p e d -> p (e d)"), self.inp["b2"].broadcast_to((P, EXPERTS * D))).then_inc(self.b_ok, 16)

    def load(self, sp, e, s):
        rows = self.moe_in[bass.ds(e * CAP, CAP), :].rearrange("(t p) d -> p t d", p=P)
        sp.dma_start(self.xe[s][:], rows).then_inc(self.e_in[s], 16)
        for w, name in ((self.w1, "w1"), (self.w2, "w2")):
            sp.dma_start(w[s][:], self.inp[name][:, bass.ds(e, 1), :, :].rearrange("p a c f -> p (a c) f")).then_inc(self.e_in[s], 16)


def attention_out(nc, sem, res, ctxt, wo, ident, experts):
    with ExitStack() as c:
        cx = [c.enter_context(nc.sbuf_tensor(f"ao_cx{h}", [P, SUB, D], F32)) for h in range(2)]
        cT = [c.enter_context(nc.sbuf_tensor(f"ao_cT{h}", [P, DC, BLK], F32)) for h in range(2)]
        pC = c.enter_context(nc.psum_tensor("ao_pC", [P, 2, DC, BLK], F32))
        pW = c.enter_context(nc.psum_tensor("ao_pW", [P, 2, BLK], F32))
        got, turned, cT_ok, made, left = (sem("ao_" + n) for n in ("got", "turned", "cT_ok", "made", "left"))
        with nc.Block() as block:
            @block.sync
            def _(sp):
                experts.load_biases(sp)
                for s in range(2):
                    experts.load(sp, s, s)

            @block.gpsimd
            def _(pool):
                pool.nop().then_inc(turned, 2)
                with pool.Fori(0, BATCH) as b:
                    with pool.Fori(0, QT // 2) as ii:
                        for h in range(2):
                            i = ii * 2 + h
                            pool.wait_ge(turned, b * QT + i + 1)
                            nc.gpsimd.tensor_copy(cx[h][:].rearrange("p s (g c) -> p g s c", g=HG),
                                                  ctxt[:, bass.ds(b * HG, HG), bass.ds(i * SUB, SUB), :]).then_inc(got, 1)

            @block.tensor
            def _(pe):
                pe.nop().then_inc(cT_ok, 2)

                def turn(j, h):
                    pe.wait_ge(got, j + 1)
                    pe.wait_ge(cT_ok, j + 1)
                    for d in range(DC):
                        for s in range(SUB):
                            last = nc.tensor.transpose(pC[:, h, d, s * P:(s + 1) * P], cx[h][:, s, d * P:(d + 1) * P], ident[:])
                    last.then_inc(turned, 1)

                def two_blocks(jj, final):
                    for h in range(2):
                        j = jj * 2 + h
                        if not (final and h):
                            turn(j + 1, 1 - h)
                        pe.wait_ge(cT_ok, j + 3)
                        for s in range(SUB):
                            pe.wait_ge(left, j * SUB + s + 1)
                            for d in range(DC):
                                last = nc.tensor.matmul(pW[:, s % 2, 0:D], cT[h][:, d, s * P:(s + 1) * P], wo[:, d, :],
                                                        start=d == 0, stop=d == DC - 1)
                            last.then_inc(made, 1)

                turn(0, 0)
                with pe.Fori(0, BLOCKS // 2 - 1) as jj:
                    two_blocks(jj, False)
                two_blocks(BLOCKS // 2 - 1, True)

            @block.scalar
            def _(act):
                act.nop().then_inc(made, SUB + 1)
                with act.Fori(0, BLOCKS // 2) as jj:
                    for h in range(2):
                        j = jj * 2 + h
                        act.wait_ge(turned, j + 3)
                        act.wait_ge(made, j * SUB + 1)
                        nc.scalar.activation(cT[h][:], pC[:, h], ACT.Copy).then_inc(cT_ok, 1)

            @block.vector
            def _(dve):
                dve.nop().then_inc(left, 2)
                with dve.Fori(0, BLOCKS) as j:
                    for s in range(SUB):
                        dve.wait_ge(made, j * SUB + s + SUB + 2)
                        row = res[:, bass.ds(j * SUB + s, 1), :].rearrange("p a n -> p (a n)")
                        nc.vector.tensor_tensor(row, row, pW[:, s % 2, 0:D], ALU.add).then_inc(left, 1)


def moe(nc, sem, res, weight, gather_at, moe_out, ident, out, experts):
    HC = CT * P // 2
    with ExitStack() as c:
        def sb(name, shape, dt=F32):
            return c.enter_context(nc.sbuf_tensor("me_" + name, shape, dt))
        w1, w2, xe, b1, b2 = experts.w1, experts.w2, experts.xe, experts.b1, experts.b2
        b_ok, e_in = experts.b_ok, experts.e_in
        b1e = sb("b1e", [P, FC])
        xT = [sb(f"xT_{s}", [P, DC, CT * P]) for s in range(2)]
        h = sb("h", [P, FC, CT * P])
        eo = [sb(f"eo_{s}", [P, CT, D]) for s in range(2)]
        AHEAD = 4
        y = [sb(f"y_{n}", [P, SUB, D]) for n in range(AHEAD)]
        pX = c.enter_context(nc.psum_tensor("me_pX", [P, 2, BLK], F32))
        pH = c.enter_context(nc.psum_tensor("me_pH", [P, 4, BLK], F32))
        pO = c.enter_context(nc.psum_tensor("me_pO", [P, 2, BLK], F32))
        stored, b1_ok, relay = sem("me_rows_stored"), sem("me_b1_ok"), sem("me_relay")
        e_out = [sem(f"me_e_out{s}") for s in range(2)]
        x_turn, x_left, h_made, h_left, o_made, o_left = (
            sem("me_" + n) for n in ("x_turn", "x_left", "h_made", "h_left", "o_made", "o_left"))
        with nc.Block() as block:
            @block.sync
            def _(sp):
                sp.nop().then_inc(o_made, 1)

                with sp.Fori(1, EXPERTS // 2) as pair:
                    for s in range(2):
                        sp.wait_ge(o_made, (pair * 2 + s - 1) * CT + 1)
                        experts.load(sp, pair * 2 + s, s)

            @block.tensor
            def _(pe):
                def turn(e, s, pair):
                    pe.wait_ge(e_in[s], pair * 48 + 48)
                    for t in range(CT):
                        pe.wait_ge(x_left, e * CT + t + 1)
                        for d in range(DC):
                            last = nc.tensor.transpose(pX[:, t % 2, d * P:(d + 1) * P], xe[s][:, t, d * P:(d + 1) * P], ident[:])
                        last.then_inc(x_turn, 1)

                def two_experts(pair, final):
                    for s in range(2):
                        e = pair * 2 + s
                        pe.wait_ge(x_left, e * CT + CT + 2)
                        for f in range(FC):
                            for k in range(2):
                                n = f * 2 + k
                                pe.wait_ge(h_left, e * FC * 2 + n + 1)
                                for d in range(DC):
                                    last = nc.tensor.matmul(pH[:, n % 4, 0:HC], w1[s][:, d, f * P:(f + 1) * P],
                                                            xT[s][:, d, k * HC:(k + 1) * HC], start=d == 0, stop=d == DC - 1)
                                last.then_inc(h_made, 1)
                        if not (final and s):
                            turn(e + 1, 1 - s, pair + s)
                        pe.wait_ge(h_left, (e + 1) * FC * 2 + 4)
                        for t in range(CT):
                            pe.wait_ge(o_left, e * CT + max(t, 1) + 1)
                            for f in range(FC):
                                last = nc.tensor.matmul(pO[:, t % 2, 0:D], h[:, f, t * P:(t + 1) * P], w2[s][:, f, :],
                                                        start=f == 0, stop=f == FC - 1)
                            last.then_inc(o_made, 1)

                turn(0, 0, 0)
                with pe.Fori(0, EXPERTS // 2 - 1) as pair:
                    two_experts(pair, False)
                two_experts(EXPERTS // 2 - 1, True)

            @block.scalar
            def _(act):
                act.nop().then_inc(h_left, 4)
                act.wait_ge(b_ok, 32)
                with act.Fori(0, EXPERTS) as e:
                    act.wait_ge(o_made, e * CT + 1)
                    act.wait_ge(h_left, e * FC * 2 + 4)
                    act.nop().then_inc(relay, 1)
                    nc.scalar.activation(b1e[:], b1[:, bass.ds(e, 1), :].rearrange("p a b -> p (a b)"), ACT.Copy).then_inc(b1_ok, 1)
                    act.wait_ge(b1_ok, e + 1)
                    for n in range(FC * 2):
                        act.wait_ge(h_made, e * FC * 2 + n + 2)
                        nc.scalar.activation(h[:, n // 2, (n % 2) * HC:(n % 2 + 1) * HC], pH[:, n % 4, 0:HC], ACT.Relu,
                                             bias=b1e[:, n // 2:n // 2 + 1]).then_inc(h_left, 1)

            @block.vector
            def _(dve):
                dve.nop().then_inc(h_made, 1)
                dve.nop().then_inc(stored, 2)
                dve.nop().then_inc(x_left, 2)
                dve.nop().then_inc(o_left, 2)
                dve.wait_ge(b_ok, 32)

                def turned(e, s):
                    if not isinstance(e, int) or e > 1:
                        dve.wait_ge(h_made, (e - 1) * FC * 2 + 1)
                    for t in range(CT):
                        dve.wait_ge(x_turn, e * CT + t + 1)
                        nc.vector.tensor_copy(xT[s][:, :, t * P:(t + 1) * P],
                                              pX[:, t % 2, 0:D].rearrange("p (c n) -> p c n", c=DC)).then_inc(x_left, 1)

                def two_experts(pair, final):
                    for s in range(2):
                        e = pair * 2 + s
                        if not (final and s):
                            turned(e + 1, 1 - s)
                        dve.wait_ge(stored, e + 1)
                        for t in range(CT):
                            dve.wait_ge(o_made, e * CT + t + 2)
                            nc.vector.tensor_tensor(eo[s][:, t, :], pO[:, t % 2, 0:D],
                                                    b2[:, bass.ds(e, 1), :].rearrange("p a d -> p (a d)"), ALU.add).then_inc(o_left, 1)

                turned(0, 0)
                with dve.Fori(0, EXPERTS // 2 - 1) as pair:
                    two_experts(pair, False)
                two_experts(EXPERTS // 2 - 1, True)

            @block.gpsimd
            def _(pool):
                with pool.Fori(0, EXPERTS // 2) as pair:
                    for s in range(2):
                        e = pair * 2 + s
                        pool.wait_ge(o_left, (e + 1) * CT + 2)
                        pool.dma_start(moe_out[bass.ds(e * CAP, CAP), :].rearrange("(t p) d -> p t d", p=P), eo[s][:]).then_inc(e_out[s], 16)
                        pool.wait_ge(e_out[s], (pair + 1) * 16)
                        pool.nop().then_inc(stored, 1)

        got = [sem(f"me_got{j}") for j in range(BLOCKS)]
        done, stored = sem("me_done"), sem("me_stored")
        rows_out = out.rearrange("b (t p) d -> p (b t) d", p=P)
        with nc.Block() as block:
            @block.gpsimd
            def _(pool):
                for j in range(BLOCKS):
                    if j >= AHEAD:
                        pool.wait_ge(done, (j - AHEAD + 1) * SUB)
                    for t in range(SUB):
                        at = j * SUB + t
                        pool.indirect_dma_start(y[j % AHEAD][:, t, :], None, moe_out,
                                                bass.IndirectOffsetOnAxis(ap=gather_at[:, at:at + 1], axis=0)).then_inc(got[j], 16)

            @block.vector
            def _(dve):
                for j in range(BLOCKS):
                    dve.wait_ge(got[j], 16 * SUB)
                    for t in range(SUB):
                        at = j * SUB + t
                        nc.vector.scalar_tensor_tensor(res[:, at, :], y[j % AHEAD][:, t, :], weight[:, at:at + 1], res[:, at, :],
                                                       ALU.mult, ALU.add).then_inc(done, 1)

            @block.sync
            def _(sp):
                for j in range(BLOCKS):
                    sp.wait_ge(done, (j + 1) * SUB)
                    sp.dma_start(rows_out[:, j * SUB:(j + 1) * SUB, :], res[:, j * SUB:(j + 1) * SUB, :]).then_inc(stored, 16)
                sp.wait_ge(stored, 16 * BLOCKS)


def rows_on_partitions(w, chunks):
    return w.reshape(chunks, P, -1).transpose(1, 0, 2)


def arrays_for(i):
    a = {"x": i["L0_attn_x"]}
    ar = np.arange(P)
    a["c_ident"] = np.eye(P, dtype=np.float32)
    a["gb"] = np.stack([i["L0_attn_ln_gamma"].reshape(DC, P).T, i["L0_attn_ln_beta"].reshape(DC, P).T], 1)
    w_in = i["L0_attn_W_in"]
    a["W_inT"] = rows_on_partitions(w_in.T, DC)
    a["W_inE"] = rows_on_partitions(w_in[:INNER], IC)
    a["W_outT"] = rows_on_partitions(i["L0_attn_W_out"].T, IC)
    a["A"], a["A_T"] = i["L0_attn_A"], i["L0_attn_A"].T
    a["BmT"] = rows_on_partitions(i["L0_attn_Bm"].T, IC)
    a["Cm"] = i["L0_attn_Cm"]
    a["c_own"] = (ar[:, None] // STATE == np.arange(GROUPS)[None]).astype(np.float32)
    starts = np.arange(BLOCKS + 1) % (SEQ // BLK) == 0
    a["c_inner"] = np.tile(1.0 - starts.astype(np.float32), (P, 1))
    a["conv"] = rows_on_partitions(np.concatenate([i["L0_attn_conv_w"][:, 0], i["L0_attn_conv_b"][:, None]], 1), IC)
    a["Wq0"] = rows_on_partitions(i["L0_ffn_Wq"], DC)
    chan = np.stack([np.tile(i["L0_ffn_" + n], 2) for n in ("bn_gamma", "bn_beta")], 1)
    a["pk_vec"] = np.concatenate([i["L0_ffn_bq"].reshape(QCH, P).T, chan], 1)
    a["key0T"], a["key1T"] = i["L0_ffn_sub_key0"].T, i["L0_ffn_sub_key1"].T
    a["downT"] = rows_on_partitions(i["L0_ffn_expert_down"].T, DC)
    a["up"] = rows_on_partitions(i["L0_ffn_expert_up"], DC)
    a["c_heads"] = (ar[:, None] % QD == ar[None] % QD).astype(np.float32) / PK_HEADS
    a["c_halves"] = (ar[:, None] // HALF == np.arange(32)[None]).astype(np.float32)
    even_odd = np.concatenate([np.arange(0, D, 2), np.arange(1, D, 2)])
    for n in "qk":
        a["W" + n] = rows_on_partitions(i["L1_attn_W" + n][:, even_odd], DC)
        a["b" + n] = i["L1_attn_b" + n][even_odd].reshape(2, P).T
    a["Wv"], a["Wo"] = (rows_on_partitions(i["L1_attn_W" + n], DC) for n in "vo")
    a["bv"], a["bo"] = i["L1_attn_bv"][None], i["L1_attn_bo"][None]
    freq = np.power(10000.0, -2.0 * np.arange(P) / D).astype(np.float32)
    angle = (freq[:, None] * np.arange(SEQ, dtype=np.float32)[None]).astype(np.float64)
    a["c_cos"], a["c_sin"] = np.cos(angle).astype(np.float32), np.sin(angle).astype(np.float32)
    later = np.where(ar[None] > ar[:, None], -1e30, 0.0).astype(np.float32)
    a["c_masks"] = np.stack([later, later.T], 1)
    a["gate"] = rows_on_partitions(i["L1_ffn_gate_w"].T, DC)
    a["gate_b"] = i["L1_ffn_gate_b"][None]
    a["w1"] = i["L1_ffn_w1"].reshape(EXPERTS, DC, P, FF).transpose(2, 0, 1, 3)
    a["b1"] = i["L1_ffn_b1"].reshape(EXPERTS, FC, P).transpose(2, 0, 1)
    a["w2"] = i["L1_ffn_w2"].reshape(EXPERTS, FC, P, D).transpose(2, 0, 1, 3)
    a["b2"] = i["L1_ffn_b2"].reshape(1, EXPERTS * D)
    a["c_before"] = (ar[:, None] <= ar[None]).astype(np.float32)
    a["c_ones"] = np.ones((P, P), np.float32)
    a["c_trash"] = (SLOTS + ar[:, None] + P * np.arange(TILES)[None]).astype(np.float32)
    a["c_expert"] = np.tile(np.arange(EXPERTS, dtype=np.float32), (P, 1))
    return {n: np.ascontiguousarray(x) for n, x in a.items()}


def kernel(**inputs):
    import concourse.bacc as bacc
    from concourse.bass_utils import run_bass_kernel_spmd

    nc = bacc.Bacc("TRN2", target_bir_lowering=False, num_devices=1)
    arrays, aps = {}, {}
    for name, a in arrays_for({n: np.asarray(v) for n, v in inputs.items()}).items():
        arrays["in_" + name] = a
        aps[name] = nc.dram_tensor("in_" + name, a.shape, mybir.dt.from_np(a.dtype), kind="ExternalInput").ap()
    out = nc.dram_tensor("out_0", (BATCH, SEQ, D), F32, kind="ExternalOutput").ap()
    program(nc, aps, out)
    return run_bass_kernel_spmd(nc, [arrays], core_ids=[0]).results[0]["out_0"]
```
